# Optimizing a Trainium2 kernel written in Bass

```python
import numpy as np
import jax
import jax.numpy as jnp

def _softmax(x, axis=-1):
    return jax.nn.softmax(x, axis=axis)

def _gelu(x):
    return jax.nn.gelu(x, approximate=True)

def _silu(x):
    return jax.nn.silu(x)

def _sigmoid(x):
    return jax.nn.sigmoid(x)

def _layernorm(x, axis=-1, eps=1e-05):
    m = jnp.mean(x, axis=axis, keepdims=True)
    v = jnp.var(x, axis=axis, keepdims=True)
    return (x - m) / jnp.sqrt(v + eps)

def _scatter_add(tgt, idx, src, axis=0):
    return tgt.at[idx].add(src)

def _segment_sum(src, seg, n):
    return jax.ops.segment_sum(src, seg, n)
kernel_name = 'mk_audio_tower_d1_tok_aud1d768_r4_f62b4b'

def setup_inputs(seed: int=0):
    np.random.seed(seed)
    _w = jnp.asarray

    def _rec_inputs():
        import jax
        import jax.numpy as jnp
        _rk = jax.random.key(seed)
        x = 8.9527e-05 + 1.00009 * jax.random.normal(jax.random.fold_in(_rk, 1), (16, 40000), jnp.float32)
        return x
    x = _rec_inputs()

    def _L0_tok_setup():
        import jax, jax.numpy as jnp
        import numpy as np
        from jax import lax
        CONV_LAYERS = [(128, 10, 5), (128, 3, 2), (128, 3, 2), (128, 3, 2), (128, 3, 2), (128, 2, 2)]
        NUM_GROUPS = 32
        EPS = 1e-05
        EMBED_DIM = 192

        def _block(x, cw, cb, gw, gb, stride):
            y = lax.conv_general_dilated(x, cw, (stride,), 'VALID', dimension_numbers=('NCH', 'OIH', 'NCH'))
            y = y + cb[None, :, None]
            B, C, T = y.shape
            yg = y.reshape(B, NUM_GROUPS, C // NUM_GROUPS * T)
            mu = yg.mean(axis=-1, keepdims=True)
            var = yg.var(axis=-1, keepdims=True)
            yn = ((yg - mu) * lax.rsqrt(var + EPS)).reshape(B, C, T)
            yn = yn * gw[None, :, None] + gb[None, :, None]
            return jax.nn.gelu(yn)

        def _forward(x, conv_params, pw, pb):
            h = x[:, None, :]
            for (cw, cb, gw, gb), (_, _, s) in zip(conv_params, CONV_LAYERS):
                h = _block(h, cw, cb, gw, gb, s)
            h = jnp.transpose(h, (0, 2, 1))
            return jnp.einsum('bfc,ec->bfe', h, pw) + pb
        key = jax.random.key(seed)
        ks = jax.random.split(key, 16)
        inp = {'x': jax.random.normal(ks[0], (2, 80000), dtype=jnp.float32)}
        in_c = 1
        for li, (oc, k, s) in enumerate(CONV_LAYERS):
            lim = 1.0 / np.sqrt(in_c * k)
            inp[f'cw{li}'] = jax.random.uniform(jax.random.fold_in(ks[1], li), (oc, in_c, k), jnp.float32, -lim, lim)
            inp[f'cb{li}'] = jax.random.uniform(jax.random.fold_in(ks[2], li), (oc,), jnp.float32, -lim, lim)
            inp[f'gw{li}'] = jnp.ones((oc,), jnp.float32)
            inp[f'gb{li}'] = jnp.zeros((oc,), jnp.float32)
            in_c = oc
        lim = 1.0 / np.sqrt(128)
        inp['pw'] = jax.random.uniform(ks[3], (EMBED_DIM, 128), jnp.float32, -lim, lim)
        inp['pb'] = jax.random.uniform(ks[4], (EMBED_DIM,), jnp.float32, -lim, lim)
        return inp
    _L0_tok_all = _L0_tok_setup()
    _L0_tok_in = {k: v for k, v in _L0_tok_all.items() if k in ('cw0', 'cb0', 'gw0', 'gb0', 'cw1', 'cb1', 'gw1', 'gb1', 'cw2', 'cb2', 'gw2', 'gb2', 'cw3', 'cb3', 'gw3', 'gb3', 'cw4', 'cb4', 'gw4', 'gb4', 'cw5', 'cb5', 'gw5', 'gb5', 'pw', 'pb')}
    del _L0_tok_all

    def _L0_attn_setup():
        import jax, jax.numpy as jnp
        import numpy as np
        import math
        D_MODEL = 192
        N_HEADS = 6
        HD = D_MODEL // N_HEADS
        RANK = D_MODEL // 4
        B, T = (128, 64)

        def _rope_tables(T, dim):
            inv = 1.0 / 10000.0 ** (jnp.arange(0, dim, 2, dtype=jnp.float32) / dim)
            t = jnp.arange(T, dtype=jnp.float32)
            freqs = jnp.outer(t, inv)
            emb = jnp.concatenate([freqs, freqs], axis=-1)
            return (jnp.cos(emb), jnp.sin(emb))

        def _rot(x):
            h = x.shape[-1] // 2
            return jnp.concatenate([-x[..., h:], x[..., :h]], axis=-1)
        key = jax.random.key(seed)
        ks = jax.random.split(key, 8)
        s_in = 1.0 / math.sqrt(D_MODEL)
        s_r = 1.0 / math.sqrt(RANK)
        inp = {'x': jax.random.normal(ks[0], (B, T, D_MODEL), dtype=jnp.float32), 'qA': jax.random.normal(ks[1], (D_MODEL, RANK), dtype=jnp.float32) * s_in, 'qB': jax.random.normal(ks[2], (RANK, D_MODEL), dtype=jnp.float32) * s_r, 'kA': jax.random.normal(ks[3], (D_MODEL, RANK), dtype=jnp.float32) * s_in, 'kB': jax.random.normal(ks[4], (RANK, D_MODEL), dtype=jnp.float32) * s_r, 'vA': jax.random.normal(ks[5], (D_MODEL, RANK), dtype=jnp.float32) * s_in, 'vB': jax.random.normal(ks[6], (RANK, D_MODEL), dtype=jnp.float32) * s_r, 'o_w': jax.random.normal(ks[7], (D_MODEL, D_MODEL), dtype=jnp.float32) * s_in}
        return inp
    _L0_attn_all = _L0_attn_setup()
    _L0_attn_in = {k: v for k, v in _L0_attn_all.items() if k in ('qA', 'qB', 'kA', 'kB', 'vA', 'vB', 'o_w')}
    del _L0_attn_all

    def _L0_ffn_setup():
        import jax, jax.numpy as jnp
        import numpy as np
        DECAY = 0.9
        EPS = 0.01
        TOP_K = 2
        key = jax.random.key(seed)
        k1, k2, k3, k4 = jax.random.split(key, 4)
        B, S, H, I, E = (4, 512, 192, 512, 8)
        return {'hidden_states': jax.random.normal(k1, (B, S, H), jnp.float32), 'router_w': jax.random.normal(k2, (E, H), jnp.float32) * 0.02, 'w1': jax.random.normal(k3, (E, I, H), jnp.float32) * 0.02, 'w2': jax.random.normal(k4, (E, H, I), jnp.float32) * 0.02}
    _L0_ffn_all = _L0_ffn_setup()
    _L0_ffn_in = {k: v for k, v in _L0_ffn_all.items() if k in ('router_w', 'w1', 'w2')}
    del _L0_ffn_all
    return {'x': x, 'L0_tok_cw0': _L0_tok_in['cw0'], 'L0_tok_cb0': _L0_tok_in['cb0'], 'L0_tok_gw0': _L0_tok_in['gw0'], 'L0_tok_gb0': _L0_tok_in['gb0'], 'L0_tok_cw1': _L0_tok_in['cw1'], 'L0_tok_cb1': _L0_tok_in['cb1'], 'L0_tok_gw1': _L0_tok_in['gw1'], 'L0_tok_gb1': _L0_tok_in['gb1'], 'L0_tok_cw2': _L0_tok_in['cw2'], 'L0_tok_cb2': _L0_tok_in['cb2'], 'L0_tok_gw2': _L0_tok_in['gw2'], 'L0_tok_gb2': _L0_tok_in['gb2'], 'L0_tok_cw3': _L0_tok_in['cw3'], 'L0_tok_cb3': _L0_tok_in['cb3'], 'L0_tok_gw3': _L0_tok_in['gw3'], 'L0_tok_gb3': _L0_tok_in['gb3'], 'L0_tok_cw4': _L0_tok_in['cw4'], 'L0_tok_cb4': _L0_tok_in['cb4'], 'L0_tok_gw4': _L0_tok_in['gw4'], 'L0_tok_gb4': _L0_tok_in['gb4'], 'L0_tok_cw5': _L0_tok_in['cw5'], 'L0_tok_cb5': _L0_tok_in['cb5'], 'L0_tok_gw5': _L0_tok_in['gw5'], 'L0_tok_gb5': _L0_tok_in['gb5'], 'L0_tok_pw': _L0_tok_in['pw'], 'L0_tok_pb': _L0_tok_in['pb'], 'L0_attn_qA': _L0_attn_in['qA'], 'L0_attn_qB': _L0_attn_in['qB'], 'L0_attn_kA': _L0_attn_in['kA'], 'L0_attn_kB': _L0_attn_in['kB'], 'L0_attn_vA': _L0_attn_in['vA'], 'L0_attn_vB': _L0_attn_in['vB'], 'L0_attn_o_w': _L0_attn_in['o_w'], 'L0_ffn_router_w': _L0_ffn_in['router_w'], 'L0_ffn_w1': _L0_ffn_in['w1'], 'L0_ffn_w2': _L0_ffn_in['w2']}

def reference(x, L0_tok_cw0, L0_tok_cb0, L0_tok_gw0, L0_tok_gb0, L0_tok_cw1, L0_tok_cb1, L0_tok_gw1, L0_tok_gb1, L0_tok_cw2, L0_tok_cb2, L0_tok_gw2, L0_tok_gb2, L0_tok_cw3, L0_tok_cb3, L0_tok_gw3, L0_tok_gb3, L0_tok_cw4, L0_tok_cb4, L0_tok_gw4, L0_tok_gb4, L0_tok_cw5, L0_tok_cb5, L0_tok_gw5, L0_tok_gb5, L0_tok_pw, L0_tok_pb, L0_attn_qA, L0_attn_qB, L0_attn_kA, L0_attn_kB, L0_attn_vA, L0_attn_vB, L0_attn_o_w, L0_ffn_router_w, L0_ffn_w1, L0_ffn_w2):
    import jax
    import jax.numpy as jnp

    def _L0_tok_ref(x, cw0, cb0, gw0, gb0, cw1, cb1, gw1, gb1, cw2, cb2, gw2, gb2, cw3, cb3, gw3, gb3, cw4, cb4, gw4, gb4, cw5, cb5, gw5, gb5, pw, pb):
        import jax, jax.numpy as jnp
        import numpy as np
        from jax import lax
        CONV_LAYERS = [(128, 10, 5), (128, 3, 2), (128, 3, 2), (128, 3, 2), (128, 3, 2), (128, 2, 2)]
        NUM_GROUPS = 32
        EPS = 1e-05
        EMBED_DIM = 192

        def _block(x, cw, cb, gw, gb, stride):
            y = lax.conv_general_dilated(x, cw, (stride,), 'VALID', dimension_numbers=('NCH', 'OIH', 'NCH'))
            y = y + cb[None, :, None]
            B, C, T = y.shape
            yg = y.reshape(B, NUM_GROUPS, C // NUM_GROUPS * T)
            mu = yg.mean(axis=-1, keepdims=True)
            var = yg.var(axis=-1, keepdims=True)
            yn = ((yg - mu) * lax.rsqrt(var + EPS)).reshape(B, C, T)
            yn = yn * gw[None, :, None] + gb[None, :, None]
            return jax.nn.gelu(yn)

        def _forward(x, conv_params, pw, pb):
            h = x[:, None, :]
            for (cw, cb, gw, gb), (_, _, s) in zip(conv_params, CONV_LAYERS):
                h = _block(h, cw, cb, gw, gb, s)
            h = jnp.transpose(h, (0, 2, 1))
            return jnp.einsum('bfc,ec->bfe', h, pw) + pb
        conv_params = [(cw0, cb0, gw0, gb0), (cw1, cb1, gw1, gb1), (cw2, cb2, gw2, gb2), (cw3, cb3, gw3, gb3), (cw4, cb4, gw4, gb4), (cw5, cb5, gw5, gb5)]
        return _forward(x, conv_params, pw, pb)

    def _L0_attn_ref(x, qA, qB, kA, kB, vA, vB, o_w):
        import jax, jax.numpy as jnp
        import numpy as np
        import math
        D_MODEL = 192
        N_HEADS = 6
        HD = D_MODEL // N_HEADS
        RANK = D_MODEL // 4
        B, T = (128, 64)

        def _rope_tables(T, dim):
            inv = 1.0 / 10000.0 ** (jnp.arange(0, dim, 2, dtype=jnp.float32) / dim)
            t = jnp.arange(T, dtype=jnp.float32)
            freqs = jnp.outer(t, inv)
            emb = jnp.concatenate([freqs, freqs], axis=-1)
            return (jnp.cos(emb), jnp.sin(emb))

        def _rot(x):
            h = x.shape[-1] // 2
            return jnp.concatenate([-x[..., h:], x[..., :h]], axis=-1)
        Bb, Tt, _ = x.shape

        def proj(A, W):
            h = x @ A @ W
            return h.reshape(Bb, Tt, N_HEADS, HD).transpose(0, 2, 1, 3)
        q = proj(qA, qB)
        k = proj(kA, kB)
        v = proj(vA, vB)
        cos, sin = _rope_tables(Tt, HD)
        q = q * cos + _rot(q) * sin
        k = k * cos + _rot(k) * sin
        att = jnp.einsum('bhqd,bhkd->bhqk', q, k) / math.sqrt(HD)
        causal = jnp.tril(jnp.ones((Tt, Tt), dtype=bool))
        att = jnp.where(causal, att, -jnp.inf)
        att = jax.nn.softmax(att, axis=-1)
        out = jnp.einsum('bhqk,bhkd->bhqd', att, v)
        out = out.transpose(0, 2, 1, 3).reshape(Bb, Tt, D_MODEL)
        return out @ o_w

    def _L0_ffn_ref(hidden_states, router_w, w1, w2):
        import jax, jax.numpy as jnp
        import numpy as np
        DECAY = 0.9
        EPS = 0.01
        TOP_K = 2
        B, S, H = hidden_states.shape
        E = router_w.shape[0]
        flat = hidden_states.reshape(B * S, H)
        logits = flat @ router_w.T
        probs = jax.nn.softmax(logits, axis=-1)
        topk_probs, topk_idx = jax.lax.top_k(probs, TOP_K)
        importance = jax.lax.stop_gradient(probs).sum(axis=0)
        running = jnp.ones((E,), dtype=flat.dtype)
        blended = running + (1.0 - DECAY) * (importance - running)
        running = blended + EPS
        balance = running[topk_idx]
        balanced = topk_probs / balance
        balanced = balanced / balanced.sum(axis=-1, keepdims=True)
        h = jnp.einsum('th,eih->tei', flat, w1)
        h = jax.nn.silu(h)
        outs = jnp.einsum('tei,ehi->teh', h, w2)
        sel = jnp.take_along_axis(outs, topk_idx[:, :, None], axis=1)
        combined = (sel * balanced[..., None]).sum(axis=1)
        return combined.reshape(B, S, H)
    h = _L0_tok_ref(x, L0_tok_cw0, L0_tok_cb0, L0_tok_gw0, L0_tok_gb0, L0_tok_cw1, L0_tok_cb1, L0_tok_gw1, L0_tok_gb1, L0_tok_cw2, L0_tok_cb2, L0_tok_gw2, L0_tok_gb2, L0_tok_cw3, L0_tok_cb3, L0_tok_gw3, L0_tok_gb3, L0_tok_cw4, L0_tok_cb4, L0_tok_gw4, L0_tok_gb4, L0_tok_cw5, L0_tok_cb5, L0_tok_gw5, L0_tok_gb5, L0_tok_pw, L0_tok_pb)
    h = h + _L0_attn_ref(_layernorm(h, axis=-1), L0_attn_qA, L0_attn_qB, L0_attn_kA, L0_attn_kB, L0_attn_vA, L0_attn_vB, L0_attn_o_w)
    h = h + _L0_ffn_ref(_layernorm(h, axis=-1), L0_ffn_router_w, L0_ffn_w1, L0_ffn_w2)
    return h

_drawn_inputs = setup_inputs


def setup_inputs(seed=0):
    import zlib

    import numpy as np

    out = dict(_drawn_inputs(seed))
    spreads = {'L0_tok_gw0': (1.0, 0.2),
     'L0_tok_gb0': (0.0, 0.1),
     'L0_tok_gw1': (1.0, 0.2),
     'L0_tok_gb1': (0.0, 0.1),
     'L0_tok_gw2': (1.0, 0.2),
     'L0_tok_gb2': (0.0, 0.1),
     'L0_tok_gw3': (1.0, 0.2),
     'L0_tok_gb3': (0.0, 0.1),
     'L0_tok_gw4': (1.0, 0.2),
     'L0_tok_gb4': (0.0, 0.1),
     'L0_tok_gw5': (1.0, 0.2),
     'L0_tok_gb5': (0.0, 0.1)}
    factors = {}
    for name, (base, spread) in spreads.items():
        noise = np.random.default_rng([zlib.crc32(name.encode()), seed]).standard_normal(out[name].shape)
        drawn = base * np.exp(spread * noise) if base else spread * noise
        out[name] = jnp.asarray(drawn.astype(out[name].dtype))
    for name, factor in factors.items():
        out[name] = (out[name] * factor).astype(out[name].dtype)
    return out
```

```python
from contextlib import ExitStack

import numpy as np

import concourse.bass as bass
from concourse import mybir

F32 = mybir.dt.float32
F16 = mybir.dt.float16
BF16 = mybir.dt.bfloat16
ALU = mybir.AluOpType
ACT = mybir.ActivationFunctionType
AX = mybir.AxisListType

P = 128
B, T_IN = 16, 40000
C = 128
GROUP = 4
E = 192
EPS = 1e-5
T0 = (T_IN - 10) // 5 + 1
T1 = (T0 - 3) // 2 + 1
T2 = (T1 - 3) // 2 + 1
T3 = (T2 - 3) // 2 + 1
T4 = (T3 - 3) // 2 + 1
T5 = (T4 - 2) // 2 + 1
U = 1000
HU = U // 2
WIN = 45
XR = WIN + 1
K0 = 10
LO = 64
S0 = 1024.0
UT = (U + P - 1) // P
TAILROWS = U - (UT - 1) * P
TQ = [P, T5 - P]

HEADS, HD = 6, 32
RANK = E // 4
NE, HID = 8, 512
HT = HID // P
GT = 4
NGRP = 2 * B // GT
DECAY, LOAD_EPS = 0.9, 0.01

MISC_PER_BODY = 14
STEPS = 37


def half_cols(last, h):
    return HU - 1 if last and h == 1 else HU


def taps_of(plane_out, planes_in, h, n, taps=3):
    for k in range(taps):
        q = 2 * plane_out + k
        shift = 1 if q >= planes_in else 0
        yield k, q % planes_in, h * HU + shift, n


def audio_tower(nc, io):
    with ExitStack() as whole:
        tok = whole.enter_context(nc.sbuf_tensor("tok", [P, B, 2, E], F32))
        ident = whole.enter_context(nc.sbuf_tensor("ident", [P, P], F32))
        mhalf = whole.enter_context(nc.sbuf_tensor("mhalf", [P, 32], F32))
        with ExitStack() as ctx:
            conv_stage(nc, io, ctx, tok, ident, mhalf)
        with ExitStack() as ctx:
            attention_stage(nc, io, ctx, tok, ident, mhalf)
        with ExitStack() as ctx:
            expert_stage(nc, io, ctx, tok, ident, mhalf)


def conv_stage(nc, io, ctx, tok, ident, mhalf):
    def sb(name, shape, dt=F32):
        return ctx.enter_context(nc.sbuf_tensor(name, shape, dt))

    def sem(name):
        return ctx.enter_context(nc.semaphore(name))

    gavg = sb("gavg", [P, P])
    sel = sb("sel", [XR, 8, K0 + 1])
    ones = sb("ones", [P, 1])
    chan = sb("chan", [P, 6, 3])
    w0f = sb("w0f", [P, 8, C])
    w0s = sb("w0s", [P, 2, 8, C], F16)
    w11 = sb("w11", [K0 + 1, C])
    w = [None] + [sb(f"w{l}", [P, 3 if l < 5 else 2, C]) for l in range(1, 6)]
    pw = sb("pw", [P, E])
    pb = sb("pb", [P, E])
    xu = sb("xu", [P, UT, XR])
    lastp = sb("lastp", [1, 2, K0 + 1])
    xs = sb("xs", [P, U], F16)
    h0 = sb("h0", [P, 8, U])
    h1 = sb("h1", [P, 4, U])
    h2 = sb("h2", [P, 2, U])
    h3 = sb("h3", [P, U])
    h4 = sb("h4", [P, T4])
    h5 = sb("h5", [P, T5])
    gram = sb("gram", [XR, XR])
    gsel = sb("gsel", [XR, 8, K0 + 1])
    g11 = sb("g11", [K0 + 1, K0 + 1])
    q11 = sb("q11", [K0 + 1, C])
    bn = sb("bn", [P, 8, 6])
    bn1 = sb("bn1", [P, 8, 6])
    st = sb("st", [P, 6, 2])
    gm = sb("gm", [P, 6, 2])
    var = sb("var", [P, 6, 3])
    rstd = sb("rstd", [P, 6])
    dmean = sb("dmean", [P, 6])
    gscale = sb("gscale", [P, 6])
    gbias = sb("gbias", [P, 6])
    scale0 = sb("scale0", [P, 1])

    ring = [ctx.enter_context(nc.psum_tensor(f"ring{i}", [P, 512], F32)) for i in range(3)]
    misc = ctx.enter_context(nc.psum_tensor("misc", [P, 512], F32))
    tail = [ctx.enter_context(nc.psum_tensor(f"tail{i}", [P, 512], F32)) for i in range(4)]

    loads = sem("loads")
    w0_loads = sem("w0_loads")
    x_loads = sem("x_loads")
    x_used = sem("x_used")
    ready = sem("ready")
    pe_conv = [sem(f"pe_l{l}") for l in range(6)]
    pe_misc = sem("pe_misc")
    dve_misc = sem("dve_misc")
    l1_out = sem("l1_out")
    stats = [sem(f"stats{l}") for l in range(6)]
    pow_in = sem("pow_in")
    pow_out = sem("pow_out")
    norm = [sem(f"norm{l}") for l in range(6)]
    gelu = [sem(f"gelu{l}") for l in range(6)]
    step = sem("step")
    alone = sem("alone")

    CH = {0: 16, 1: 8, 2: 4, 3: 2, 4: 1, 5: 1}

    with nc.Block() as block:
        @block.sync
        def _(sp):
            sp.dma_start(chan[:], io["chan"]).then_inc(loads, 16)
            sp.dma_start(ident[:], io["ident"]).then_inc(loads, 16)
            sp.dma_start(gavg[:], io["gavg"]).then_inc(loads, 16)
            sp.dma_start(sel[:], io["sel"]).then_inc(loads, 16)
            sp.dma_start(w11[:], io["w11"]).then_inc(loads, 16)
            sp.dma_start(w0f[:], io["w0win"]).then_inc(w0_loads, 16)

            def load_x(b):
                sp.dma_start(xu[:], io["xw"][b]).then_inc(x_loads, 16)
                sp.dma_start(lastp[:, 0, :], io["xlast"][b]).then_inc(x_loads, 16)

            load_x(0)
            for l in range(1, 6):
                sp.dma_start(w[l][:], io[f"w{l}T"]).then_inc(loads, 16)
            sp.dma_start(pw[:], io["pwT"]).then_inc(loads, 16)
            sp.dma_start(pb[:], io["pb"].broadcast_to([P, E])).then_inc(loads, 16)
            with sp.Fori(1, B) as b:
                sp.wait_ge(x_used, b)
                load_x(b)

        LOADS_ALL = 16 * 12
        X_LOADS = 16 * 2

        @block.tensor
        def _(pe):
            def misc_free(m, apart=False):
                if not (isinstance(m[0], int) and m[0] == 0):
                    pe.wait_ge(dve_misc, m[0])
                    if apart:
                        pe.sem_inc(alone, 1)
                m[0] = m[0] + 1

            def transposes(h, b, m):
                if h == 0:
                    pe.wait_ge(x_loads, (b + 1) * X_LOADS)
                misc_free(m, apart=True)
                for j in range(4 * h, 4 * h + 4):
                    rows = P if j < UT - 1 else TAILROWS
                    mm = pe.transpose(misc[0:XR, (j % 4) * P:(j % 4) * P + rows], xu[0:rows, j, :],
                                      ident[0:rows, 0:rows])
                mm.then_inc(pe_misc, 1)

            def gram_matrix(m):
                misc_free(m)
                for j in range(UT):
                    rows = P if j < UT - 1 else TAILROWS
                    mm = pe.matmul(misc[0:XR, 0:XR], xu[0:rows, j, :], xu[0:rows, j, :],
                                   start=(j == 0), stop=(j == UT - 1))
                mm.then_inc(pe_misc, 1)

            def gram_select(m):
                misc_free(m, apart=True)
                pe.matmul(misc[0:XR, 0:88], gram[:], sel[:].rearrange("p v k -> p (v k)"),
                          start=True, stop=True).then_inc(pe_misc, 1)

            def gram_taps(m):
                misc_free(m, apart=True)
                pe.matmul(misc[0:K0 + 1, 0:K0 + 1], lastp[:, 1, :], lastp[:, 0, :],
                          start=True, stop=False).then_inc(x_used, 1)
                for v in range(8):
                    mm = pe.matmul(misc[0:K0 + 1, 0:K0 + 1], sel[:, v, :], gsel[:, v, :],
                                   start=False, stop=(v == 7))
                mm.then_inc(pe_misc, 1)

            def gram_weights(m):
                misc_free(m, apart=True)
                pe.matmul(misc[0:K0 + 1, 0:C], g11[:], w11[:], start=True, stop=True).then_inc(pe_misc, 1)

            def moments0(m, b):
                misc_free(m)
                pe.matmul(misc[:, 0:1], w11[:], g11[:, K0:K0 + 1], start=True, stop=True)
                pe.matmul(misc[:, 1:2], q11[:], ones[0:K0 + 1, :], start=True, stop=True).then_inc(pe_misc, 1)

            def group_mean(l, m, b):
                if l > 0:
                    pe.wait_ge(stats[l], b + 1)
                misc_free(m)
                pe.matmul(misc[:, 0:2], gavg[:], st[:, l, :], start=True, stop=True).then_inc(pe_misc, 1)

            def ring_free(k, b):
                if k < 3:
                    pe.wait_ge(gelu[0], 16 * (b + 1) + k - 3 + 1)
                elif k < 11:
                    pe.wait_ge(l1_out, 8 * b + k - 3 + 1)
                else:
                    pe.wait_ge(gelu[0], 16 * (b + 1) + k - 8 - 3 + 1)

            def conv0(c, b, ringed=True):
                v, h = c // 2, c % 2
                n = half_cols(v == 7, h)
                bank = ring[(8 + c) % 3]
                if ringed:
                    ring_free(8 + c, b - 1)
                elif c >= 3:
                    pe.wait_ge(gelu[0], c - 2)
                for part in range(2):
                    mm = pe.matmul(bank[:, 0:n], w0s[0:LO + XR, part, v, :], xs[0:LO + XR, h * HU:h * HU + n],
                                   start=(part == 0), stop=(part == 1))
                mm.then_inc(pe_conv[0], 1)

            def conv1(c, b):
                q, h = c // 2, c % 2
                n = half_cols(q == 3, h)
                ring_free(c, b)
                pe.wait_ge(gelu[0], 16 * b + (min(2 * (2 * q + 2) + h + 1, 16)))
                for k, plane, col, n in taps_of(q, 8, h, n):
                    mm = pe.matmul(ring[c % 3][:, 0:n], w[1][:, k, :], h0[:, plane, col:col + n],
                                   start=(k == 0), stop=(k == 2))
                mm.then_inc(pe_conv[1], 1)

            def conv2(c, b):
                q, h = c // 2, c % 2
                n = half_cols(q == 1, h)
                if c == 0 and not (isinstance(b, int) and b == 0):
                    pe.wait_ge(gelu[5], b)
                pe.wait_ge(gelu[1], 8 * b + (3, 6, 7, 8)[c])
                for k, plane, col, n in taps_of(q, 4, h, n):
                    mm = pe.matmul(tail[c][:, 0:n], w[2][:, k, :], h1[:, plane, col:col + n],
                                   start=(k == 0), stop=(k == 2))
                mm.then_inc(pe_conv[2], 1)

            def conv3(c, b):
                n = half_cols(True, c)
                pe.wait_ge(gelu[2], 4 * b + 4)
                for k, plane, col, n in taps_of(0, 2, c, n):
                    mm = pe.matmul(tail[c][:, 0:n], w[3][:, k, :], h2[:, plane, col:col + n],
                                   start=(k == 0), stop=(k == 2))
                mm.then_inc(pe_conv[3], 1)

            def conv45(l, b):
                src, n, taps = (h3, T4, 3) if l == 4 else (h4, T5, 2)
                pe.wait_ge(gelu[l - 1], CH[l - 1] * (b + 1))
                for k in range(taps):
                    mm = pe.matmul(tail[l - 2][:, 0:n], w[l][:, k, :], src[:, k:k + 2 * n - 1:2],
                                   start=(k == 0), stop=(k == taps - 1))
                mm.then_inc(pe_conv[l], 1)

            def project(m, b):
                pe.wait_ge(gelu[5], b + 1)
                misc_free(m)
                for t in range(2):
                    mm = pe.matmul(misc[0:TQ[t], t * E:(t + 1) * E], h5[:, t * P:t * P + TQ[t]], pw[:],
                                   start=(t == 0), stop=(t == 1), skip_group_check=True)
                mm.then_inc(pe_misc, 1)

            def body(b, m, before, after):
                conv1(0, b)
                if before:
                    group_mean(2, m, b - 1)
                if after:
                    transposes(0, b + 1, m)
                conv1(1, b)
                if after:
                    transposes(1, b + 1, m)
                conv1(2, b)
                if after:
                    gram_matrix(m)
                if before:
                    conv3(0, b - 1)
                    conv3(1, b - 1)
                conv1(3, b)
                if before:
                    group_mean(3, m, b - 1)
                if after:
                    gram_select(m)
                conv1(4, b)
                if after:
                    gram_taps(m)
                if before:
                    conv45(4, b - 1)
                conv1(5, b)
                if before:
                    group_mean(4, m, b - 1)
                if after:
                    gram_weights(m)
                conv1(6, b)
                if after:
                    moments0(m, b + 1)
                if before:
                    conv45(5, b - 1)
                conv1(7, b)
                if after:
                    group_mean(0, m, b + 1)
                if before:
                    group_mean(5, m, b - 1)
                if after:
                    for c in range(3):
                        conv0(c, b + 1)
                group_mean(1, m, b)
                if after:
                    for c in range(3, 5):
                        conv0(c, b + 1)
                if before:
                    project(m, b - 1)
                for c in range(4):
                    conv2(c, b)
                    if after:
                        for k in range(5 + 3 * c, min(8 + 3 * c, 16)):
                            conv0(k, b + 1)

            pe.wait_ge(loads, LOADS_ALL)
            pe.wait_ge(ready, 2)
            m = [0]
            transposes(0, 0, m)
            transposes(1, 0, m)
            gram_matrix(m)
            gram_select(m)
            gram_taps(m)
            gram_weights(m)
            moments0(m, 0)
            group_mean(0, m, 0)
            for c in range(16):
                conv0(c, 0, ringed=False)
            body(0, m, False, True)
            base = m[0]
            with pe.Fori(1, B - 1) as b:
                m = [(b - 1) * MISC_PER_BODY + base]
                body(b, m, True, True)
            m = [base + (B - 2) * MISC_PER_BODY]
            body(B - 1, m, True, False)
            b = B
            group_mean(2, m, b - 1)
            conv3(0, b - 1)
            conv3(1, b - 1)
            group_mean(3, m, b - 1)
            conv45(4, b - 1)
            group_mean(4, m, b - 1)
            conv45(5, b - 1)
            group_mean(5, m, b - 1)
            project(m, b - 1)

        @block.scalar
        def _(act):
            def norm_gelu(l, c, b, out, psum, n, scale=None):
                if c == 0:
                    act.wait_ge(norm[l], b + 1)
                if l != 1:
                    act.wait_ge(pe_conv[l], CH[l] * b + c + 1)
                act.activation(out, psum, ACT.Gelu_apprx_tanh, bias=gbias[:, l:l + 1],
                               scale=gscale[:, l:l + 1] if scale is None else scale).then_inc(gelu[l], 1)

            def gelu0(c, b, bank):
                v, h = c // 2, c % 2
                n = half_cols(v == 7, h)
                norm_gelu(0, c, b, h0[:, v, h * HU:h * HU + n], bank[:, 0:n], n, scale=scale0[:, 0:1])

            def gelu1(i, b):
                q, h = ((0, 0), (1, 0), (2, 0), (0, 1), (1, 1), (2, 1), (3, 0), (3, 1))[i]
                n = half_cols(q == 3, h)
                s = h1[:, q, h * HU:h * HU + n]
                norm_gelu(1, i, b, s, s, n)

            def gelu2(c, b):
                q, h = c // 2, c % 2
                n = half_cols(q == 1, h)
                norm_gelu(2, c, b, h2[:, q, h * HU:h * HU + n], tail[c][:, 0:n], n)

            def gelu3(c, b):
                n = half_cols(True, c)
                norm_gelu(3, c, b, h3[:, c * HU:c * HU + n], tail[c][:, 0:n], n)

            def late(b):
                for c in range(4):
                    gelu2(c, b)
                for c in range(2):
                    gelu3(c, b)
                norm_gelu(4, 0, b, h4[:, 0:T4], tail[2][:, 0:T4], T4)
                norm_gelu(5, 0, b, h5[:, 0:T5], tail[3][:, 0:T5], T5)

            def body(b, before, after):
                if before:
                    late(b - 1)
                if after:
                    for c in range(5):
                        gelu0(c, b + 1, ring[(8 + c) % 3])
                for i in range(8):
                    gelu1(i, b)
                if after:
                    for c in range(5, 16):
                        gelu0(c, b + 1, ring[(8 + c) % 3])

            for c in range(16):
                gelu0(c, 0, ring[(8 + c) % 3])
            body(0, False, True)
            with act.Fori(1, B - 1) as b:
                body(b, True, True)
            body(B - 1, True, False)
            late(B - 1)

        @block.gpsimd
        def _(pool):
            order0 = [0]
            body_first, body_mid, body_last, end = [0, 1], [2, 3, 4, 0, 5, 1], [2, 3, 4, 5, 1], [2, 3, 4, 5]
            pool.wait_ge(ready, 1)

            def powers(order, base):
                for i, l in enumerate(order):
                    pool.wait_ge(pow_in, base + (i + 1))
                    pool.tensor_tensor(rstd[:, l:l + 1], var[:, l, 2:3], mhalf[:, 0:1], ALU.pow).then_inc(pow_out, 1)

            powers(order0, 0)
            powers(body_first, 1)
            with pool.Fori(1, B - 1) as b:
                powers(body_mid, b * 6 - 3)
            powers(body_last, 6 * (B - 1) - 3)
            powers(end, 6 * (B - 1) - 3 + 5)

        @block.vector
        def _(dve):
            s = [0]
            count = [0]
            pw_n = [0]

            def then(ins):
                ins.then_inc(step, 1)
                s[0] = s[0] + 1
                count[0] += 1
                dve.wait_ge(step, s[0])

            def misc_there(m):
                m[0] = m[0] + 1
                dve.wait_ge(pe_misc, m[0])

            def split_x(h, m):
                n = (4 * P, U - 4 * P)[h]
                hi = xs[0:XR, h * 4 * P:h * 4 * P + n]
                misc_there(m)
                then(dve.tensor_copy(hi, misc[0:XR, 0:n]))
                dve.tensor_tensor(xs[LO:LO + XR, h * 4 * P:h * 4 * P + n], misc[0:XR, 0:n], hi,
                                  ALU.subtract).then_inc(dve_misc, 1)

            def keep(m, out, width, rows, scale=None):
                misc_there(m)
                src = misc[0:rows, 0:width]
                if scale is None:
                    dve.tensor_copy(out, src).then_inc(dve_misc, 1)
                else:
                    dve.tensor_scalar(out, src, scale, None, ALU.mult).then_inc(dve_misc, 1)

            def neg_last():
                then(dve.tensor_scalar(lastp[:, 1, :], lastp[:, 0, :], -1.0, None, ALU.mult))

            def finish_norm(l, m):
                misc_there(m)
                mean, sq = gm[:, l, 0:1], gm[:, l, 1:2]
                dve.tensor_copy(gm[:, l, :], misc[:, 0:2]).then_inc(dve_misc, 1)
                dve.wait_ge(dve_misc, m[0])
                then(dve.scalar_tensor_tensor(out=var[:, l, 0:1], in0=mean, scalar=mean, in1=sq,
                                              op0=ALU.mult, op1=ALU.subtract))
                then(dve.tensor_scalar(var[:, l, 1:2], var[:, l, 0:1], -1.0, 0.0, ALU.mult, ALU.max))
                dve.tensor_scalar(var[:, l, 2:3], var[:, l, 1:2], EPS, None, ALU.add).then_inc(pow_in, 1)
                if l == 0:
                    dve.tensor_scalar(dmean[:, l:l + 1], mean, -1.0, None, ALU.mult)
                else:
                    dve.tensor_tensor(dmean[:, l:l + 1], chan[:, l, 0:1], mean, ALU.subtract)
                pw_n[0] = pw_n[0] + 1
                dve.wait_ge(pow_out, pw_n[0])
                then(dve.tensor_tensor(gscale[:, l:l + 1], rstd[:, l:l + 1], chan[:, l, 1:2], ALU.mult))
                if l == 0:
                    then(dve.tensor_scalar(scale0[:], gscale[:, l:l + 1], 1.0 / S0, None, ALU.mult))
                dve.scalar_tensor_tensor(out=gbias[:, l:l + 1], in0=dmean[:, l:l + 1], scalar=gscale[:, l:l + 1],
                                         in1=chan[:, l, 2:3], op0=ALU.mult, op1=ALU.add).then_inc(norm[l], 1)

            def moments(l, bn, chunks):
                dve.sem_inc(alone, 1)
                then(dve.bn_aggr(st[:, l, :], bn[:, 0:chunks, :].rearrange("p c s -> p (c s)")))
                then(dve.tensor_tensor(st[:, l, 0:1], st[:, l, 0:1], chan[:, l, 0:1], ALU.add))
                dve.scalar_tensor_tensor(out=st[:, l, 1:2], in0=st[:, l, 0:1], scalar=st[:, l, 0:1],
                                         in1=st[:, l, 1:2], op0=ALU.mult, op1=ALU.add).then_inc(stats[l], 1)

            def out1(c, b):
                q, h = c // 2, c % 2
                n = half_cols(q == 3, h)
                y = h1[:, q, h * HU:h * HU + n]
                dve.wait_ge(pe_conv[1], 8 * b + c + 1)
                dve.tensor_copy(y, ring[c % 3][:, 0:n]).then_inc(l1_out, 1)
                dve.wait_ge(l1_out, 8 * b + c + 1)
                ins = dve.bn_stats(bn1[:, c, :], y)
                if c == 7:
                    then(ins)
                    moments(1, bn1, 8)

            def stats_of(l, b):
                for c in range(CH[l]):
                    n = {2: half_cols(c >= 2, c % 2), 3: half_cols(True, c), 4: T4, 5: T5}[l]
                    bank = tail[c] if l < 4 else tail[l - 2]
                    dve.wait_ge(pe_conv[l], CH[l] * b + c + 1)
                    ins = dve.bn_stats(bn[:, c, :], bank[:, 0:n])
                then(ins)
                moments(l, bn, CH[l])

            def tokens(m, b):
                misc_there(m)
                dve.tensor_tensor(tok[:, b, 0, :], misc[:, 0:E], pb[:], ALU.add)
                dve.tensor_tensor(tok[0:TQ[1], b, 1, :], misc[0:TQ[1], E:2 * E], pb[0:TQ[1], :],
                                  ALU.add).then_inc(dve_misc, 1)

            def prep(i, m, b):
                if i == 0:
                    split_x(0, m)
                elif i == 1:
                    split_x(1, m)
                elif i == 2:
                    neg_last()
                    keep(m, gram[:], XR, XR)
                elif i == 3:
                    keep(m, gsel[:].rearrange("p v k -> p (v k)"), 88, XR)
                elif i == 4:
                    keep(m, g11[:], K0 + 1, K0 + 1, scale=1.0 / T0)
                elif i == 5:
                    misc_there(m)
                    dve.tensor_tensor(q11[:], misc[0:K0 + 1, 0:C], w11[:], ALU.mult).then_inc(dve_misc, 1)
                elif i == 6:
                    misc_there(m)
                    dve.tensor_copy(st[:, 0, :], misc[:, 0:2]).then_inc(dve_misc, 1)

            def body(b, m, before, after):
                out1(0, b)
                if before:
                    finish_norm(2, m)
                if after:
                    prep(0, m, b)
                out1(1, b)
                if after:
                    prep(1, m, b)
                out1(2, b)
                if after:
                    prep(2, m, b)
                if before:
                    stats_of(3, b - 1)
                out1(3, b)
                if before:
                    finish_norm(3, m)
                if after:
                    prep(3, m, b)
                out1(4, b)
                if after:
                    prep(4, m, b)
                if before:
                    stats_of(4, b - 1)
                out1(5, b)
                if before:
                    finish_norm(4, m)
                if after:
                    prep(5, m, b)
                out1(6, b)
                if after:
                    prep(6, m, b)
                if before:
                    stats_of(5, b - 1)
                out1(7, b)
                if after:
                    finish_norm(0, m)
                if before:
                    finish_norm(5, m)
                finish_norm(1, m)
                if before:
                    tokens(m, b - 1)
                stats_of(2, b)

            dve.memset(ones[:], 1.0)
            dve.memset(tok[:, :, 1, :], 0.0)
            dve.memset(xs[:], 0.0)
            dve.memset(mhalf[:], -0.5).then_inc(ready, 1)
            dve.wait_ge(w0_loads, 16)
            then(dve.tensor_scalar(w0f[:], w0f[:], S0, None, ALU.mult))
            then(dve.tensor_copy(w0s[:, 0, :, :], w0f[:]))
            dve.tensor_tensor(w0s[:, 1, :, :], w0f[:], w0s[:, 0, :, :], ALU.subtract).then_inc(ready, 1)
            dve.wait_ge(loads, LOADS_ALL)
            m = [0]
            dve.wait_ge(x_loads, X_LOADS)
            for i in range(7):
                prep(i, m, -1)
            finish_norm(0, m)
            body(0, m, False, True)
            base, s_base, p_base = m[0], s[0], pw_n[0]
            with dve.Fori(1, B - 1) as b:
                m = [(b - 1) * MISC_PER_BODY + base]
                s[0] = (b - 1) * STEPS + s_base
                pw_n[0] = (b - 1) * 6 + p_base
                n0 = count[0]
                body(b, m, True, True)
                assert count[0] - n0 == STEPS, count[0] - n0
            m = [base + (B - 2) * MISC_PER_BODY]
            s[0] = s_base + (B - 2) * STEPS
            pw_n[0] = p_base + (B - 2) * 6
            body(B - 1, m, True, False)
            b = B
            finish_norm(2, m)
            stats_of(3, b - 1)
            finish_norm(3, m)
            stats_of(4, b - 1)
            finish_norm(4, m)
            stats_of(5, b - 1)
            finish_norm(5, m)
            tokens(m, b - 1)


def attention_stage(nc, io, ctx, tok, ident, mhalf):
    def sb(name, shape, dt=F32):
        return ctx.enter_context(nc.sbuf_tensor(name, shape, dt))

    def sem(name):
        return ctx.enter_context(nc.semaphore(name))

    xn = sb("xn", [P, 2, E])
    xT = sb("xT", [P, 2, 2 * P])
    rT = sb("rT", [RANK, 3, 2 * P])
    rot = sb("rot", [96, 2, 2 * P])
    qk = sb("qk", [96, 2, 2, 2 * P])
    va = sb("va", [P, 2, HEADS, HD + 1])
    nmax = sb("nmax", [P, 2, HEADS])
    probs = sb("probs", [P, HEADS, 2 * P])
    pT = sb("pT", [P, 3, HEADS, P])
    rec = sb("rec", [P, 2, HEADS])
    on = sb("on", [P, 2, E])
    oT = sb("oT", [P, 2, 2 * P])
    a_w = sb("a_w", [P, 2, 3, RANK])
    b_w = sb("b_w", [RANK, 2, 2, E])
    vb_w = sb("vb_w", [RANK, E])
    o_w = sb("o_w", [P, 2, E])
    rope = sb("rope", [96, 2, 2, 2 * P])
    maskf = sb("maskf", [P, P])
    mask = sb("mask", [P, P], BF16)
    identb = sb("identb", [P, P], BF16)
    bn = sb("a_bn", [P, 2, 6])
    mv = sb("a_mv", [P, B, 2, 2])
    veps = sb("a_veps", [P, 32])
    rstd = sb("a_rstd", [P, 32])

    front = [ctx.enter_context(nc.psum_tensor(f"front{i}", [P, 512], F32)) for i in range(2)]
    sc = ctx.enter_context(nc.psum_tensor("sc", [P, 3, 2, 2 * P], F32))
    pt = [ctx.enter_context(nc.psum_tensor(f"pt{i}", [P, 4, P], F32)) for i in range(2)]
    outp = ctx.enter_context(nc.psum_tensor("outp", [P, 512], F32))

    loads = sem("a_loads")
    ones_set = sem("a_ones")
    mask_set = sem("mask_set")
    step = sem("a_step")
    var_in = sem("a_var_in")
    rstd_out = sem("a_rstd_out")
    xn_set = sem("xn_set")
    xT_mm = sem("xT_mm")
    xT_set = sem("xT_set")
    r_mm = sem("r_mm")
    r_set = sem("r_set")
    qk_mm = sem("qk_mm")
    qk_set = sem("qk_set")
    v_mm = sem("v_mm")
    v_set = sem("v_set")
    s_mm = sem("s_mm")
    max_set = sem("max_set")
    exp_set = sem("exp_set")
    pt_mm = sem("pt_mm")
    pt_set = sem("pt_set")
    o_mm = sem("o_mm")
    on_set = sem("on_set")
    oT_mm = sem("oT_mm")
    oT_set = sem("oT_set")
    out_mm = sem("out_mm")
    out_set = sem("out_set")

    PT = [(0, [(h, 0) for h in range(4)]), (0, [(4, 0), (5, 0)]),
          (1, [(h, 0) for h in range(4)]), (1, [(4, 0), (5, 0), (0, 1), (1, 1)]), (1, [(h, 1) for h in range(2, 6)])]

    def first(b):
        return isinstance(b, int) and b == 0

    with nc.Block() as block:
        @block.sync
        def _(sp):
            for dst, name in ((a_w[:], "a_w"), (b_w[:], "b_w"), (vb_w[:], "vb_w"), (o_w[:], "o_w"),
                              (rope[:], "rope"), (maskf[:], "mask")):
                sp.dma_start(dst, io[name]).then_inc(loads, 16)

        @block.tensor
        def _(pe):
            pe.wait_ge(loads, 16 * 6)

            def tokens_T(b):
                pe.wait_ge(xn_set, b + 1)
                if not first(b):
                    pe.wait_ge(v_set, b)
                for t in range(2):
                    pe.transpose(front[0][:, t * P:(t + 1) * P], xn[:, t, 0:P], ident[:])
                    mm = pe.transpose(front[0][0:64, (2 + t) * P:(3 + t) * P], xn[:, t, P:E], ident[:])
                mm.then_inc(xT_mm, 1)

            def factor(b):
                pe.wait_ge(xT_set, b + 1)
                if not first(b):
                    pe.wait_ge(qk_set, 2 * b)
                for i in range(3):
                    out = front[1][0:RANK, i * 2 * P:(i + 1) * 2 * P] if i < 2 else front[0][0:RANK, 0:2 * P]
                    pe.matmul(out, a_w[:, 0, i, :], xT[:, 0, :], start=True, stop=False)
                    mm = pe.matmul(out, a_w[0:64, 1, i, :], xT[0:64, 1, :], start=False, stop=True)
                    if i:
                        mm.then_inc(r_mm, 1)

            def qk_tile(t, b):
                pe.wait_ge(r_set, 2 * b + 2)
                if t:
                    pe.wait_ge(qk_set, 2 * b + 1)
                for r in range(2):
                    for i in range(2):
                        mm = pe.matmul(front[r][0:96, i * 2 * P:(i + 1) * 2 * P], b_w[:, i, r, 96 * t:96 * t + 96],
                                       rT[:, i, :], start=True, stop=True)
                mm.then_inc(qk_mm, 1)

            def values(b):
                pe.wait_ge(qk_set, 2 * b + 2)
                for t in range(2):
                    mm = pe.matmul(front[0][:, t * E:(t + 1) * E], rT[:, 2, t * P:(t + 1) * P], vb_w[:],
                                   start=True, stop=True)
                mm.then_inc(v_mm, 1)

            def scores(qt, b):
                pe.wait_ge(qk_set, 2 * b + 2)
                if qt or not first(b):
                    pe.wait_ge(exp_set, 2 * b + qt)
                n = (qt + 1) * P
                for g in range(3):
                    for t in range(2):
                        pe.matmul(sc[:, g, t, n - P:n], identb[:], mask[:], start=(t == 0), stop=False,
                                  skip_group_check=True)
                for t in range(2):
                    for g in range(3):
                        head = slice(32 * g, 32 * g + 32)
                        mm = pe.matmul(sc[:, g, t, 0:n], qk[head, t, 0, qt * P:(qt + 1) * P],
                                       qk[head, t, 1, 0:n], start=False, stop=(t == 1), skip_group_check=True)
                mm.then_inc(s_mm, 1)

            def probs_T(i, b):
                qt, blocks = PT[i]
                pe.wait_ge(exp_set, 2 * b + qt + 1)
                if not (first(b) and i < 2):
                    pe.wait_ge(pt_set, 5 * b + max(i - 1, 0))
                for j, (h, kt) in enumerate(blocks):
                    mm = pe.transpose(pt[i % 2][:, j, :], probs[:, h, kt * P:(kt + 1) * P], ident[:])
                mm.then_inc(pt_mm, 1)

            def weighted(qt, b):
                pe.wait_ge(pt_set, 5 * b + (2 if qt == 0 else 5))
                pe.wait_ge(v_set, b + 1)
                if qt == 0 and not first(b):
                    pe.wait_ge(out_set, b)
                for h in range(HEADS):
                    o = outp[:, (qt * HEADS + h) * (HD + 1):(qt * HEADS + h + 1) * (HD + 1)]
                    for kt in range(qt + 1):
                        mm = pe.matmul(o, pT[:, qt + kt, h, :], va[:, kt, h, :], start=(kt == 0), stop=(kt == qt))
                if qt == 1:
                    mm.then_inc(o_mm, 1)

            def out_T(b):
                pe.wait_ge(on_set, b + 1)
                for t in range(2):
                    pe.transpose(outp[:, t * P:(t + 1) * P], on[:, t, 0:P], ident[:])
                    mm = pe.transpose(outp[0:64, (2 + t) * P:(3 + t) * P], on[:, t, P:E], ident[:])
                mm.then_inc(oT_mm, 1)

            def out_proj(b):
                pe.wait_ge(oT_set, b + 1)
                for t in range(2):
                    o = outp[:, t * E:(t + 1) * E]
                    pe.matmul(o, oT[:, 0, t * P:(t + 1) * P], o_w[:, 0, :], start=True, stop=False)
                    mm = pe.matmul(o, oT[0:64, 1, t * P:(t + 1) * P], o_w[0:64, 1, :], start=False, stop=True)
                mm.then_inc(out_mm, 1)

            def body(b, after):
                scores(0, b)
                if after:
                    tokens_T(b + 1)
                    factor(b + 1)
                probs_T(0, b)
                probs_T(1, b)
                scores(1, b)
                if after:
                    qk_tile(0, b + 1)
                weighted(0, b)
                if after:
                    qk_tile(1, b + 1)
                for i in range(2, 5):
                    probs_T(i, b)
                weighted(1, b)
                if after:
                    values(b + 1)
                out_T(b)
                out_proj(b)

            pe.wait_ge(mask_set, 2)
            tokens_T(0)
            factor(0)
            qk_tile(0, 0)
            qk_tile(1, 0)
            values(0)
            body(0, True)
            with pe.Fori(1, B - 1) as b:
                body(b, True)
            body(B - 1, False)

        @block.scalar
        def _(act):
            def move_xT(b):
                act.wait_ge(xT_mm, b + 1)
                act.copy(xT[:, 0, :], front[0][:, 0:2 * P])
                act.copy(xT[0:64, 1, :], front[0][0:64, 2 * P:4 * P]).then_inc(xT_set, 1)

            def move_r(b):
                act.wait_ge(r_mm, 2 * b + 1)
                act.copy(rT[:, 0:2, :], front[1][0:RANK, :].rearrange("p (i n) -> p i n", i=2)).then_inc(r_set, 1)
                act.wait_ge(r_mm, 2 * b + 2)
                act.copy(rT[:, 2, :], front[0][0:RANK, 0:2 * P]).then_inc(r_set, 1)

            def move_v(b):
                act.wait_ge(v_mm, b + 1)
                for t in range(2):
                    ins = act.copy(va[:, t, :, 0:HD], front[0][:, t * E:(t + 1) * E].rearrange("p (h d) -> p h d", d=HD))
                ins.then_inc(v_set, 1)

            def exps(qt, b):
                act.wait_ge(max_set, 2 * b + qt + 1)
                if qt == 0 and not first(b):
                    act.wait_ge(pt_mm, 5 * b)
                if qt == 1:
                    act.wait_ge(pt_mm, 5 * b + 2)
                n = (qt + 1) * P
                for h in range(HEADS):
                    ins = act.activation(probs[:, h, 0:n], sc[:, h % 3, h // 3, 0:n], ACT.Exp,
                                         bias=nmax[:, qt, h:h + 1], scale=1.0)
                ins.then_inc(exp_set, 1)

            def move_pT(i, b):
                qt, blocks = PT[i]
                act.wait_ge(pt_mm, 5 * b + i + 1)
                runs = {}
                for j, (h, kt) in enumerate(blocks):
                    runs.setdefault(kt, []).append((j, h))
                for kt, r in runs.items():
                    (j0, h0), n = r[0], len(r)
                    ins = act.copy(pT[:, qt + kt, h0:h0 + n, :], pt[i % 2][:, j0:j0 + n, :])
                ins.then_inc(pt_set, 1)

            def move_oT(b):
                act.wait_ge(oT_mm, b + 1)
                act.copy(oT[:, 0, :], outp[:, 0:2 * P])
                act.copy(oT[0:64, 1, :], outp[0:64, 2 * P:4 * P]).then_inc(oT_set, 1)

            def body(b, after):
                if after:
                    move_xT(b + 1)
                exps(0, b)
                if after:
                    move_r(b + 1)
                move_pT(0, b)
                move_pT(1, b)
                exps(1, b)
                for i in range(2, 5):
                    move_pT(i, b)
                if after:
                    move_v(b + 1)
                move_oT(b)

            act.wait_ge(ones_set, 1)
            move_xT(0)
            move_r(0)
            move_v(0)
            body(0, True)
            with act.Fori(1, B - 1) as b:
                body(b, True)
            body(B - 1, False)

        @block.gpsimd
        def _(pool):
            pool.wait_ge(var_in, 1)
            pool.tensor_tensor(rstd[:], veps[:], mhalf[:], ALU.pow).then_inc(rstd_out, 1)

        @block.vector
        def _(dve):
            dve.memset(va[:], 1.0).then_inc(ones_set, 1)
            dve.wait_ge(loads, 16 * 6)
            dve.tensor_copy(mask[:], maskf[:]).then_inc(mask_set, 1)
            dve.tensor_copy(identb[:], ident[:]).then_inc(mask_set, 1)
            token_moments(dve, tok, bn, mv, step)
            dve.tensor_scalar(veps[:], mv[:].rearrange("p b t s -> p (b t) s")[:, :, 1], EPS, None,
                              ALU.add).then_inc(var_in, 1)
            dve.wait_ge(rstd_out, 1)
            steps = [2 * B * 2]

            def then(ins):
                ins.then_inc(step, 1)
                steps[0] = steps[0] + 1
                dve.wait_ge(step, steps[0])

            def normalise(b):
                if not first(b):
                    dve.wait_ge(xT_mm, b)
                for t in range(2):
                    ins = dve.tensor_scalar(xn[:, t, :], tok[:, b, t, :], mv[:, b, t, 0:1],
                                            rstd[:, bass.ds(2 * b + t, 1)], ALU.subtract, ALU.mult)
                ins.then_inc(xn_set, 1)

            def rotate(t, b):
                dve.wait_ge(qk_mm, 2 * b + t + 1)
                q = qk[:, t, :, :]
                dve.tensor_tensor(q, front[0][0:96, :].rearrange("p (i n) -> p i n", i=2), rope[:, 0], ALU.mult)
                then(dve.tensor_tensor(rot[:], front[1][0:96, :].rearrange("p (i n) -> p i n", i=2), rope[:, 1],
                                       ALU.mult))
                dve.tensor_tensor(q, q, rot[:], ALU.add).then_inc(qk_set, 1)

            def maxima(qt, b):
                dve.wait_ge(s_mm, 2 * b + qt + 1)
                n = (qt + 1) * P
                dve.tensor_reduce(nmax[:, qt, :].rearrange("p (t g) -> p g t", g=3), sc[:, :, :, 0:n],
                                  AX.X, ALU.max, negate=True).then_inc(max_set, 1)

            def divide(b):
                dve.wait_ge(o_mm, b + 1)
                o = outp[:, 0:2 * HEADS * (HD + 1)].rearrange("p (t h d) -> p (t h) d", t=2, d=HD + 1)
                r = rec[:].rearrange("p t h -> p (t h)")
                then(dve.reciprocal(r, o[:, :, HD]))
                dve.tensor_tensor(on[:].rearrange("p t (h d) -> p (t h) d", d=HD), o[:, :, 0:HD],
                                  r.unsqueeze(2).broadcast_to([P, 2 * HEADS, HD]), ALU.mult).then_inc(on_set, 1)

            def residual(b):
                dve.wait_ge(out_mm, b + 1)
                x = tok[:, b, :, :]
                dve.tensor_tensor(x, outp[:, 0:2 * E].rearrange("p (t e) -> p t e", t=2), x,
                                  ALU.add).then_inc(out_set, 1)

            def body(b, after):
                if after:
                    normalise(b + 1)
                maxima(0, b)
                maxima(1, b)
                if after:
                    rotate(0, b + 1)
                    rotate(1, b + 1)
                divide(b)
                residual(b)

            normalise(0)
            rotate(0, 0)
            rotate(1, 0)
            body(0, True)
            base = steps[0]
            with dve.Fori(1, B - 1) as b:
                steps[0] = base + (b - 1) * 3
                body(b, True)
            steps[0] = base + (B - 2) * 3
            body(B - 1, False)


def token_moments(dve, tok, bn, mv, step):
    for b in range(B):
        for t in range(2):
            dve.bn_stats(bn[:, t, :], tok[:, b, t, :]).then_inc(step, 1)
            dve.wait_ge(step, b * 4 + (2 * t + 1))
            dve.bn_aggr(mv[:, b, t, :], bn[:, t, :]).then_inc(step, 1)
            dve.wait_ge(step, b * 4 + (2 * t + 2))


def expert_stage(nc, io, ctx, tok, ident, mhalf):
    def sb(name, shape, dt=F32):
        return ctx.enter_context(nc.sbuf_tensor(name, shape, dt))

    def sem(name):
        return ctx.enter_context(nc.semaphore(name))

    NT = 2 * B
    xn = sb("e_xn", [P, 2, E])
    xTs = sb("e_xTs", [P, 2, 2 * P])
    xT = sb("e_xT", [P, 2, NT * P])
    w1a = sb("w1a", [P, NE, HID])
    w1b = sb("w1b", [64, NE, HID])
    w2 = sb("w2x", [P, NE, HT, E])
    rw = sb("rw", [P, 2, NE])
    hT = sb("hT", [P, 2, HT, GT * P])
    bn = sb("e_bn", [P, 2, 6])
    mv = sb("e_mv", [P, B, 2, 2])
    veps = sb("e_veps", [P, 32])
    rstd = sb("e_rstd", [P, 32])
    lg = sb("lg", [P, NT, NE])
    pr = sb("pr", [P, NT, NE])
    key = sb("key", [P, NT, NE])
    sel1 = sb("sel1", [P, NT, NE])
    sel2 = sb("sel2", [P, NT, NE])
    rest = sb("rest", [P, NT, NE])
    wgt = sb("wgt", [P, NT, NE])
    col = sb("col", [P, 4, NT])
    imp2 = sb("imp2", [P, 2, NE])
    run = sb("run", [P, 2, NE])
    iota = sb("iota", [P, NT, NE])
    count_w = sb("count_w", [P, 2, P])

    hp = [ctx.enter_context(nc.psum_tensor(f"hp{i}", [P, 512], F32)) for i in range(4)]
    op = [ctx.enter_context(nc.psum_tensor(f"op{i}", [P, 2, E], F32)) for i in range(4)]

    loads = sem("e_loads")
    step = sem("e_step")
    var_in = sem("e_var_in")
    rstd_out = sem("e_rstd_out")
    xn_set = sem("e_xn_set")
    xT_mm = sem("e_xT_mm")
    xT_set = sem("e_xT_set")
    lg_mm = sem("lg_mm")
    lg_set = sem("lg_set")
    xT_kept = sem("xT_kept")
    ex_in = sem("ex_in")
    ex_out = sem("ex_out")
    imp_in = sem("imp_in")
    imp_mm = sem("imp_mm")
    imp_read = sem("imp_read")
    h_mm = sem("h_mm")
    h_set = sem("h_set")
    y_mm = sem("y_mm")
    y_set = sem("y_set")
    done = sem("done")

    def first(b):
        return isinstance(b, int) and b == 0

    with nc.Block() as block:
        @block.sync
        def _(sp):
            for dst, name in ((rw[:], "rw"), (iota[:], "iota"), (count_w[:], "count_w"), (w1a[:], "w1a"),
                              (w1b[:], "w1b"), (w2[:], "w2x")):
                sp.dma_start(dst, io[name]).then_inc(loads, 16)
            sp.wait_ge(y_set, NGRP * NE * 2)
            for t in range(2):
                sp.dma_start(io["out"][:, t * P:t * P + TQ[t], :].rearrange("b t e -> t b e"),
                             tok[0:TQ[t], :, t, :]).then_inc(done, 16)
            sp.wait_ge(done, 32)

        @block.tensor
        def _(pe):
            pe.wait_ge(loads, 16 * 6)

            def route(b):
                pe.wait_ge(xn_set, b + 1)
                if not first(b):
                    pe.wait_ge(xT_set, b)
                for t in range(2):
                    pe.transpose(hp[0][:, t * P:(t + 1) * P], xn[:, t, 0:P], ident[:])
                    mm = pe.transpose(hp[0][0:64, (2 + t) * P:(3 + t) * P], xn[:, t, P:E], ident[:])
                mm.then_inc(xT_mm, 1)
                pe.wait_ge(xT_set, b + 1)
                if not first(b):
                    pe.wait_ge(lg_set, b)
                for t in range(2):
                    pe.matmul(hp[1][:, t * NE:(t + 1) * NE], xTs[:, 0, t * P:(t + 1) * P], rw[:, 0, :],
                              start=True, stop=False)
                    mm = pe.matmul(hp[1][:, t * NE:(t + 1) * NE], xTs[0:64, 1, t * P:(t + 1) * P], rw[0:64, 1, :],
                                   start=False, stop=True)
                mm.then_inc(lg_mm, 1)

            route(0)
            with pe.Fori(1, B) as b:
                route(b)
            pe.wait_ge(imp_in, 1)
            for t in range(2):
                mm = pe.matmul(op[3][:, 0, 0:NE], count_w[:, t, :], imp2[:, t, :], start=(t == 0), stop=(t == 1))
            mm.then_inc(imp_mm, 1)

            def hidden(e, g):
                for i in range(HT):
                    if not (first(g) and e == 0):
                        pe.wait_ge(h_set, g * (NE * HT) + (e * HT + i - HT + 1))
                    pe.matmul(hp[i][:], w1a[:, e, i * P:(i + 1) * P], xT[:, 0, bass.ds(g * (GT * P), GT * P)],
                              start=True, stop=False)
                    pe.matmul(hp[i][:], w1b[:, e, i * P:(i + 1) * P], xT[0:64, 1, bass.ds(g * (GT * P), GT * P)],
                              start=False, stop=True).then_inc(h_mm, 1)

            def output(e, g):
                pe.wait_ge(h_set, g * (NE * HT) + (e + 1) * HT)
                if first(g) and e == 1:
                    pe.wait_ge(imp_read, 1)
                for j in range(2):
                    bank = op[(e % 2) * 2 + j]
                    if not (first(g) and e < 2):
                        pe.wait_ge(y_set, g * (NE * 2) + (2 * e + j - 4 + 1))
                    for k in range(2):
                        for i in range(HT):
                            mm = pe.matmul(bank[:, k, :], hT[:, e % 2, i, (2 * j + k) * P:(2 * j + k + 1) * P],
                                           w2[:, e, i, :], start=(i == 0), stop=(i == HT - 1))
                    mm.then_inc(y_mm, 1)

            def group(g):
                hidden(0, g)
                for e in range(NE):
                    if e + 1 < NE:
                        hidden(e + 1, g)
                    output(e, g)

            pe.wait_ge(xT_kept, B)
            group(0)
            with pe.Fori(1, NGRP) as g:
                group(g)

        @block.scalar
        def _(act):
            def move_xT(b):
                act.wait_ge(xT_mm, b + 1)
                if not first(b):
                    act.wait_ge(xT_kept, b)
                act.copy(xTs[:, 0, :], hp[0][:, 0:2 * P])
                act.copy(xTs[0:64, 1, :], hp[0][0:64, 2 * P:4 * P]).then_inc(xT_set, 1)

            move_xT(0)
            with act.Fori(1, B) as b:
                move_xT(b)
            act.wait_ge(ex_in, 1)
            act.activation(pr[:], lg[:], ACT.Exp).then_inc(ex_out, 1)

            def silu(g):
                for e in range(NE):
                    for i in range(HT):
                        act.wait_ge(h_mm, g * (NE * HT) + (e * HT + i + 1))
                        if i == 0 and not (first(g) and e < 2):
                            act.wait_ge(y_mm, g * (NE * 2) + (2 * (e - 2) + 2))
                        act.activation(hT[:, e % 2, i, :], hp[i][:], ACT.Silu).then_inc(h_set, 1)

            silu(0)
            with act.Fori(1, NGRP) as g:
                silu(g)

        @block.gpsimd
        def _(pool):
            pool.wait_ge(var_in, 1)
            pool.tensor_tensor(rstd[:], veps[:], mhalf[:], ALU.pow).then_inc(rstd_out, 1)

        @block.vector
        def _(dve):
            dve.wait_ge(loads, 16 * 6)
            token_moments(dve, tok, bn, mv, step)
            dve.tensor_scalar(veps[:], mv[:].rearrange("p b t s -> p (b t) s")[:, :, 1], EPS, None,
                              ALU.add).then_inc(var_in, 1)
            dve.wait_ge(rstd_out, 1)
            steps = [2 * B * 2]

            def then(ins):
                ins.then_inc(step, 1)
                steps[0] = steps[0] + 1
                dve.wait_ge(step, steps[0])

            def tile_pair(b):
                if not first(b):
                    dve.wait_ge(xT_mm, b)
                for t in range(2):
                    ins = dve.tensor_scalar(xn[:, t, :], tok[:, b, t, :], mv[:, b, t, 0:1],
                                            rstd[:, bass.ds(2 * b + t, 1)], ALU.subtract, ALU.mult)
                ins.then_inc(xn_set, 1)
                dve.wait_ge(xT_set, b + 1)
                dve.tensor_copy(xT[:, 0, bass.ds(b * (2 * P), 2 * P)], xTs[:, 0, :])
                dve.tensor_copy(xT[0:64, 1, bass.ds(b * (2 * P), 2 * P)], xTs[0:64, 1, :]).then_inc(xT_kept, 1)
                dve.wait_ge(lg_mm, b + 1)
                dve.tensor_copy(lg[:, bass.ds(2 * b, 2), :],
                                hp[1][:, 0:2 * NE].rearrange("p (t e) -> p t e", t=2)).then_inc(lg_set, 1)

            tile_pair(0)
            with dve.Fori(1, B) as b:
                tile_pair(b)
            dve.wait_ge(lg_set, B)

            def by_tile(c):
                return col[:, c, :].unsqueeze(2).broadcast_to([P, NT, NE])

            then(dve.tensor_reduce(col[:, 0, :], lg[:], AX.X, ALU.max))
            dve.tensor_tensor(lg[:], lg[:], by_tile(0), ALU.subtract).then_inc(ex_in, 1)
            dve.wait_ge(ex_out, 1)
            then(dve.tensor_reduce(col[:, 1, :], pr[:], AX.X, ALU.add))
            then(dve.reciprocal(col[:, 1, :], col[:, 1, :]))
            then(dve.tensor_tensor(pr[:], pr[:], by_tile(1), ALU.mult))
            dve.tensor_reduce(imp2[:], pr[:].rearrange("p (b t) e -> p t e b", t=2), AX.X, ALU.add).then_inc(imp_in, 1)

            def pick(src, out):
                then(dve.tensor_reduce(col[:, 2, :], src[:], AX.X, ALU.max))
                then(dve.tensor_tensor(key[:], src[:], by_tile(2), ALU.is_equal))
                then(dve.scalar_tensor_tensor(out=key[:].rearrange("p t e -> p (t e)"),
                                              in0=key[:].rearrange("p t e -> p (t e)"), scalar=-float(NE),
                                              in1=iota[:].rearrange("p t e -> p (t e)"), op0=ALU.mult, op1=ALU.add))
                then(dve.tensor_reduce(col[:, 3, :], key[:], AX.X, ALU.min))
                then(dve.tensor_tensor(out[:], key[:], by_tile(3), ALU.is_equal))

            pick(pr, sel1)
            then(dve.scalar_tensor_tensor(out=rest[:].rearrange("p t e -> p (t e)"),
                                          in0=sel1[:].rearrange("p t e -> p (t e)"), scalar=-2.0,
                                          in1=pr[:].rearrange("p t e -> p (t e)"), op0=ALU.mult, op1=ALU.add))
            pick(rest, sel2)
            then(dve.tensor_tensor(sel1[:], sel1[:], sel2[:], ALU.add))
            then(dve.tensor_tensor(pr[:], pr[:], sel1[:], ALU.mult))
            dve.wait_ge(imp_mm, 1)
            dve.tensor_scalar(run[:, 0, :], op[3][:, 0, 0:NE], -1.0, 1.0 - DECAY, ALU.add,
                              ALU.mult).then_inc(imp_read, 1)
            dve.wait_ge(imp_read, 1)
            then(dve.tensor_scalar(run[:, 0, :], run[:, 0, :], 1.0, LOAD_EPS, ALU.add, ALU.add))
            then(dve.reciprocal(run[:, 1, :], run[:, 0, :]))
            then(dve.tensor_tensor(pr[:], pr[:], run[:, 1, :].unsqueeze(1).broadcast_to([P, NT, NE]), ALU.mult))
            then(dve.tensor_reduce(col[:, 1, :], pr[:], AX.X, ALU.add))
            then(dve.reciprocal(col[:, 1, :], col[:, 1, :]))
            then(dve.tensor_tensor(wgt[:], pr[:], by_tile(1), ALU.mult))

            def combine(g):
                for e in range(NE):
                    for j in range(2):
                        dve.wait_ge(y_mm, g * (NE * 2) + (2 * e + j + 1))
                        if e:
                            dve.wait_ge(y_set, g * (NE * 2) + (2 * (e - 1) + j + 1))
                        for k in range(2):
                            x = tok[:, bass.ds(2 * g + j, 1), k, :].rearrange("p o e -> p (o e)")
                            ins = dve.scalar_tensor_tensor(
                                out=x, in0=op[(e % 2) * 2 + j][:, k, :],
                                scalar=wgt[:, bass.ds(4 * g + 2 * j + k, 1), e], in1=x, op0=ALU.mult, op1=ALU.add)
                        ins.then_inc(y_set, 1)

            combine(0)
            with dve.Fori(1, NGRP) as g:
                combine(g)




def laid_out(inputs):
    f = np.float32
    got = {k: np.asarray(v) for k, v in inputs.items()}
    x = got["x"]
    a = {}
    xp = np.zeros((B, 40 * UT * P + XR), f)
    xp[:, :T_IN] = x
    idx = 40 * np.arange(UT * P)[:, None] + np.arange(WIN)[None, :]
    xw = np.ones((B, UT * P, XR), f)
    xw[:, :, :WIN] = xp[:, idx]
    a["xw"] = np.ascontiguousarray(xw.reshape(B, UT, P, XR).transpose(0, 2, 1, 3))
    last = np.zeros((B, 1, K0 + 1), f)
    last[:, 0, :5] = x[:, 5 * T0:]
    last[:, 0, K0] = 1.0
    a["xlast"] = last
    w0 = got["L0_tok_cw0"].reshape(C, K0).T
    w0win = np.zeros((P, 8, C), f)
    for base in (0, LO):
        for v in range(8):
            w0win[base + 5 * v:base + 5 * v + K0, v, :] = w0
        w0win[base + WIN, :, :] = got["L0_tok_cb0"]
    a["w0win"] = w0win
    a["w11"] = np.concatenate([w0, got["L0_tok_cb0"][None]], 0)
    for l in range(1, 6):
        a[f"w{l}T"] = np.ascontiguousarray(got[f"L0_tok_cw{l}"].transpose(1, 2, 0))
    a["chan"] = np.stack([np.stack([got[f"L0_tok_{n}{l}"] for n in ("cb", "gw", "gb")], -1)
                          for l in range(6)], 1)
    a["pwT"] = np.ascontiguousarray(got["L0_tok_pw"].T)
    a["pb"] = got["L0_tok_pb"][None]
    a["ident"] = np.eye(P, dtype=f)
    a["gavg"] = np.kron(np.eye(C // GROUP), np.full((GROUP, GROUP), 1.0 / GROUP)).astype(f)
    sel = np.zeros((XR, 8, K0 + 1), f)
    for v in range(8):
        sel[5 * v + np.arange(K0), v, np.arange(K0)] = 1.0
        sel[WIN, v, K0] = 1.0
    a["sel"] = sel
    a_w = np.zeros((P, 2, 3, RANK), f)
    for i, n in enumerate("qkv"):
        m = got[f"L0_attn_{n}A"]
        a_w[:, 0, i], a_w[:64, 1, i] = m[:P], m[P:]
    a["a_w"] = a_w
    swap = (np.arange(E) // HD) * HD + (np.arange(E) % HD + HD // 2) % HD
    a["b_w"] = np.stack([np.stack([got[f"L0_attn_{n}B"], got[f"L0_attn_{n}B"][:, swap]], 1) for n in "qk"], 1)
    a["vb_w"] = got["L0_attn_vB"]
    o_w = np.zeros((P, 2, E), f)
    o_w[:, 0], o_w[:64, 1] = got["L0_attn_o_w"][:P], got["L0_attn_o_w"][P:]
    a["o_w"] = o_w
    inv = (1.0 / 10000.0 ** (np.arange(0, HD, 2, dtype=f) / f(HD))).astype(f)
    angle = np.outer(np.concatenate([inv, inv]), np.arange(2 * P, dtype=f)).astype(f)
    sign = np.where(np.arange(HD) < HD // 2, -1.0, 1.0)[:, None]
    rope = np.stack([np.cos(angle.astype(np.float64)), sign * np.sin(angle.astype(np.float64))], 1)
    rope = np.stack([rope / np.sqrt(HD), rope], 2)
    a["rope"] = np.tile(rope, (3, 1, 1, 1)).astype(f)
    rw = np.zeros((P, 2, NE), f)
    rw[:, 0], rw[:64, 1] = got["L0_ffn_router_w"].T[:P], got["L0_ffn_router_w"].T[P:]
    a["rw"] = rw
    w1 = got["L0_ffn_w1"].transpose(2, 0, 1)
    a["w1a"], a["w1b"] = np.ascontiguousarray(w1[:P]), np.ascontiguousarray(w1[P:])
    a["w2x"] = np.ascontiguousarray(got["L0_ffn_w2"].reshape(NE, E, HT, P).transpose(3, 0, 2, 1))
    a["iota"] = np.tile(np.arange(NE, dtype=f), (P, 2 * B, 1))
    count_w = np.ones((P, 2, P), f)
    count_w[TQ[1]:, 1] = 0.0
    a["count_w"] = count_w
    a["mask"] = np.where(np.arange(P)[:, None] >= np.arange(P)[None], 0.0, -1e30).astype(f)
    return a


def kernel(**inputs):
    import concourse.bacc as bacc
    from concourse.bass_utils import run_bass_kernel_spmd

    nc = bacc.Bacc("TRN2", target_bir_lowering=False, num_devices=1)
    arrays, io = {}, {}
    for name, a in laid_out(inputs).items():
        arrays[f"in_{name}"] = a
        io[name] = nc.dram_tensor(f"in_{name}", a.shape, mybir.dt.from_np(a.dtype), kind="ExternalInput").ap()
    io["out"] = nc.dram_tensor("out_0", (B, T5, E), F32, kind="ExternalOutput").ap()
    audio_tower(nc, io)
    r = run_bass_kernel_spmd(nc, [arrays], core_ids=[0])
    return r.results[0]["out_0"]
```

```python
from contextlib import ExitStack

import numpy as np

import concourse.bass as bass
from concourse import mybir

F32 = mybir.dt.float32
F16 = mybir.dt.float16
BF16 = mybir.dt.bfloat16
U32 = mybir.dt.uint32
I32 = mybir.dt.int32
ALU = mybir.AluOpType
ACT = mybir.ActivationFunctionType
AX = mybir.AxisListType

P = 128
B, T_IN = 16, 40000
C = 128
GROUP = 4
E = 192
EPS = 1e-5
T0 = (T_IN - 10) // 5 + 1
T1 = (T0 - 3) // 2 + 1
T2 = (T1 - 3) // 2 + 1
T3 = (T2 - 3) // 2 + 1
T4 = (T3 - 3) // 2 + 1
T5 = (T4 - 2) // 2 + 1
U = 1000
HU = U // 2
WIN = 45
XR = WIN + 1
K0 = 10
LO = 64
S0 = 1024.0
UT = (U + P - 1) // P
TAILROWS = U - (UT - 1) * P
TQ = [P, T5 - P]

HEADS, HD = 6, 32
RANK = E // 4
NE, HID = 8, 512
HT = HID // P
NT = 2 * B
CAP = ((B * T5 + 2 * P - 1) // P) * P
NBLK = (2 * B * T5 + NE * (P - 1)) // P
ASTEPS = 27
DECAY, LOAD_EPS = 0.9, 0.01

MISC_PER_BODY = 14
STEPS = 39


def half_cols(last, h):
    return HU - 1 if last and h == 1 else HU


L1_CHUNKS = [(q, h) for q in (0, 3, 1, 2) for h in range(2)]
L0_CHUNKS = [(v, h) for v in (7, 0, 1, 2, 3, 4, 5, 6) for h in range(2)]
GELU1 = [(0, 0), (1, 0), (2, 0), (0, 1), (1, 1), (2, 1), (3, 0), (3, 1)]
RING = ([(1, c) for c in range(7)] + [(0, c) for c in range(5)] + [(1, 7)] + [(0, c) for c in range(5, 16)])


def ring_bank(use):
    return RING.index(use) % 3


def taps_of(plane_out, planes_in, h, n, taps=3):
    for k in range(taps):
        q = 2 * plane_out + k
        shift = 1 if q >= planes_in else 0
        yield k, q % planes_in, h * HU + shift, n


def audio_tower(nc, io):
    with ExitStack() as whole:
        tok = whole.enter_context(nc.sbuf_tensor("tok", [P, B, 2, E], F32))
        ident = whole.enter_context(nc.sbuf_tensor("ident", [P, P], F32))
        mhalf = whole.enter_context(nc.sbuf_tensor("mhalf", [P, 32], F32))
        moe = expert_state(nc, whole)
        att = attention_state(nc, whole)
        with ExitStack() as ctx:
            conv_stage(nc, io, ctx, tok, ident, mhalf, moe, att)
        with ExitStack() as ctx:
            attention_stage(nc, ctx, tok, ident, mhalf, moe, att)
        with ExitStack() as ctx:
            expert_stage(nc, io, ctx, tok, ident, moe)


def conv_stage(nc, io, ctx, tok, ident, mhalf, moe, att):
    def sb(name, shape, dt=F32):
        return ctx.enter_context(nc.sbuf_tensor(name, shape, dt))

    def sem(name):
        return ctx.enter_context(nc.semaphore(name))

    gavg = sb("gavg", [P, P])
    sel = sb("sel", [XR, 8, K0 + 1])
    ones = sb("ones", [P, 1])
    chan = sb("chan", [P, 6, 3])
    w0f = sb("w0f", [P, 8, C])
    w0s = sb("w0s", [P, 2, 8, C], F16)
    w11 = sb("w11", [K0 + 1, C])
    w = [None] + [sb(f"w{l}", [P, 3 if l < 5 else 2, C]) for l in range(1, 6)]
    pw = sb("pw", [P, E])
    pb = sb("pb", [P, E])
    xu = sb("xu", [P, UT, XR])
    lastp = sb("lastp", [1, 2, K0 + 1])
    xs = sb("xs", [P, U], F16)
    h0 = sb("h0", [P, 8, U])
    h1r = sb("h1r", [P, 4, U])
    h1 = sb("h1", [P, 4, U])
    h2 = sb("h2", [P, 2, U])
    h3 = sb("h3", [P, U])
    h4 = sb("h4", [P, T4])
    h5 = sb("h5", [P, T5])
    gram = sb("gram", [XR, XR])
    gsel = sb("gsel", [XR, 8, K0 + 1])
    g11 = sb("g11", [K0 + 1, K0 + 1])
    q11 = sb("q11", [K0 + 1, C])
    bn = sb("bn", [P, 8, 6])
    bn1 = sb("bn1", [P, 8, 6])
    bn_tok = sb("bn_tok", [P, 2, 6])
    mv_tok = sb("mv_tok", [P, 2, 2])
    st = sb("st", [P, 6, 2])
    gm = sb("gm", [P, 6, 2])
    var = sb("var", [P, 6, 3])
    rstd = sb("rstd", [P, 6])
    dmean = sb("dmean", [P, 6])
    gscale = sb("gscale", [P, 6])
    gbias = sb("gbias", [P, 6])
    scale0 = sb("scale0", [P, 1])

    ring = [ctx.enter_context(nc.psum_tensor(f"ring{i}", [P, 512], F32)) for i in range(3)]
    misc = ctx.enter_context(nc.psum_tensor("misc", [P, 512], F32))
    tail = [ctx.enter_context(nc.psum_tensor(f"tail{i}", [P, 512], F32)) for i in range(4)]

    loads = sem("loads")
    w0_loads = sem("w0_loads")
    x_loads = sem("x_loads")
    ready = sem("ready")
    pe_conv = [sem(f"pe_l{l}") for l in range(6)]
    pe_misc = sem("pe_misc")
    dve_misc = sem("dve_misc")
    l1_out = sem("l1_out")
    stats = [sem(f"stats{l}") for l in range(6)]
    pow_in = sem("pow_in")
    pow_out = sem("pow_out")
    norm = [sem(f"norm{l}") for l in range(6)]
    gelu = [sem(f"gelu{l}") for l in range(6)]
    step = sem("step")
    alone = sem("alone")

    CH = {0: 16, 1: 8, 2: 4, 3: 2, 4: 1, 5: 1}

    with nc.Block() as block:
        @block.sync
        def _(sp):
            sp.dma_start(chan[:], io["chan"]).then_inc(loads, 16)
            sp.dma_start(ident[:], io["ident"]).then_inc(loads, 16)
            sp.dma_start(gavg[:], io["gavg"]).then_inc(loads, 16)
            sp.dma_start(sel[:], io["sel"]).then_inc(loads, 16)
            sp.dma_start(w11[:], io["w11"]).then_inc(loads, 16)
            sp.dma_start(w0f[:], io["w0win"]).then_inc(w0_loads, 16)

            def load_x(b):
                sp.dma_start(xu[:], io["xw"][b]).then_inc(x_loads, 16)
                sp.dma_start(lastp[:, 0, :], io["xlast"][b]).then_inc(x_loads, 16)

            load_x(0)
            for l in range(1, 6):
                sp.dma_start(w[l][:], io[f"w{l}T"]).then_inc(loads, 16)
            sp.dma_start(pw[:], io["pwT"]).then_inc(loads, 16)
            sp.dma_start(pb[:], io["pb"].broadcast_to([P, E])).then_inc(loads, 16)
            for dst, name in ((moe.w1[:, 0], "w1a"), (moe.w1[0:64, 1], "w1b"), (moe.w2[:], "w2x"), (moe.rw[:], "rw")):
                sp.dma_start(dst, io[name]).then_inc(moe.loads, 16)
            for dst, name in ((att.a_w, "a_w"), (att.b_w, "b_w"), (att.vb_w, "vb_w"), (att.o_w, "o_w"),
                              (att.rope, "rope"), (att.maskf, "mask"), (att.countf, "count"),
                              (att.iota, "iota"), (moe.run, "row0")):
                sp.dma_start(dst[:], io[name]).then_inc(att.loads, 16)
            with sp.Fori(1, B) as b:
                sp.wait_ge(pe_conv[0], b * 16 - 15)
                load_x(b)

        LOADS_ALL = 16 * 12
        X_LOADS = 16 * 2

        @block.tensor
        def _(pe):
            def misc_free(m, apart=False):
                if not (isinstance(m[0], int) and m[0] == 0):
                    pe.wait_ge(dve_misc, m[0])
                    if apart:
                        pe.sem_inc(alone, 1)
                m[0] = m[0] + 1

            def transposes(h, b, m):
                misc_free(m, apart=True)
                for j in range(4 * h, 4 * h + 4):
                    rows = P if j < UT - 1 else TAILROWS
                    mm = pe.transpose(misc[0:XR, (j % 4) * P:(j % 4) * P + rows], xu[0:rows, j, :],
                                      ident[0:rows, 0:rows])
                mm.then_inc(pe_misc, 1)

            def gram_matrix(b, m):
                pe.wait_ge(x_loads, (b + 1) * X_LOADS)
                misc_free(m)
                for j in range(UT):
                    rows = P if j < UT - 1 else TAILROWS
                    mm = pe.matmul(misc[0:XR, 0:XR], xu[0:rows, j, :], xu[0:rows, j, :],
                                   start=(j == 0), stop=(j == UT - 1))
                mm.then_inc(pe_misc, 1)

            def gram_select(m):
                misc_free(m, apart=True)
                pe.matmul(misc[0:XR, 0:88], gram[:], sel[:].rearrange("p v k -> p (v k)"),
                          start=True, stop=True).then_inc(pe_misc, 1)

            def gram_taps(m):
                misc_free(m, apart=True)
                pe.matmul(misc[0:K0 + 1, 0:K0 + 1], lastp[:, 1, :], lastp[:, 0, :],
                          start=True, stop=False)
                for v in range(8):
                    mm = pe.matmul(misc[0:K0 + 1, 0:K0 + 1], sel[:, v, :], gsel[:, v, :],
                                   start=False, stop=(v == 7))
                mm.then_inc(pe_misc, 1)

            def gram_weights(m):
                misc_free(m, apart=True)
                pe.matmul(misc[0:K0 + 1, 0:C], g11[:], w11[:], start=True, stop=True).then_inc(pe_misc, 1)

            def moments0(m, b):
                misc_free(m)
                pe.matmul(misc[:, 0:1], w11[:], g11[:, K0:K0 + 1], start=True, stop=True)
                pe.matmul(misc[:, 1:2], q11[:], ones[0:K0 + 1, :], start=True, stop=True).then_inc(pe_misc, 1)

            def group_mean(l, m, b):
                if l > 0:
                    pe.wait_ge(stats[l], b + 1)
                misc_free(m)
                pe.matmul(misc[:, 0:2], gavg[:], st[:, l, :], start=True, stop=True).then_inc(pe_misc, 1)

            def ring_free(use, b, front):
                k = RING.index(use) - 3
                while k >= 0 and RING[k][0] == 0 and not front:
                    k -= 3
                l, c = RING[k]
                t = b + (l == 0) - (k < 0)
                if l:
                    pe.wait_ge(l1_out, 8 * t + c + 1)
                else:
                    pe.wait_ge(gelu[0], 16 * t + c + 1)

            def conv0(c, b, ringed=True):
                v, h = L0_CHUNKS[c]
                n = half_cols(v == 7, h)
                bank = ring[ring_bank((0, c))]
                if ringed:
                    ring_free((0, c), b - 1, True)
                else:
                    before = [i for i in range(c) if ring_bank((0, i)) == ring_bank((0, c))]
                    if before:
                        pe.wait_ge(gelu[0], before[-1] + 1)
                for part in range(2):
                    mm = pe.matmul(bank[:, 0:n], w0s[0:LO + XR, part, v, :], xs[0:LO + XR, h * HU:h * HU + n],
                                   start=(part == 0), stop=(part == 1))
                mm.then_inc(pe_conv[0], 1)

            def conv1(c, b, front):
                q, h = L1_CHUNKS[c]
                n = half_cols(q == 3, h)
                bank = ring[ring_bank((1, c))]
                ring_free((1, c), b, front)
                pe.wait_ge(gelu[0], 16 * b + {0: 7, 3: 15, 1: 15, 2: 15}[q] + h)
                for k, plane, col, n in taps_of(q, 8, h, n):
                    mm = pe.matmul(bank[:, 0:n], w[1][:, k, :], h0[:, plane, col:col + n],
                                   start=(k == 0), stop=(k == 2))
                mm.then_inc(pe_conv[1], 1)

            def conv2(c, b):
                q, h = c // 2, c % 2
                n = half_cols(q == 1, h)
                if not (isinstance(b, int) and b == 0):
                    pe.wait_ge(gelu[(3, 3, 4, 5)[c]], CH[(3, 3, 4, 5)[c]] * b)
                pe.wait_ge(gelu[1], 8 * b + (3, 6, 7, 8)[c])
                for k, plane, col, n in taps_of(q, 4, h, n):
                    mm = pe.matmul(tail[c][:, 0:n], w[2][:, k, :], h1[:, plane, col:col + n],
                                   start=(k == 0), stop=(k == 2))
                mm.then_inc(pe_conv[2], 1)

            def conv3(c, b):
                n = half_cols(True, c)
                pe.wait_ge(gelu[2], 4 * b + 4)
                for k, plane, col, n in taps_of(0, 2, c, n):
                    mm = pe.matmul(tail[c][:, 0:n], w[3][:, k, :], h2[:, plane, col:col + n],
                                   start=(k == 0), stop=(k == 2))
                mm.then_inc(pe_conv[3], 1)

            def conv45(l, b):
                src, n, taps = (h3, T4, 3) if l == 4 else (h4, T5, 2)
                pe.wait_ge(gelu[l - 1], CH[l - 1] * (b + 1))
                for k in range(taps):
                    mm = pe.matmul(tail[l - 2][:, 0:n], w[l][:, k, :], src[:, k:k + 2 * n - 1:2],
                                   start=(k == 0), stop=(k == taps - 1))
                mm.then_inc(pe_conv[l], 1)

            def project(m, b):
                pe.wait_ge(gelu[5], b + 1)
                misc_free(m)
                for t in range(2):
                    mm = pe.matmul(misc[0:TQ[t], t * E:(t + 1) * E], h5[:, t * P:t * P + TQ[t]], pw[:],
                                   start=(t == 0), stop=(t == 1), skip_group_check=True)
                mm.then_inc(pe_misc, 1)

            def body(b, m, now=True, front=True, tail1=True, tail2=True):
                if now:
                    conv1(0, b, front)
                if front:
                    gram_matrix(b + 1, m)
                if tail2:
                    conv45(5, b - 2)
                if now:
                    conv1(1, b, front)
                if front:
                    gram_select(m)
                if tail1:
                    conv2(0, b - 1)
                if now:
                    conv1(2, b, front)
                if front:
                    gram_taps(m)
                if tail1:
                    conv2(1, b - 1)
                if tail2:
                    group_mean(5, m, b - 2)
                if tail1:
                    conv2(2, b - 1)
                if now:
                    conv1(3, b, front)
                if tail2:
                    project(m, b - 2)
                if tail1:
                    conv2(3, b - 1)
                if front:
                    gram_weights(m)
                if front:
                    moments0(m, b + 1)
                if now:
                    conv1(4, b, front)
                if tail1:
                    group_mean(2, m, b - 1)
                if front:
                    group_mean(0, m, b + 1)
                if now:
                    conv1(5, b, front)
                if front:
                    transposes(0, b + 1, m)
                if now:
                    conv1(6, b, front)
                if front:
                    transposes(1, b + 1, m)
                if tail1:
                    conv3(0, b - 1)
                if front:
                    pe.wait_ge(dve_misc, m[0])
                    for c in range(0, 3):
                        conv0(c, b + 1)
                if tail1:
                    conv3(1, b - 1)
                if front:
                    for c in range(3, 5):
                        conv0(c, b + 1)
                if now:
                    conv1(7, b, front)
                if tail1:
                    group_mean(3, m, b - 1)
                if front:
                    for c in range(5, 12):
                        conv0(c, b + 1)
                if now:
                    group_mean(1, m, b)
                if tail1:
                    conv45(4, b - 1)
                if front:
                    for c in range(12, 15):
                        conv0(c, b + 1)
                if tail1:
                    group_mean(4, m, b - 1)
                if front:
                    conv0(15, b + 1)

            pe.wait_ge(loads, LOADS_ALL)
            pe.wait_ge(ready, 2)
            m = [0]
            gram_matrix(0, m)
            gram_select(m)
            gram_taps(m)
            gram_weights(m)
            moments0(m, 0)
            group_mean(0, m, 0)
            transposes(0, 0, m)
            transposes(1, 0, m)
            pe.wait_ge(dve_misc, m[0])
            for c in range(16):
                conv0(c, 0, ringed=False)
            body(0, m, tail1=False, tail2=False)
            body(1, m, tail2=False)
            base = m[0]
            with pe.Fori(2, B - 1) as b:
                m = [(b - 2) * MISC_PER_BODY + base]
                body(b, m)
            m = [base + (B - 3) * MISC_PER_BODY]
            body(B - 1, m, front=False)
            body(B, m, now=False, front=False)
            body(B + 1, m, now=False, front=False, tail1=False)

        @block.scalar
        def _(act):
            def norm_gelu(l, c, b, out, psum, n, scale=None):
                if c == 0:
                    act.wait_ge(norm[l], b + 1)
                if l != 1:
                    act.wait_ge(pe_conv[l], CH[l] * b + c + 1)
                act.activation(out, psum, ACT.Gelu_apprx_tanh, bias=gbias[:, l:l + 1],
                               scale=gscale[:, l:l + 1] if scale is None else scale).then_inc(gelu[l], 1)

            def gelu0(c, b):
                v, h = L0_CHUNKS[c]
                n = half_cols(v == 7, h)
                norm_gelu(0, c, b, h0[:, v, h * HU:h * HU + n], ring[ring_bank((0, c))][:, 0:n], n,
                          scale=scale0[:, 0:1])

            def gelu1(i, b):
                q, h = GELU1[i]
                n = half_cols(q == 3, h)
                if i == 0 and not (isinstance(b, int) and b == 0):
                    act.wait_ge(pe_conv[2], 4 * b)
                norm_gelu(1, i, b, h1[:, q, h * HU:h * HU + n], h1r[:, q, h * HU:h * HU + n], n)

            def gelu2(c, b):
                q, h = c // 2, c % 2
                n = half_cols(q == 1, h)
                norm_gelu(2, c, b, h2[:, q, h * HU:h * HU + n], tail[c][:, 0:n], n)

            def gelu3(c, b):
                n = half_cols(True, c)
                norm_gelu(3, c, b, h3[:, c * HU:c * HU + n], tail[c][:, 0:n], n)

            def body(b, now=True, front=True, tail1=True, tail2=True):
                if tail2:
                    norm_gelu(4, 0, b - 2, h4[:, 0:T4], tail[2][:, 0:T4], T4)
                if tail1:
                    for i in range(8):
                        gelu1(i, b - 1)
                if tail2:
                    norm_gelu(5, 0, b - 2, h5[:, 0:T5], tail[3][:, 0:T5], T5)
                if tail1:
                    for c in range(4):
                        gelu2(c, b - 1)
                if front:
                    for c in range(9):
                        gelu0(c, b + 1)
                if tail1:
                    for c in range(2):
                        gelu3(c, b - 1)
                if front:
                    for c in range(9, 16):
                        gelu0(c, b + 1)

            for c in range(16):
                gelu0(c, 0)
            body(0, tail1=False, tail2=False)
            body(1, tail2=False)
            with act.Fori(2, B - 1) as b:
                body(b)
            body(B - 1, front=False)
            body(B, now=False, front=False)
            body(B + 1, now=False, front=False, tail1=False)

        @block.gpsimd
        def _(pool):
            pool.wait_ge(ready, 1)

            def powers(order, base):
                for i, l in enumerate(order):
                    pool.wait_ge(pow_in, base + (i + 1))
                    pool.tensor_tensor(rstd[:, l:l + 1], var[:, l, 2:3], mhalf[:, 0:1], ALU.pow).then_inc(pow_out, 1)

            start = [0] + [0, 1] + [2, 0, 3, 1, 4]
            powers(start, 0)
            with pool.Fori(2, B - 1) as b:
                powers([5, 2, 0, 3, 1, 4], (b - 2) * 6 + len(start))
            powers([5, 2, 3, 1, 4] + [5, 2, 3, 4] + [5], len(start) + 6 * (B - 3))

        @block.vector
        def _(dve):
            s = [0]
            count = [0]
            pw_n = [0]

            def then(ins):
                ins.then_inc(step, 1)
                s[0] = s[0] + 1
                count[0] += 1
                dve.wait_ge(step, s[0])

            def misc_there(m):
                m[0] = m[0] + 1
                dve.wait_ge(pe_misc, m[0])

            def split_x(h, m):
                n = (4 * P, U - 4 * P)[h]
                hi = xs[0:XR, h * 4 * P:h * 4 * P + n]
                misc_there(m)
                then(dve.tensor_copy(hi, misc[0:XR, 0:n]))
                dve.tensor_tensor(xs[LO:LO + XR, h * 4 * P:h * 4 * P + n], misc[0:XR, 0:n], hi,
                                  ALU.subtract).then_inc(dve_misc, 1)

            def keep(m, out, width, rows, scale=None):
                misc_there(m)
                src = misc[0:rows, 0:width]
                if scale is None:
                    dve.tensor_copy(out, src).then_inc(dve_misc, 1)
                else:
                    dve.tensor_scalar(out, src, scale, None, ALU.mult).then_inc(dve_misc, 1)

            def neg_last():
                then(dve.tensor_scalar(lastp[:, 1, :], lastp[:, 0, :], -1.0, None, ALU.mult))

            def finish_norm(l, m):
                misc_there(m)
                mean, sq = gm[:, l, 0:1], gm[:, l, 1:2]
                dve.tensor_copy(gm[:, l, :], misc[:, 0:2]).then_inc(dve_misc, 1)
                dve.wait_ge(dve_misc, m[0])
                then(dve.scalar_tensor_tensor(out=var[:, l, 0:1], in0=mean, scalar=mean, in1=sq,
                                              op0=ALU.mult, op1=ALU.subtract))
                then(dve.tensor_scalar(var[:, l, 1:2], var[:, l, 0:1], -1.0, 0.0, ALU.mult, ALU.max))
                dve.tensor_scalar(var[:, l, 2:3], var[:, l, 1:2], EPS, None, ALU.add).then_inc(pow_in, 1)
                if l == 0:
                    dve.tensor_scalar(dmean[:, l:l + 1], mean, -1.0, None, ALU.mult)
                else:
                    dve.tensor_tensor(dmean[:, l:l + 1], chan[:, l, 0:1], mean, ALU.subtract)
                pw_n[0] = pw_n[0] + 1
                dve.wait_ge(pow_out, pw_n[0])
                then(dve.tensor_tensor(gscale[:, l:l + 1], rstd[:, l:l + 1], chan[:, l, 1:2], ALU.mult))
                if l == 0:
                    then(dve.tensor_scalar(scale0[:], gscale[:, l:l + 1], 1.0 / S0, None, ALU.mult))
                dve.scalar_tensor_tensor(out=gbias[:, l:l + 1], in0=dmean[:, l:l + 1], scalar=gscale[:, l:l + 1],
                                         in1=chan[:, l, 2:3], op0=ALU.mult, op1=ALU.add).then_inc(norm[l], 1)

            def moments(l, bn, chunks):
                dve.sem_inc(alone, 1)
                then(dve.bn_aggr(st[:, l, :], bn[:, 0:chunks, :].rearrange("p c s -> p (c s)")))
                then(dve.tensor_tensor(st[:, l, 0:1], st[:, l, 0:1], chan[:, l, 0:1], ALU.add))
                dve.scalar_tensor_tensor(out=st[:, l, 1:2], in0=st[:, l, 0:1], scalar=st[:, l, 0:1],
                                         in1=st[:, l, 1:2], op0=ALU.mult, op1=ALU.add).then_inc(stats[l], 1)

            def out1(c, b):
                move1(c, b)
                stats1(c, b)

            def move1(c, b):
                q, h = L1_CHUNKS[c]
                n = half_cols(q == 3, h)
                y = h1r[:, q, h * HU:h * HU + n]
                dve.wait_ge(pe_conv[1], 8 * b + c + 1)
                if not (isinstance(b, int) and b == 0):
                    dve.wait_ge(gelu[1], 8 * b - 7 + GELU1.index((q, h)))
                dve.tensor_copy(y, ring[ring_bank((1, c))][:, 0:n]).then_inc(l1_out, 1)

            def stats1(c, b):
                q, h = L1_CHUNKS[c]
                dve.wait_ge(l1_out, 8 * b + c + 1)
                ins = dve.bn_stats(bn1[:, c, :], h1r[:, q, h * HU:h * HU + half_cols(q == 3, h)])
                if c == 7:
                    then(ins)
                    moments(1, bn1, 8)

            def stats_of(l, b, chunks=None):
                for c in chunks or range(CH[l]):
                    n = {2: half_cols(c >= 2, c % 2), 3: half_cols(True, c), 4: T4, 5: T5}[l]
                    bank = tail[c] if l < 4 else tail[l - 2]
                    dve.wait_ge(pe_conv[l], CH[l] * b + c + 1)
                    ins = dve.bn_stats(bn[:, c, :], bank[:, 0:n])
                if c == CH[l] - 1:
                    then(ins)
                    moments(l, bn, CH[l])

            def tokens(m, b):
                misc_there(m)
                dve.tensor_tensor(tok[:, b, 0, :], misc[:, 0:E], pb[:], ALU.add)
                dve.tensor_tensor(tok[0:TQ[1], b, 1, :], misc[0:TQ[1], E:2 * E], pb[0:TQ[1], :],
                                  ALU.add).then_inc(dve_misc, 1)
                dve.wait_ge(dve_misc, m[0])
                dve.sem_inc(alone, 1)
                for t in range(2):
                    ins = dve.bn_stats(bn_tok[:, t, :], tok[:, b, t, :])
                then(ins)
                dve.sem_inc(alone, 1)
                for t in range(2):
                    ins = dve.bn_aggr(mv_tok[:, t, :], bn_tok[:, t, :])
                then(ins)
                dve.tensor_copy(att.mv[:, 0, b, :], mv_tok[:, :, 0])
                dve.tensor_scalar(att.mv[:, 1, b, :], mv_tok[:, :, 1], EPS, None, ALU.add)

            def prep(i, m, b):
                if i == 0:
                    split_x(0, m)
                elif i == 1:
                    split_x(1, m)
                elif i == 2:
                    keep(m, gram[:], XR, XR)
                    neg_last()
                elif i == 3:
                    keep(m, gsel[:].rearrange("p v k -> p (v k)"), 88, XR)
                elif i == 4:
                    keep(m, g11[:], K0 + 1, K0 + 1, scale=1.0 / T0)
                elif i == 5:
                    misc_there(m)
                    dve.tensor_tensor(q11[:], misc[0:K0 + 1, 0:C], w11[:], ALU.mult).then_inc(dve_misc, 1)
                elif i == 6:
                    misc_there(m)
                    dve.tensor_copy(st[:, 0, :], misc[:, 0:2]).then_inc(dve_misc, 1)

            def body(b, m, now=True, front=True, tail1=True, tail2=True):
                if now:
                    out1(0, b)
                if front:
                    prep(2, m, b)
                if tail2:
                    stats_of(5, b - 2)
                if now:
                    out1(1, b)
                if front:
                    prep(3, m, b)
                if tail1:
                    stats_of(2, b - 1, [0])
                if now:
                    out1(2, b)
                if front:
                    prep(4, m, b)
                if tail1:
                    stats_of(2, b - 1, [1])
                if tail2:
                    finish_norm(5, m)
                if tail1:
                    stats_of(2, b - 1, [2])
                if now:
                    out1(3, b)
                if tail2:
                    tokens(m, b - 2)
                if front:
                    prep(5, m, b)
                if tail1:
                    stats_of(2, b - 1, [3])
                if front:
                    prep(6, m, b)
                if tail1:
                    finish_norm(2, m)
                if front:
                    finish_norm(0, m)
                if now:
                    out1(4, b)
                if front:
                    prep(0, m, b)
                if now:
                    out1(5, b)
                if now:
                    out1(6, b)
                if front:
                    prep(1, m, b)
                if tail1:
                    stats_of(3, b - 1)
                if now:
                    move1(7, b)
                if tail1:
                    finish_norm(3, m)
                if now:
                    stats1(7, b)
                    finish_norm(1, m)
                if tail1:
                    stats_of(4, b - 1)
                    finish_norm(4, m)

            dve.memset(ones[:], 1.0)
            dve.memset(tok[:, :, 1, :], 0.0)
            dve.memset(xs[:], 0.0)
            dve.memset(mhalf[:], -0.5).then_inc(ready, 1)
            dve.wait_ge(w0_loads, 16)
            then(dve.tensor_scalar(w0f[:], w0f[:], S0, None, ALU.mult))
            then(dve.tensor_copy(w0s[:, 0, :, :], w0f[:]))
            dve.tensor_tensor(w0s[:, 1, :, :], w0f[:], w0s[:, 0, :, :], ALU.subtract).then_inc(ready, 1)
            dve.wait_ge(loads, LOADS_ALL)
            m = [0]
            dve.wait_ge(x_loads, X_LOADS)
            for i in range(2, 7):
                prep(i, m, -1)
            finish_norm(0, m)
            prep(0, m, -1)
            prep(1, m, -1)
            body(0, m, tail1=False, tail2=False)
            body(1, m, tail2=False)
            base, s_base, p_base = m[0], s[0], pw_n[0]
            with dve.Fori(2, B - 1) as b:
                m = [(b - 2) * MISC_PER_BODY + base]
                s[0] = (b - 2) * STEPS + s_base
                pw_n[0] = (b - 2) * 6 + p_base
                n0 = count[0]
                body(b, m)
                assert count[0] - n0 == STEPS, count[0] - n0
            m = [base + (B - 3) * MISC_PER_BODY]
            s[0] = s_base + (B - 3) * STEPS
            pw_n[0] = p_base + (B - 3) * 6
            body(B - 1, m, front=False)
            body(B, m, now=False, front=False)
            body(B + 1, m, now=False, front=False, tail1=False)


class Experts:
    pass


def expert_state(nc, ctx):
    def sb(name, shape, dt=F32):
        return ctx.enter_context(nc.sbuf_tensor(name, shape, dt))

    m = Experts()
    m.w1 = sb("moe_w1", [P, 2, NE, HID])
    m.w2 = sb("moe_w2", [P, NE, HT, E])
    m.rw = sb("moe_rw", [P, 2, NE])
    m.pr = sb("pr", [P, NT, NE])
    m.sel = sb("moe_sel", [P, 2, NT, NE])
    m.at = sb("at", [P, NT, 2])
    m.run = sb("run", [P, NE])
    m.xs = nc.dram_tensor("xs_rows", (NE * CAP + P, E), F32)
    m.ys = nc.dram_tensor("ys_rows", (NBLK * P, E), F32)
    m.loads = ctx.enter_context(nc.semaphore("moe_loads"))
    m.rows = ctx.enter_context(nc.semaphore("moe_rows"))
    return m


class Attention:
    pass


def attention_state(nc, ctx):
    def sb(name, shape, dt=F32):
        return ctx.enter_context(nc.sbuf_tensor(name, shape, dt))

    a = Attention()
    a.a_w = sb("a_w", [P, 2, 3, RANK])
    a.b_w = sb("b_w", [RANK, 2, 2, E])
    a.vb_w = sb("vb_w", [RANK, E])
    a.o_w = sb("o_w", [P, 2, E])
    a.rope = sb("rope", [96, 2, 2, 2 * P])
    a.maskf = sb("maskf", [P, P])
    a.iota = sb("iota", [P, 2, NE])
    a.countf = sb("countf", [P, 3, P])
    a.mv = sb("a_mv", [P, 2, B, 2])
    a.loads = ctx.enter_context(nc.semaphore("a_loads"))
    return a


def attention_stage(nc, ctx, tok, ident, mhalf, moe, att):
    def sb(name, shape, dt=F32):
        return ctx.enter_context(nc.sbuf_tensor(name, shape, dt))

    def sem(name):
        return ctx.enter_context(nc.semaphore(name))

    xn = sb("xn", [P, 2, E])
    xT = sb("xT", [P, 2, 2 * P])
    rT = sb("rT", [RANK, 3, 2 * P])
    rot = sb("rot", [96, 2, 2 * P])
    qk = sb("qk", [96, 2, 2, 2 * P])
    vz = sb("vz", [P, 2, 7 * P])
    nmax = sb("nmax", [P, 2, HEADS])
    probs = sb("probs", [P, HEADS, 2 * P])
    pT = sb("pT", [P, HEADS, 3, P])
    total = sb("total", [P, 2, HEADS])
    rec = sb("rec", [P, 2, HEADS])
    oT = sb("oT", [P, 2, 2 * P])
    mask = sb("mask", [P, P], BF16)
    identb = sb("identb", [P, P], BF16)
    rstd = sb("a_rstd", [P, 32])

    xn2 = sb("xn2", [P, 2, E])
    xcopy = sb("xcopy", [P, 2, E])
    x2T = sb("x2T", [P, 2, 2 * P])
    bn2 = sb("bn2", [P, 2, 6])
    mv2 = sb("mv2", [P, 2, 2])
    veps2 = sb("veps2", [P, 2])
    rstd2 = sb("rstd2", [P, 2])
    lg = sb("lg", [P, 2, NE])
    ex = sb("ex", [P, 2, NE])
    col = sb("col", [P, 6, 2])
    key = sb("key", [P, 2, NE])
    picks = sb("picks", [P, 2, 2, NE])
    rest = sb("rest", [P, 2, NE])
    member = sb("member", [P, 2, NE], BF16)
    where = sb("where", [P, 2, NE])
    chosen = sb("chosen", [P, 2, 2, NE])
    rowf = sb("rowf", [P, 2, 2])
    rowi = sb("rowi", [P, 2, 2], U32)
    count = sb("count", [P, 3, P], BF16)

    front = [ctx.enter_context(nc.psum_tensor(f"front{i}", [P, 512], F32)) for i in range(2)]
    sc = ctx.enter_context(nc.psum_tensor("sc", [P, 3, 2, 2 * P], F32))
    pt = [ctx.enter_context(nc.psum_tensor(f"pt{i}", [P, 4, P], F32)) for i in range(2)]
    outp = ctx.enter_context(nc.psum_tensor("outp", [P, 512], F32))

    a_w, b_w, vb_w, o_w, rope = att.a_w, att.b_w, att.vb_w, att.o_w, att.rope
    zeros_set = sem("a_zeros")
    mask_set = sem("mask_set")
    step = sem("a_step")
    rstd_out = sem("a_rstd_out")
    xn_set = sem("xn_set")
    xT_mm = sem("xT_mm")
    xT_set = sem("xT_set")
    r_mm = sem("r_mm")
    r_set = sem("r_set")
    qk_mm = sem("qk_mm")
    qk_set = sem("qk_set")
    v_mm = sem("v_mm")
    v_set = sem("v_set")
    s_mm = sem("s_mm")
    max_set = sem("max_set")
    exp_set = sem("exp_set")
    pt_mm = sem("pt_mm")
    pt_set = sem("pt_set")
    o_mm = sem("o_mm")
    probs_set = sem("probs_set")
    oT_set = sem("oT_set")
    out_mm = sem("out_mm")
    out_set = sem("out_set")
    alone2 = sem("alone2")
    alone3 = sem("alone3")
    var2_in = sem("var2_in")
    rstd2_out = sem("rstd2_out")
    xn2_set = sem("xn2_set")
    x2T_mm = sem("x2T_mm")
    x2T_set = sem("x2T_set")
    lg_mm = sem("lg_mm")
    lg_set = sem("lg_set")
    ex_set = sem("ex_set")
    member_set = sem("member_set")
    rank_mm = sem("rank_mm")
    row_set = sem("row_set")
    rank_read = sem("rank_read")

    PT = [(0, [(h, 0) for h in range(4)]), (0, [(4, 0), (5, 0)]),
          (1, [(h, 0) for h in range(4)]), (1, [(4, 0), (5, 0), (0, 1), (1, 1)]), (1, [(h, 1) for h in range(2, 6)])]

    def first(b):
        return isinstance(b, int) and b == 0

    with nc.Block() as block:
        @block.tensor
        def _(pe):
            pe.wait_ge(att.loads, 16 * 9)

            def tokens_T(b):
                pe.wait_ge(xn_set, b + 1)
                if not first(b):
                    pe.wait_ge(v_set, b)
                if not (isinstance(b, int) and b < 3):
                    pe.wait_ge(lg_set, b - 2)
                for t in range(2):
                    pe.transpose(front[0][:, t * P:(t + 1) * P], xn[:, t, 0:P], ident[:])
                    mm = pe.transpose(front[0][0:64, (2 + t) * P:(3 + t) * P], xn[:, t, P:E], ident[:])
                mm.then_inc(xT_mm, 1)

            def factor(b):
                pe.wait_ge(xT_set, b + 1)
                if not first(b):
                    pe.wait_ge(qk_set, 2 * b)
                if not (isinstance(b, int) and b < 3):
                    pe.wait_ge(x2T_set, b - 2)
                for i in range(3):
                    out = front[1][0:RANK, i * 2 * P:(i + 1) * 2 * P] if i < 2 else front[0][0:RANK, 0:2 * P]
                    pe.matmul(out, a_w[:, 0, i, :], xT[:, 0, :], start=True, stop=False)
                    mm = pe.matmul(out, a_w[0:64, 1, i, :], xT[0:64, 1, :], start=False, stop=True)
                    if i:
                        mm.then_inc(r_mm, 1)

            def qk_tile(t, b):
                pe.wait_ge(r_set, 2 * b + 2)
                if t:
                    pe.wait_ge(qk_set, 2 * b + 1)
                for r in range(2):
                    for i in range(2):
                        mm = pe.matmul(front[r][0:96, i * 2 * P:(i + 1) * 2 * P], b_w[:, i, r, 96 * t:96 * t + 96],
                                       rT[:, i, :], start=True, stop=True)
                mm.then_inc(qk_mm, 1)

            def values(b):
                pe.wait_ge(qk_set, 2 * b + 2)
                for t in range(2):
                    mm = pe.matmul(front[0][:, t * E:(t + 1) * E], rT[:, 2, t * P:(t + 1) * P], vb_w[:],
                                   start=True, stop=True)
                mm.then_inc(v_mm, 1)

            def scores(qt, b):
                pe.wait_ge(qk_set, 2 * b + 2)
                if qt or not first(b):
                    pe.wait_ge(exp_set, 2 * b + qt)
                n = (qt + 1) * P
                for g in range(3):
                    for t in range(2):
                        pe.matmul(sc[:, g, t, n - P:n], identb[:], mask[:], start=(t == 0), stop=False,
                                  skip_group_check=True)
                for t in range(2):
                    for g in range(3):
                        head = slice(32 * g, 32 * g + 32)
                        mm = pe.matmul(sc[:, g, t, 0:n], qk[head, t, 0, qt * P:(qt + 1) * P],
                                       qk[head, t, 1, 0:n], start=False, stop=(t == 1), skip_group_check=True)
                mm.then_inc(s_mm, 1)

            def probs_T(i, b):
                qt, blocks = PT[i]
                pe.wait_ge(probs_set, 2 * b + qt + 1)
                if not (first(b) and i < 2):
                    pe.wait_ge(pt_set, 5 * b + max(i - 1, 0))
                for j, (h, kt) in enumerate(blocks):
                    mm = pe.transpose(pt[i % 2][:, j, :], probs[:, h, kt * P:(kt + 1) * P], ident[:])
                mm.then_inc(pt_mm, 1)

            def weighted(t, b):
                if t == 0:
                    pe.wait_ge(pt_set, 5 * b + 5)
                    pe.wait_ge(v_set, b + 1)
                    if not first(b):
                        pe.wait_ge(out_set, b)
                rows, heads = ((P, range(4)), (2 * HD, range(4, HEADS)))[t]
                for h in heads:
                    for kt in range(2):
                        mm = pe.matmul(outp[0:rows, (2 * t + kt) * P:(2 * t + 2) * P], vz[:, kt, h * P:h * P + rows],
                                       pT[:, h, 2 * kt:2 + kt, :].rearrange("p j n -> p (j n)"),
                                       start=(h == heads[0] and kt == 0), stop=(h == heads[-1] and kt == 1),
                                       skip_group_check=True)
                if t == 1:
                    mm.then_inc(o_mm, 1)

            def out_proj(b):
                pe.wait_ge(oT_set, b + 1)
                if not (isinstance(b, int) and b < 2):
                    pe.wait_ge(rank_read, b - 1)
                for t in range(2):
                    o = outp[:, t * E:(t + 1) * E]
                    pe.matmul(o, oT[:, 0, t * P:(t + 1) * P], o_w[:, 0, :], start=True, stop=False)
                    mm = pe.matmul(o, oT[0:64, 1, t * P:(t + 1) * P], o_w[0:64, 1, :], start=False, stop=True)
                mm.then_inc(out_mm, 1)

            def route_T(b, f):
                pe.wait_ge(xn2_set, b + 1)
                pe.wait_ge(qk_set, 2 * f)
                for t in range(2):
                    pe.transpose(front[1][:, t * P:(t + 1) * P], xn2[:, t, 0:P], ident[:])
                    mm = pe.transpose(front[1][0:64, (2 + t) * P:(3 + t) * P], xn2[:, t, P:E], ident[:])
                mm.then_inc(x2T_mm, 1)

            def logits(b, f):
                pe.wait_ge(x2T_set, b + 1)
                pe.wait_ge(v_set, f)
                for t in range(2):
                    pe.matmul(front[0][:, t * NE:(t + 1) * NE], x2T[:, 0, t * P:(t + 1) * P], moe.rw[:, 0, :],
                              start=True, stop=False)
                    mm = pe.matmul(front[0][:, t * NE:(t + 1) * NE], x2T[0:64, 1, t * P:(t + 1) * P],
                                   moe.rw[0:64, 1, :], start=False, stop=True)
                mm.then_inc(lg_mm, 1)

            def ranks(b):
                pe.wait_ge(member_set, b + 1)
                pe.wait_ge(oT_set, min(b + 3, B) if isinstance(b, int) else b + 3)
                if not first(b):
                    pe.wait_ge(rank_read, b)
                o = outp[:, 0:3 * NE]
                pe.matmul(o[:, 0:NE], count[:, 0, :], member[:, 0, :], start=True, stop=True)
                pe.matmul(o[:, NE:2 * NE], count[:, 0, :], member[:, 1, :], start=True, stop=False)
                pe.matmul(o[:, NE:2 * NE], count[:, 1, :], member[:, 0, :], start=False, stop=True)
                pe.matmul(o[:, 2 * NE:3 * NE], count[:, 1, :], member[:, 0, :], start=True, stop=False)
                pe.matmul(o[:, 2 * NE:3 * NE], count[:, 2, :], member[:, 1, :], start=False,
                          stop=True).then_inc(rank_mm, 1)

            def body(b, after, late, later):
                scores(0, b)
                if after:
                    tokens_T(b + 1)
                if late:
                    out_proj(b - 1)
                if after:
                    factor(b + 1)
                scores(1, b)
                probs_T(0, b)
                if after:
                    qk_tile(0, b + 1)
                probs_T(1, b)
                if after:
                    qk_tile(1, b + 1)
                front_done = b + 2 if after else B
                for i in range(2, 5):
                    probs_T(i, b)
                weighted(0, b)
                if late:
                    route_T(b - 1, front_done)
                weighted(1, b)
                if after:
                    values(b + 1)
                if later:
                    ranks(b - 2)
                if late:
                    logits(b - 1, front_done)

            pe.wait_ge(mask_set, 3)
            pe.wait_ge(moe.loads, 16 * 4)
            tokens_T(0)
            factor(0)
            qk_tile(0, 0)
            qk_tile(1, 0)
            values(0)
            body(0, True, False, False)
            body(1, True, True, False)
            with pe.Fori(2, B - 1) as b:
                body(b, True, True, True)
            body(B - 1, False, True, True)
            out_proj(B - 1)
            pe.wait_ge(out_set, B)
            ranks(B - 2)
            route_T(B - 1, B)
            pe.wait_ge(lg_set, B - 1)
            logits(B - 1, B)
            ranks(B - 1)

        @block.scalar
        def _(act):
            def move_x2T(b):
                act.wait_ge(x2T_mm, b + 1)
                act.copy(x2T[:, 0, :], front[1][:, 0:2 * P])
                act.copy(x2T[0:64, 1, :], front[1][0:64, 2 * P:4 * P]).then_inc(x2T_set, 1)

            def exp_logits(b):
                act.wait_ge(lg_set, b + 1)
                act.activation(ex[:], lg[:], ACT.Exp).then_inc(ex_set, 1)

            def move_xT(b):
                act.wait_ge(xT_mm, b + 1)
                act.copy(xT[:, 0, :], front[0][:, 0:2 * P])
                act.copy(xT[0:64, 1, :], front[0][0:64, 2 * P:4 * P]).then_inc(xT_set, 1)

            def move_r(b):
                act.wait_ge(r_mm, 2 * b + 1)
                act.copy(rT[:, 0:2, :], front[1][0:RANK, :].rearrange("p (i n) -> p i n", i=2)).then_inc(r_set, 1)
                act.wait_ge(r_mm, 2 * b + 2)
                act.copy(rT[:, 2, :], front[0][0:RANK, 0:2 * P]).then_inc(r_set, 1)

            def move_v(b):
                act.wait_ge(v_mm, b + 1)
                if not first(b):
                    act.wait_ge(o_mm, b)
                for t in range(2):
                    for h0, h1 in ((0, 4), (4, HEADS)):
                        n = h1 - h0
                        own = vz[:, t, h0 * P:h0 * P + n * (P + HD)].rearrange("p (h x) -> p h x", h=n)
                        ins = act.copy(own[:, :, 0:HD], front[0][:, t * E + h0 * HD:t * E + h1 * HD].rearrange(
                            "p (h d) -> p h d", d=HD))
                ins.then_inc(v_set, 1)

            def exps(qt, b):
                act.wait_ge(max_set, 2 * b + qt + 1)
                if qt == 0 and not first(b):
                    act.wait_ge(pt_mm, 5 * b)
                if qt == 1:
                    act.wait_ge(pt_mm, 5 * b + 2)
                n = (qt + 1) * P
                for h in range(HEADS):
                    ins = act.activation(probs[:, h, 0:n], sc[:, h % 3, h // 3, 0:n], ACT.Exp,
                                         bias=nmax[:, qt, h:h + 1], scale=1.0)
                ins.then_inc(exp_set, 1)

            def move_pT(i, b):
                qt, blocks = PT[i]
                act.wait_ge(pt_mm, 5 * b + i + 1)
                if i == 0 and not first(b):
                    act.wait_ge(o_mm, b)
                runs = {}
                for j, (h, kt) in enumerate(blocks):
                    runs.setdefault(kt, []).append((j, h))
                for kt, r in runs.items():
                    (j0, h0), n = r[0], len(r)
                    ins = act.copy(pT[:, h0:h0 + n, qt + kt, :], pt[i % 2][:, j0:j0 + n, :])
                ins.then_inc(pt_set, 1)

            def move_oT(b):
                act.wait_ge(o_mm, b + 1)
                if not first(b):
                    act.wait_ge(out_mm, b)
                act.copy(oT[:, 0, :], outp[:, 0:2 * P])
                act.copy(oT[0:64, 1, :], outp[0:64, 2 * P:4 * P]).then_inc(oT_set, 1)

            def body(b, after, late):
                if after:
                    move_xT(b + 1)
                exps(0, b)
                if after:
                    move_r(b + 1)
                move_pT(0, b)
                move_pT(1, b)
                exps(1, b)
                for i in range(2, 5):
                    move_pT(i, b)
                if late:
                    move_x2T(b - 1)
                move_oT(b)
                if after:
                    move_v(b + 1)
                if late:
                    exp_logits(b - 1)

            act.wait_ge(zeros_set, 1)
            move_xT(0)
            move_r(0)
            move_v(0)
            body(0, True, False)
            with act.Fori(1, B - 1) as b:
                body(b, True, True)
            body(B - 1, False, True)
            move_x2T(B - 1)
            exp_logits(B - 1)

        @block.gpsimd
        def _(pool):
            pool.tensor_tensor(rstd[:].rearrange("p (b t) -> p b t", t=2), att.mv[:, 1],
                               mhalf[:].rearrange("p (b t) -> p b t", t=2), ALU.pow).then_inc(rstd_out, 1)

            def power(b):
                pool.wait_ge(var2_in, b + 1)
                pool.tensor_tensor(rstd2[:], veps2[:], mhalf[:, 0:2], ALU.pow).then_inc(rstd2_out, 1)

            def scatter(b):
                pool.wait_ge(row_set, b + 1)
                pool.sem_inc(alone3, 1)
                for t in range(2):
                    for c in range(2):
                        pool.indirect_dma_start(
                            moe.xs.ap(), bass.IndirectOffsetOnAxis(rowi[0:TQ[t], c, t:t + 1], 0),
                            xcopy[0:TQ[t], t, :], None).then_inc(moe.rows, 16)

            power(0)
            with pool.Fori(1, B - 1) as b:
                power(b)
                scatter(b - 1)
            scatter(B - 2)
            power(B - 1)
            scatter(B - 1)

        @block.vector
        def _(dve):
            dve.memset(vz[:], 0.0).then_inc(zeros_set, 1)
            dve.wait_ge(att.loads, 16 * 9)
            dve.tensor_copy(mask[:], att.maskf[:]).then_inc(mask_set, 1)
            dve.tensor_copy(identb[:], ident[:]).then_inc(mask_set, 1)
            dve.tensor_copy(count[:], att.countf[:]).then_inc(mask_set, 1)
            dve.wait_ge(rstd_out, 1)
            steps, counted = [0], [0]

            def then(ins):
                ins.then_inc(step, 1)
                steps[0] = steps[0] + 1
                counted[0] += 1
                dve.wait_ge(step, steps[0])

            def normalise(b):
                if not first(b):
                    dve.wait_ge(xT_mm, b)
                for t in range(2):
                    ins = dve.tensor_scalar(xn[:, t, :], tok[:, b, t, :], att.mv[:, 0, b, t:t + 1],
                                            rstd[:, bass.ds(2 * b + t, 1)], ALU.subtract, ALU.mult)
                ins.then_inc(xn_set, 1)

            def rotate(t, b):
                dve.wait_ge(qk_mm, 2 * b + t + 1)
                q = qk[:, t, :, :]
                dve.tensor_tensor(q, front[0][0:96, :].rearrange("p (i n) -> p i n", i=2), rope[:, 0], ALU.mult)
                then(dve.tensor_tensor(rot[:], front[1][0:96, :].rearrange("p (i n) -> p i n", i=2), rope[:, 1],
                                       ALU.mult))
                dve.tensor_tensor(q, q, rot[:], ALU.add).then_inc(qk_set, 1)

            def maxima(qt, b):
                dve.wait_ge(s_mm, 2 * b + qt + 1)
                n = (qt + 1) * P
                dve.tensor_reduce(nmax[:, qt, :].rearrange("p (t g) -> p g t", g=3), sc[:, :, :, 0:n],
                                  AX.X, ALU.max, negate=True).then_inc(max_set, 1)

            def divide(qt, b):
                dve.wait_ge(exp_set, 2 * b + qt + 1)
                p = probs[:, :, 0:(qt + 1) * P]
                then(dve.tensor_reduce(total[:, qt, :], p, AX.X, ALU.add))
                then(dve.reciprocal(rec[:, qt, :], total[:, qt, :]))
                dve.tensor_tensor(p, p, rec[:, qt, :].unsqueeze(2).broadcast_to([P, HEADS, (qt + 1) * P]),
                                  ALU.mult).then_inc(probs_set, 1)

            def residual(b):
                dve.wait_ge(out_mm, b + 1)
                x = tok[:, b, :, :]
                dve.tensor_tensor(x, outp[:, 0:2 * E].rearrange("p (t e) -> p t e", t=2), x,
                                  ALU.add).then_inc(out_set, 1)

            def second_moments(b):
                dve.wait_ge(out_set, b + 1)
                dve.sem_inc(alone2, 1)
                for t in range(2):
                    ins = dve.bn_stats(bn2[:, t, :], tok[:, b, t, :])
                then(ins)
                dve.sem_inc(alone2, 1)
                for t in range(2):
                    ins = dve.bn_aggr(mv2[:, t, :], bn2[:, t, :])
                then(ins)
                dve.tensor_scalar(veps2[:], mv2[:, :, 1], EPS, None, ALU.add).then_inc(var2_in, 1)

            def normalise2(b):
                dve.wait_ge(rstd2_out, b + 1)
                for t in range(2):
                    ins = dve.tensor_scalar(xn2[:, t, :], tok[:, b, t, :], mv2[:, t, 0:1], rstd2[:, t:t + 1],
                                            ALU.subtract, ALU.mult)
                ins.then_inc(xn2_set, 1)

            def wide(c):
                return col[:, c, :].unsqueeze(2).broadcast_to([P, 2, NE])

            def shifted_logits(b):
                dve.wait_ge(lg_mm, b + 1)
                o = front[0][:, 0:2 * NE].rearrange("p (t e) -> p t e", t=2)
                then(dve.tensor_reduce(col[:, 0, :], o, AX.X, ALU.max))
                dve.tensor_tensor(lg[:], o, wide(0), ALU.subtract).then_inc(lg_set, 1)

            def pick(src, c):
                flat = "p t e -> p (t e)"
                then(dve.tensor_reduce(col[:, 2, :], src, AX.X, ALU.max))
                then(dve.tensor_tensor(key[:], src, wide(2), ALU.is_equal))
                then(dve.scalar_tensor_tensor(out=key[:].rearrange(flat), in0=key[:].rearrange(flat),
                                              scalar=-float(NE), in1=att.iota[:].rearrange(flat),
                                              op0=ALU.mult, op1=ALU.add))
                then(dve.tensor_reduce(col[:, 3, :], key[:], AX.X, ALU.min))
                then(dve.tensor_tensor(picks[:, c], key[:], wide(3), ALU.is_equal))

            def choose(b):
                flat = "p t e -> p (t e)"
                dve.wait_ge(ex_set, b + 1)
                then(dve.tensor_reduce(col[:, 1, :], ex[:], AX.X, ALU.add))
                then(dve.reciprocal(col[:, 1, :], col[:, 1, :]))
                p = ex[:]
                then(dve.tensor_tensor(p, p, wide(1), ALU.mult))
                dve.tensor_copy(moe.pr[:, bass.ds(2 * b, 2), :], p)
                pick(p, 0)
                then(dve.scalar_tensor_tensor(out=rest[:].rearrange(flat), in0=picks[:, 0].rearrange(flat),
                                              scalar=-2.0, in1=p.rearrange(flat), op0=ALU.mult, op1=ALU.add))
                pick(rest[:], 1)
                dve.tensor_copy(moe.sel[:, :, bass.ds(2 * b, 2), :], picks[:])
                dve.tensor_tensor(member[:], picks[:, 0], picks[:, 1], ALU.add).then_inc(member_set, 1)

            def copy_rows(b):
                if not first(b):
                    dve.wait_ge(moe.rows, b * 64)
                then(dve.tensor_copy(xcopy[:], xn2[:]))

            def place(b):
                dve.wait_ge(rank_mm, b + 1)
                run = moe.run[:].unsqueeze(1).broadcast_to([P, 2, NE])
                o = outp[:, 0:3 * NE]
                then(dve.tensor_tensor(where[:], o[:, 0:2 * NE].rearrange("p (t e) -> p t e", t=2), run, ALU.add))
                dve.tensor_tensor(moe.run[:], o[:, 2 * NE:3 * NE], moe.run[:], ALU.add).then_inc(rank_read, 1)
                for c in range(2):
                    ins = dve.tensor_tensor(chosen[:, c], where[:], picks[:, c], ALU.mult)
                then(ins)
                then(dve.tensor_reduce(rowf[:], chosen[:], AX.X, ALU.add))
                if not first(b):
                    dve.wait_ge(moe.rows, b * 64)
                dve.tensor_copy(moe.at[:, bass.ds(2 * b, 2), :], rowf[:].rearrange("p c t -> p t c"))
                dve.tensor_copy(rowi[:], rowf[:]).then_inc(row_set, 1)

            def body(b, after, late, later, ahead=True):
                maxima(0, b)
                if late:
                    residual(b - 1)
                divide(0, b)
                maxima(1, b)
                if after:
                    rotate(0, b + 1)
                if late:
                    second_moments(b - 1)
                divide(1, b)
                if after:
                    rotate(1, b + 1)
                if later:
                    copy_rows(b - 2)
                if late:
                    normalise2(b - 1)
                if ahead:
                    normalise(b + 2)
                if later:
                    choose(b - 2)
                    place(b - 2)
                if late:
                    shifted_logits(b - 1)

            normalise(0)
            rotate(0, 0)
            rotate(1, 0)
            normalise(1)
            body(0, True, False, False)
            body(1, True, True, False)
            base = steps[0]
            with dve.Fori(2, B - 2) as b:
                steps[0] = base + (b - 2) * ASTEPS
                n0 = counted[0]
                body(b, True, True, True)
                assert counted[0] - n0 == ASTEPS, counted[0] - n0
            steps[0] = base + (B - 4) * ASTEPS
            body(B - 2, True, True, True, ahead=False)
            body(B - 1, False, True, True, ahead=False)
            residual(B - 1)
            second_moments(B - 1)
            choose(B - 2)
            copy_rows(B - 2)
            place(B - 2)
            normalise2(B - 1)
            shifted_logits(B - 1)
            choose(B - 1)
            copy_rows(B - 1)
            place(B - 1)


def expert_stage(nc, io, ctx, tok, ident, moe):
    def sb(name, shape, dt=F32):
        return ctx.enter_context(nc.sbuf_tensor(name, shape, dt))

    def sem(name):
        return ctx.enter_context(nc.semaphore(name))

    NG = 8
    zero = sb("zero", [P, E])
    lane = sb("lane", [P, NE])
    behind = sb("behind", [P, NE], U32)
    nblk = sb("nblk", [P, 5, NE])
    nblki = sb("nblki", [P, 2, NE], I32)
    onerow = sb("onerow", [P, NE])
    blk = sb("blk", [1, NBLK, NE])
    past = sb("past", [1, 2, NBLK, NE])
    tabf = sb("tabf", [1, 2, NBLK])
    tab = sb("tab", [1, 2, NBLK], I32)
    count_w = sb("count_w", [P, 2, P])
    imp2 = sb("imp2", [P, 2, NE])
    load = sb("load", [P, 3, NE])
    g = sb("g", [P, 2, NT, NE])
    wts = sb("wts", [P, 3, NT, 2])
    result_at = sb("result_at", [P, NT, 2], U32)
    col = sb("w_col", [P, 2, NT])
    xb = sb("xb", [P, 2, E])
    xT = sb("b_xT", [P, 2, 2, P])
    hs = sb("hs", [P, 2, HID])
    hT = sb("hT", [P, 2, HT, P])
    yb = sb("yb", [P, 2, E])
    got = sb("got", [P, NG, E])

    px = [ctx.enter_context(nc.psum_tensor(f"px{i}", [P, 2, P], F32)) for i in range(2)]
    ph = [ctx.enter_context(nc.psum_tensor(f"ph{i}", [P, HID], F32)) for i in range(2)]
    pt = [ctx.enter_context(nc.psum_tensor(f"pht{i}", [P, HT, P], F32)) for i in range(2)]
    py = [ctx.enter_context(nc.psum_tensor(f"py{i}", [P, 512], F32)) for i in range(2)]

    loads = sem("e_loads")
    step = sem("e_step")
    zero_set = sem("zero_set")
    behind_set = sem("behind_set")
    rest_out = sem("rest_out")
    tab_set = sem("tab_set")
    x_in = [sem(f"x_in{i}") for i in range(2)]
    x_mm = sem("x_mm")
    x_set = sem("x_set")
    h_mm = sem("h_mm")
    h_set = sem("h_set")
    t_mm = sem("t_mm")
    t_set = sem("t_set")
    y_mm = sem("y_mm")
    y_set = sem("y_set")
    y_out = [sem(f"y_out{i}") for i in range(2)]
    at_set = sem("at_set")
    imp_in = sem("imp_in")
    imp_mm = sem("imp_mm")
    imp_read = sem("imp_read")
    gate_set = sem("gate_set")
    g_in = [sem(f"g_in{i}") for i in range(NG)]
    added = sem("added")
    done = sem("done")

    ZERO_ROWS = 16 * NE

    def is_int(j):
        return isinstance(j, int)

    with nc.Block() as block:
        @block.sync
        def _(sp):
            for dst, name in ((lane[:], "lane"), (blk[:], "block0"), (count_w[:], "count_w")):
                sp.dma_start(dst, io[name]).then_inc(loads, 16)
            sp.wait_ge(zero_set, 1)
            sp.dma_start(moe.xs.ap()[NE * CAP:NE * CAP + P, :], zero[:]).then_inc(rest_out, 16)
            sp.wait_ge(tab_set, 1)
            sp.wait_ge(moe.rows, 64 * B + ZERO_ROWS)
            sp.wait_ge(rest_out, 16)

            def row(j):
                return sp.value_load(tab[0:1, 1, bass.ds(j, 1)] if not is_int(j) else tab[0:1, 1, j:j + 1],
                                     min_val=0, max_val=NE * CAP)

            def load(j, par):
                if not (is_int(j) and j < 2):
                    sp.wait_ge(x_mm, j - 1)
                sp.dma_start(xb[:, par, :], moe.xs.ap()[bass.ds(row(j), P), :]).then_inc(x_in[par], 16)

            def store(j, par):
                sp.wait_ge(y_set, j + 1)
                sp.dma_start(moe.ys.ap()[bass.ds(j * P, P), :], yb[:, par, :]).then_inc(y_out[par], 16)

            load(0, 0)
            load(1, 1)
            load(2, 0)
            load(3, 1)
            with sp.Fori(2, NBLK // 2) as i:
                for par in range(2):
                    load(2 * i + par, par)
                    store(2 * i + (par - 4), par)
            for j in range(NBLK - 4, NBLK):
                store(j, j % 2)
            sp.wait_ge(added, 2 * NT)
            for t in range(2):
                sp.dma_start(io["out"][:, t * P:t * P + TQ[t], :].rearrange("b t e -> t b e"),
                             tok[0:TQ[t], :, t, :]).then_inc(done, 16)
            sp.wait_ge(done, 32)

        @block.tensor
        def _(pe):
            def load_T(j, par):
                pe.wait_ge(x_in[par], (j // 2 + 1) * 16 if is_int(j) else (j + (2 - par)) * 8)
                if not (is_int(j) and j < 2):
                    pe.wait_ge(x_set, j - 1)
                pe.transpose(px[par][:, 0, :], xb[:, par, 0:P], ident[:])
                pe.transpose(px[par][0:64, 1, :], xb[:, par, P:E], ident[:]).then_inc(x_mm, 1)

            def expert(j):
                return pe.value_load(tab[0:1, 0, bass.ds(j, 1)] if not is_int(j) else tab[0:1, 0, j:j + 1],
                                     min_val=0, max_val=NE - 1)

            def hidden(j, par):
                e = expert(j)
                pe.wait_ge(x_set, j + 1)
                if not (is_int(j) and j < 2):
                    pe.wait_ge(h_set, j - 1)
                w = moe.w1[:].rearrange("p c e n -> p c (e n)")
                pe.matmul(ph[par][:], xT[:, par, 0, :], w[:, 0, bass.ds(e * HID, HID)], start=True, stop=False)
                pe.matmul(ph[par][:], xT[0:64, par, 1, :], w[0:64, 1, bass.ds(e * HID, HID)],
                          start=False, stop=True).then_inc(h_mm, 1)

            def hidden_T(j, par):
                pe.wait_ge(h_set, j + 1)
                if not (is_int(j) and j < 2):
                    pe.wait_ge(t_set, j - 1)
                for i in range(HT):
                    mm = pe.transpose(pt[par][:, i, :], hs[:, par, i * P:(i + 1) * P], ident[:])
                mm.then_inc(t_mm, 1)

            def output(j, par):
                e = expert(j)
                pe.wait_ge(t_set, j + 1)
                if not (is_int(j) and j < 2):
                    pe.wait_ge(y_set, j - 1)
                w = moe.w2[:].rearrange("p e i n -> p (e i n)")
                for i in range(HT):
                    mm = pe.matmul(py[par][:, 0:E], hT[:, par, i, :], w[:, bass.ds(e * (HT * E) + i * E, E)],
                                   start=(i == 0), stop=(i == HT - 1))
                mm.then_inc(y_mm, 1)

            pe.wait_ge(loads, 16 * 3)
            pe.wait_ge(imp_in, 1)
            for t in range(2):
                mm = pe.matmul(py[1][:, 0:NE], count_w[:, t, :], imp2[:, t, :], start=(t == 0), stop=(t == 1))
            mm.then_inc(imp_mm, 1)
            pe.wait_ge(tab_set, 1)
            load_T(0, 0)
            hidden(0, 0)
            load_T(1, 1)
            hidden(1, 1)
            hidden_T(0, 0)
            load_T(2, 0)
            pe.wait_ge(imp_read, 1)

            def pair(i):
                for par in range(2):
                    hidden(2 * i + par, par)
                    hidden_T(2 * i + (par - 1), 1 - par)
                    output(2 * i + (par - 2), par)
                    load_T(2 * i + (par + 1), 1 - par)

            pair(1)
            with pe.Fori(2, NBLK // 2 - 1) as i:
                pair(i)
            j = NBLK - 2
            hidden(j, 0)
            hidden_T(j - 1, 1)
            output(j - 2, 0)
            load_T(j + 1, 1)
            hidden(j + 1, 1)
            hidden_T(j, 0)
            output(j - 1, 1)
            hidden_T(j + 1, 1)
            output(j, 0)
            output(j + 1, 1)

        @block.scalar
        def _(act):
            def move_xT(j, par):
                act.wait_ge(x_mm, j + 1)
                if not (is_int(j) and j < 2):
                    act.wait_ge(h_mm, j - 1)
                act.copy(xT[:, par, 0, :], px[par][:, 0, :])
                act.copy(xT[0:64, par, 1, :], px[par][0:64, 1, :]).then_inc(x_set, 1)

            def silu(j, par):
                act.wait_ge(h_mm, j + 1)
                if not (is_int(j) and j < 2):
                    act.wait_ge(t_mm, j - 1)
                act.activation(hs[:, par, :], ph[par][:], ACT.Silu).then_inc(h_set, 1)

            move_xT(0, 0)
            silu(0, 0)
            move_xT(1, 1)
            silu(1, 1)
            move_xT(2, 0)
            with act.Fori(1, NBLK // 2 - 1) as i:
                for par in range(2):
                    silu(2 * i + par, par)
                    move_xT(2 * i + (par + 1), 1 - par)
            j = NBLK - 2
            silu(j, 0)
            move_xT(j + 1, 1)
            silu(j + 1, 1)

        @block.gpsimd
        def _(pool):
            pool.wait_ge(behind_set, 1)
            for e in range(NE):
                pool.indirect_dma_start(moe.xs.ap(), bass.IndirectOffsetOnAxis(behind[:, e:e + 1], 0),
                                        zero[:], None).then_inc(moe.rows, 16)
            pool.wait_ge(at_set, 1)
            for par in range(2):
                pool.wait_ge(y_out[par], 16 * (NBLK // 2))
            for k in range(2 * NT):
                t, c = k // 2, k % 2
                n = TQ[t % 2]
                if k >= NG:
                    pool.wait_ge(added, k - NG + 1)
                pool.indirect_dma_start(got[0:n, k % NG, :], None, moe.ys.ap(),
                                        bass.IndirectOffsetOnAxis(result_at[0:n, t, c:c + 1], 0)
                                        ).then_inc(g_in[k % NG], 16)

        @block.vector
        def _(dve):
            steps = [0]

            def then(ins):
                ins.then_inc(step, 1)
                steps[0] = steps[0] + 1
                dve.wait_ge(step, steps[0])

            dve.memset(onerow[:], 1.0)
            dve.memset(zero[:], 0.0).then_inc(zero_set, 1)
            dve.wait_ge(loads, 16 * 3)
            dve.tensor_tensor(behind[:], moe.run[:], lane[:], ALU.add).then_inc(behind_set, 1)
            n0 = nblk[:, 0, :]
            then(dve.tensor_copy(nblk[:, 1, :], moe.run[:]))
            for e in range(NE):
                ins = dve.tensor_scalar(nblk[:, 0, e:e + 1], nblk[:, 1, e:e + 1], float(P - 1 - e * CAP), None, ALU.add)
            then(ins)
            then(dve.tensor_copy(nblki[:, 0, :], n0))
            then(dve.tensor_scalar(nblki[:, 1, :], nblki[:, 0, :], 7, None, ALU.arith_shift_right))
            then(dve.tensor_copy(nblk[:, 1, :], nblki[:, 1, :]))
            then(dve.tensor_tensor_scan(nblk[:, 2, :], onerow[:], nblk[:, 1, :], 0.0, ALU.mult, ALU.add))
            then(dve.tensor_scalar(nblk[:, 3, :], nblk[:, 1, :], -float(P), float(CAP), ALU.mult, ALU.add))
            ends = nblk[0:1, 2, :].unsqueeze(1).broadcast_to([1, NBLK, NE])
            adds = nblk[0:1, 3, :].unsqueeze(1).broadcast_to([1, NBLK, NE])
            then(dve.tensor_tensor(past[:, 0], blk[:], ends, ALU.is_ge))
            then(dve.tensor_tensor(past[:, 1], past[:, 0], adds, ALU.mult))
            then(dve.tensor_reduce(tabf[:], past[:], AX.X, ALU.add))
            then(dve.scalar_tensor_tensor(out=tabf[:, 1, :], in0=blk[:, :, 0], scalar=float(P), in1=tabf[:, 1, :],
                                          op0=ALU.mult, op1=ALU.add))
            dve.tensor_scalar(tabf[:, 0, :], tabf[:, 0, :], float(NE - 1), None, ALU.min)
            then(dve.tensor_scalar(tabf[:, 1, :], tabf[:, 1, :], float(NE * CAP), None, ALU.min))
            dve.tensor_copy(tab[:], tabf[:]).then_inc(tab_set, 1)
            then(dve.tensor_tensor(nblk[:, 4, :], nblk[:, 2, :], nblk[:, 1, :], ALU.subtract))
            for e in range(NE):
                ins = dve.tensor_scalar(nblk[:, 3, e:e + 1], nblk[:, 4, e:e + 1], float(P), -float(e * CAP),
                                        ALU.mult, ALU.add)
            then(ins)
            shift = nblk[:, 3, :].unsqueeze(1).broadcast_to([P, NT, NE])
            for c in range(2):
                then(dve.tensor_tensor(g[:, c], moe.sel[:, c], shift, ALU.mult))
                then(dve.tensor_reduce(wts[:, 0, :, c], g[:, c], AX.X, ALU.add))
            then(dve.tensor_tensor(wts[:, 2], wts[:, 0], moe.at[:], ALU.add))
            dve.tensor_copy(result_at[:], wts[:, 2]).then_inc(at_set, 1)
            dve.tensor_reduce(imp2[:], moe.pr[:].rearrange("p (b t) e -> p t e b", t=2), AX.X,
                              ALU.add).then_inc(imp_in, 1)
            dve.wait_ge(imp_mm, 1)
            dve.tensor_scalar(load[:, 0, :], py[1][:, 0:NE], -1.0, 1.0 - DECAY, ALU.add, ALU.mult).then_inc(imp_read, 1)
            dve.wait_ge(imp_read, 1)
            then(dve.tensor_scalar(load[:, 1, :], load[:, 0, :], 1.0, LOAD_EPS, ALU.add, ALU.add))
            then(dve.reciprocal(load[:, 2, :], load[:, 1, :]))
            w = load[:, 2, :].unsqueeze(1).broadcast_to([P, NT, NE])
            then(dve.tensor_tensor(moe.pr[:], moe.pr[:], w, ALU.mult))
            for c in range(2):
                then(dve.tensor_tensor(g[:, c], moe.pr[:], moe.sel[:, c], ALU.mult))
                then(dve.tensor_reduce(wts[:, 0, :, c], g[:, c], AX.X, ALU.add))
            then(dve.tensor_tensor(col[:, 0, :], wts[:, 0, :, 0], wts[:, 0, :, 1], ALU.add))
            then(dve.reciprocal(col[:, 1, :], col[:, 0, :]))
            then(dve.tensor_tensor(wts[:, 1], wts[:, 0], col[:, 1, :].unsqueeze(2).broadcast_to([P, NT, 2]), ALU.mult))

            def move_hT(j, par):
                dve.wait_ge(t_mm, j + 1)
                if not (is_int(j) and j < 2):
                    dve.wait_ge(y_mm, j - 1)
                dve.tensor_copy(hT[:, par], pt[par][:]).then_inc(t_set, 1)

            def move_y(j, par):
                dve.wait_ge(y_mm, j + 1)
                if not (is_int(j) and j < 2):
                    dve.wait_ge(y_out[par], (j // 2) * 16 if is_int(j) else (j - par) * 8)
                dve.tensor_copy(yb[:, par, :], py[par][:, 0:E]).then_inc(y_set, 1)

            move_hT(0, 0)
            move_hT(1, 1)
            move_y(0, 0)
            move_hT(2, 0)
            move_y(1, 1)
            with dve.Fori(1, NBLK // 2 - 1) as i:
                for par in range(2):
                    move_hT(2 * i + (par + 1), 1 - par)
                    move_y(2 * i + par, par)
            move_hT(NBLK - 1, 1)
            move_y(NBLK - 2, 0)
            move_y(NBLK - 1, 1)
            for k in range(2 * NT):
                t, c = k // 2, k % 2
                n = TQ[t % 2]
                x = tok[0:n, t // 2, t % 2, :]
                dve.wait_ge(g_in[k % NG], 16 * (k // NG + 1))
                if c:
                    dve.wait_ge(added, k)
                dve.scalar_tensor_tensor(out=x, in0=got[0:n, k % NG, :], scalar=wts[0:n, 1, t, c:c + 1], in1=x,
                                         op0=ALU.mult, op1=ALU.add).then_inc(added, 1)




def laid_out(inputs):
    f = np.float32
    got = {k: np.asarray(v) for k, v in inputs.items()}
    x = got["x"]
    a = {}
    xp = np.zeros((B, 40 * UT * P + XR), f)
    xp[:, :T_IN] = x
    idx = 40 * np.arange(UT * P)[:, None] + np.arange(WIN)[None, :]
    xw = np.ones((B, UT * P, XR), f)
    xw[:, :, :WIN] = xp[:, idx]
    a["xw"] = np.ascontiguousarray(xw.reshape(B, UT, P, XR).transpose(0, 2, 1, 3))
    last = np.zeros((B, 1, K0 + 1), f)
    last[:, 0, :5] = x[:, 5 * T0:]
    last[:, 0, K0] = 1.0
    a["xlast"] = last
    w0 = got["L0_tok_cw0"].reshape(C, K0).T
    w0win = np.zeros((P, 8, C), f)
    for base in (0, LO):
        for v in range(8):
            w0win[base + 5 * v:base + 5 * v + K0, v, :] = w0
        w0win[base + WIN, :, :] = got["L0_tok_cb0"]
    a["w0win"] = w0win
    a["w11"] = np.concatenate([w0, got["L0_tok_cb0"][None]], 0)
    for l in range(1, 6):
        a[f"w{l}T"] = np.ascontiguousarray(got[f"L0_tok_cw{l}"].transpose(1, 2, 0))
    a["chan"] = np.stack([np.stack([got[f"L0_tok_{n}{l}"] for n in ("cb", "gw", "gb")], -1)
                          for l in range(6)], 1)
    a["pwT"] = np.ascontiguousarray(got["L0_tok_pw"].T)
    a["pb"] = got["L0_tok_pb"][None]
    a["ident"] = np.eye(P, dtype=f)
    a["gavg"] = np.kron(np.eye(C // GROUP), np.full((GROUP, GROUP), 1.0 / GROUP)).astype(f)
    sel = np.zeros((XR, 8, K0 + 1), f)
    for v in range(8):
        sel[5 * v + np.arange(K0), v, np.arange(K0)] = 1.0
        sel[WIN, v, K0] = 1.0
    a["sel"] = sel
    a_w = np.zeros((P, 2, 3, RANK), f)
    for i, n in enumerate("qkv"):
        m = got[f"L0_attn_{n}A"]
        a_w[:, 0, i], a_w[:64, 1, i] = m[:P], m[P:]
    a["a_w"] = a_w
    swap = (np.arange(E) // HD) * HD + (np.arange(E) % HD + HD // 2) % HD
    a["b_w"] = np.stack([np.stack([got[f"L0_attn_{n}B"], got[f"L0_attn_{n}B"][:, swap]], 1) for n in "qk"], 1)
    a["vb_w"] = got["L0_attn_vB"]
    o_w = np.zeros((P, 2, E), f)
    o_w[:, 0], o_w[:64, 1] = got["L0_attn_o_w"][:P], got["L0_attn_o_w"][P:]
    a["o_w"] = o_w
    inv = (1.0 / 10000.0 ** (np.arange(0, HD, 2, dtype=f) / f(HD))).astype(f)
    angle = np.outer(np.concatenate([inv, inv]), np.arange(2 * P, dtype=f)).astype(f)
    sign = np.where(np.arange(HD) < HD // 2, -1.0, 1.0)[:, None]
    rope = np.stack([np.cos(angle.astype(np.float64)), sign * np.sin(angle.astype(np.float64))], 1)
    rope = np.stack([rope / np.sqrt(HD), rope], 2)
    a["rope"] = np.tile(rope, (3, 1, 1, 1)).astype(f)
    rw = np.zeros((P, 2, NE), f)
    rw[:, 0], rw[:64, 1] = got["L0_ffn_router_w"].T[:P], got["L0_ffn_router_w"].T[P:]
    a["rw"] = rw
    w1 = got["L0_ffn_w1"].transpose(2, 0, 1)
    a["w1a"], a["w1b"] = np.ascontiguousarray(w1[:P]), np.ascontiguousarray(w1[P:])
    a["w2x"] = np.ascontiguousarray(got["L0_ffn_w2"].reshape(NE, E, HT, P).transpose(3, 0, 2, 1))
    a["iota"] = np.tile(np.arange(NE, dtype=f), (P, 2, 1))
    count = np.ones((P, 3, P), f)
    count[:, 0] = np.triu(np.ones((P, P)), 1)
    count[TQ[1]:, 2] = 0.0
    a["count"] = count
    a["row0"] = np.tile(np.arange(NE, dtype=f) * CAP, (P, 1))
    a["lane"] = np.tile(np.arange(P, dtype=f)[:, None], (1, NE))
    a["block0"] = np.tile(np.arange(NBLK, dtype=f)[None, :, None], (1, 1, NE))
    count_w = np.ones((P, 2, P), f)
    count_w[TQ[1]:, 1] = 0.0
    a["count_w"] = count_w
    a["mask"] = np.where(np.arange(P)[:, None] >= np.arange(P)[None], 0.0, -1e30).astype(f)
    return a


def kernel(**inputs):
    import concourse.bacc as bacc
    from concourse.bass_utils import run_bass_kernel_spmd

    nc = bacc.Bacc("TRN2", target_bir_lowering=False, num_devices=1)
    arrays, io = {}, {}
    for name, a in laid_out(inputs).items():
        arrays[f"in_{name}"] = a
        io[name] = nc.dram_tensor(f"in_{name}", a.shape, mybir.dt.from_np(a.dtype), kind="ExternalInput").ap()
    io["out"] = nc.dram_tensor("out_0", (B, T5, E), F32, kind="ExternalOutput").ap()
    audio_tower(nc, io)
    r = run_bass_kernel_spmd(nc, [arrays], core_ids=[0])
    return r.results[0]["out_0"]
```

```python
from contextlib import ExitStack

import numpy as np

import concourse.bass as bass
from concourse import mybir

F32 = mybir.dt.float32
F16 = mybir.dt.float16
BF16 = mybir.dt.bfloat16
U32 = mybir.dt.uint32
I32 = mybir.dt.int32
ALU = mybir.AluOpType
ACT = mybir.ActivationFunctionType
AX = mybir.AxisListType

P = 128
B, T_IN = 16, 40000
C = 128
GROUP = 4
E = 192
EPS = 1e-5
T0 = (T_IN - 10) // 5 + 1
T1 = (T0 - 3) // 2 + 1
T2 = (T1 - 3) // 2 + 1
T3 = (T2 - 3) // 2 + 1
T4 = (T3 - 3) // 2 + 1
T5 = (T4 - 2) // 2 + 1
U = 1000
HU = U // 2
WIN = 45
XR = WIN + 1
K0 = 10
LO = 64
S0 = 1024.0
UT = (U + P - 1) // P
TAILROWS = U - (UT - 1) * P
TQ = [P, T5 - P]

HEADS, HD = 6, 32
RANK = E // 4
NE, HID = 8, 512
HT = HID // P
NT = 2 * B
CAP = ((B * T5 + 2 * P - 1) // P) * P
NBLK = (2 * B * T5 + NE * (P - 1)) // P
ASTEPS = 28
XW = E + 1
RESULTS = NT * P * 2
SX, SH = 1024.0, 256.0
DECAY, LOAD_EPS = 0.9, 0.01

MISC_PER_BODY = 14
STEPS = 39


def half_cols(last, h):
    return HU - 1 if last and h == 1 else HU


L1_CHUNKS = [(q, h) for q in (0, 3, 1, 2) for h in range(2)]
L0_CHUNKS = [(v, h) for v in (7, 0, 1, 2, 3, 4, 5, 6) for h in range(2)]
GELU1 = [(0, 0), (1, 0), (2, 0), (0, 1), (1, 1), (2, 1), (3, 0), (3, 1)]
RING = ([(1, c) for c in range(7)] + [(0, c) for c in range(5)] + [(1, 7)] + [(0, c) for c in range(5, 16)])


def ring_bank(use):
    return RING.index(use) % 3


def taps_of(plane_out, planes_in, h, n, taps=3):
    for k in range(taps):
        q = 2 * plane_out + k
        shift = 1 if q >= planes_in else 0
        yield k, q % planes_in, h * HU + shift, n


def audio_tower(nc, io):
    with ExitStack() as whole:
        tok = whole.enter_context(nc.sbuf_tensor("tok", [P, B, 2, E], F32))
        ident = whole.enter_context(nc.sbuf_tensor("ident", [P, P], F32))
        mhalf = whole.enter_context(nc.sbuf_tensor("mhalf", [P, 32], F32))
        moe = expert_state(nc, whole)
        att = attention_state(nc, whole)
        with ExitStack() as ctx:
            conv_stage(nc, io, ctx, tok, ident, mhalf, moe, att)
        split_weights(nc, whole, moe)
        with ExitStack() as ctx:
            attention_stage(nc, ctx, tok, ident, mhalf, moe, att)
        with ExitStack() as ctx:
            expert_stage(nc, io, ctx, tok, ident, moe)


def conv_stage(nc, io, ctx, tok, ident, mhalf, moe, att):
    def sb(name, shape, dt=F32):
        return ctx.enter_context(nc.sbuf_tensor(name, shape, dt))

    def sem(name):
        return ctx.enter_context(nc.semaphore(name))

    gavg = sb("gavg", [P, P])
    sel = sb("sel", [XR, 8, K0 + 1])
    ones = sb("ones", [P, 1])
    chan = sb("chan", [P, 6, 3])
    w0f = sb("w0f", [P, 8, C])
    w0s = sb("w0s", [P, 2, 8, C], F16)
    w11 = sb("w11", [K0 + 1, C])
    w = [None] + [sb(f"w{l}", [P, 3 if l < 5 else 2, C]) for l in range(1, 6)]
    pw = sb("pw", [P, E])
    pb = sb("pb", [P, E])
    xu = sb("xu", [P, UT, XR])
    lastp = sb("lastp", [1, 2, K0 + 1])
    xs = sb("xs", [P, U], F16)
    h0 = sb("h0", [P, 8, U])
    h1r = sb("h1r", [P, 4, U])
    h1 = sb("h1", [P, 4, U])
    h2 = sb("h2", [P, 2, U])
    h3 = sb("h3", [P, U])
    h4 = sb("h4", [P, T4])
    h5 = sb("h5", [P, T5])
    gram = sb("gram", [XR, XR])
    gsel = sb("gsel", [XR, 8, K0 + 1])
    g11 = sb("g11", [K0 + 1, K0 + 1])
    q11 = sb("q11", [K0 + 1, C])
    bn = sb("bn", [P, 8, 6])
    bn1 = sb("bn1", [P, 8, 6])
    bn_tok = sb("bn_tok", [P, 2, 6])
    mv_tok = sb("mv_tok", [P, 2, 2])
    st = sb("st", [P, 6, 2])
    gm = sb("gm", [P, 6, 2])
    var = sb("var", [P, 6, 3])
    rstd = sb("rstd", [P, 6])
    dmean = sb("dmean", [P, 6])
    gscale = sb("gscale", [P, 6])
    gbias = sb("gbias", [P, 6])
    scale0 = sb("scale0", [P, 1])

    ring = [ctx.enter_context(nc.psum_tensor(f"ring{i}", [P, 512], F32)) for i in range(3)]
    misc = ctx.enter_context(nc.psum_tensor("misc", [P, 512], F32))
    tail = [ctx.enter_context(nc.psum_tensor(f"tail{i}", [P, 512], F32)) for i in range(4)]

    loads = sem("loads")
    w0_loads = sem("w0_loads")
    x_loads = sem("x_loads")
    ready = sem("ready")
    pe_conv = [sem(f"pe_l{l}") for l in range(6)]
    pe_misc = sem("pe_misc")
    dve_misc = sem("dve_misc")
    l1_out = sem("l1_out")
    stats = [sem(f"stats{l}") for l in range(6)]
    pow_in = sem("pow_in")
    pow_out = sem("pow_out")
    norm = [sem(f"norm{l}") for l in range(6)]
    gelu = [sem(f"gelu{l}") for l in range(6)]
    step = sem("step")
    alone = sem("alone")

    CH = {0: 16, 1: 8, 2: 4, 3: 2, 4: 1, 5: 1}

    with nc.Block() as block:
        @block.sync
        def _(sp):
            sp.dma_start(chan[:], io["chan"]).then_inc(loads, 16)
            sp.dma_start(ident[:], io["ident"]).then_inc(loads, 16)
            sp.dma_start(gavg[:], io["gavg"]).then_inc(loads, 16)
            sp.dma_start(sel[:], io["sel"]).then_inc(loads, 16)
            sp.dma_start(w11[:], io["w11"]).then_inc(loads, 16)
            sp.dma_start(w0f[:], io["w0win"]).then_inc(w0_loads, 16)

            def load_x(b):
                sp.dma_start(xu[:], io["xw"][b]).then_inc(x_loads, 16)
                sp.dma_start(lastp[:, 0, :], io["xlast"][b]).then_inc(x_loads, 16)

            load_x(0)
            for l in range(1, 6):
                sp.dma_start(w[l][:], io[f"w{l}T"]).then_inc(loads, 16)
            sp.dma_start(pw[:], io["pwT"]).then_inc(loads, 16)
            sp.dma_start(pb[:], io["pb"].broadcast_to([P, E])).then_inc(loads, 16)
            for dst, name in ((moe.w1[:, 0], "w1a"), (moe.w1[0:64, 1], "w1b"), (moe.w2[:], "w2x"), (moe.rw[:], "rw")):
                sp.dma_start(dst, io[name]).then_inc(moe.loads, 16)
            for dst, name in ((att.a_w, "a_w"), (att.b_w, "b_w"), (att.vb_w, "vb_w"), (att.o_w, "o_w"),
                              (att.rope, "rope"), (att.maskf, "mask"), (att.countf, "count"),
                              (att.iota, "iota"), (moe.run, "row0"), (moe.goal, "goal")):
                sp.dma_start(dst[:], io[name]).then_inc(att.loads, 16)
            with sp.Fori(1, B) as b:
                sp.wait_ge(pe_conv[0], b * 16 - 15)
                load_x(b)

        LOADS_ALL = 16 * 12
        X_LOADS = 16 * 2

        @block.tensor
        def _(pe):
            def misc_free(m, apart=False):
                if not (isinstance(m[0], int) and m[0] == 0):
                    pe.wait_ge(dve_misc, m[0])
                    if apart:
                        pe.sem_inc(alone, 1)
                m[0] = m[0] + 1

            def transposes(h, b, m):
                misc_free(m, apart=True)
                for j in range(4 * h, 4 * h + 4):
                    rows = P if j < UT - 1 else TAILROWS
                    mm = pe.transpose(misc[0:XR, (j % 4) * P:(j % 4) * P + rows], xu[0:rows, j, :],
                                      ident[0:rows, 0:rows])
                mm.then_inc(pe_misc, 1)

            def gram_matrix(b, m):
                pe.wait_ge(x_loads, (b + 1) * X_LOADS)
                misc_free(m)
                for j in range(UT):
                    rows = P if j < UT - 1 else TAILROWS
                    mm = pe.matmul(misc[0:XR, 0:XR], xu[0:rows, j, :], xu[0:rows, j, :],
                                   start=(j == 0), stop=(j == UT - 1))
                mm.then_inc(pe_misc, 1)

            def gram_select(m):
                misc_free(m, apart=True)
                pe.matmul(misc[0:XR, 0:88], gram[:], sel[:].rearrange("p v k -> p (v k)"),
                          start=True, stop=True).then_inc(pe_misc, 1)

            def gram_taps(m):
                misc_free(m, apart=True)
                pe.matmul(misc[0:K0 + 1, 0:K0 + 1], lastp[:, 1, :], lastp[:, 0, :],
                          start=True, stop=False)
                for v in range(8):
                    mm = pe.matmul(misc[0:K0 + 1, 0:K0 + 1], sel[:, v, :], gsel[:, v, :],
                                   start=False, stop=(v == 7))
                mm.then_inc(pe_misc, 1)

            def gram_weights(m):
                misc_free(m, apart=True)
                pe.matmul(misc[0:K0 + 1, 0:C], g11[:], w11[:], start=True, stop=True).then_inc(pe_misc, 1)

            def moments0(m, b):
                misc_free(m)
                pe.matmul(misc[:, 0:1], w11[:], g11[:, K0:K0 + 1], start=True, stop=True)
                pe.matmul(misc[:, 1:2], q11[:], ones[0:K0 + 1, :], start=True, stop=True).then_inc(pe_misc, 1)

            def group_mean(l, m, b):
                if l > 0:
                    pe.wait_ge(stats[l], b + 1)
                misc_free(m)
                pe.matmul(misc[:, 0:2], gavg[:], st[:, l, :], start=True, stop=True).then_inc(pe_misc, 1)

            def ring_free(use, b, front):
                k = RING.index(use) - 3
                while k >= 0 and RING[k][0] == 0 and not front:
                    k -= 3
                l, c = RING[k]
                t = b + (l == 0) - (k < 0)
                if l:
                    pe.wait_ge(l1_out, 8 * t + c + 1)
                else:
                    pe.wait_ge(gelu[0], 16 * t + c + 1)

            def conv0(c, b, ringed=True):
                v, h = L0_CHUNKS[c]
                n = half_cols(v == 7, h)
                bank = ring[ring_bank((0, c))]
                if ringed:
                    ring_free((0, c), b - 1, True)
                else:
                    before = [i for i in range(c) if ring_bank((0, i)) == ring_bank((0, c))]
                    if before:
                        pe.wait_ge(gelu[0], before[-1] + 1)
                for part in range(2):
                    mm = pe.matmul(bank[:, 0:n], w0s[0:LO + XR, part, v, :], xs[0:LO + XR, h * HU:h * HU + n],
                                   start=(part == 0), stop=(part == 1))
                mm.then_inc(pe_conv[0], 1)

            def conv1(c, b, front):
                q, h = L1_CHUNKS[c]
                n = half_cols(q == 3, h)
                bank = ring[ring_bank((1, c))]
                ring_free((1, c), b, front)
                pe.wait_ge(gelu[0], 16 * b + {0: 7, 3: 15, 1: 15, 2: 15}[q] + h)
                for k, plane, col, n in taps_of(q, 8, h, n):
                    mm = pe.matmul(bank[:, 0:n], w[1][:, k, :], h0[:, plane, col:col + n],
                                   start=(k == 0), stop=(k == 2))
                mm.then_inc(pe_conv[1], 1)

            def conv2(c, b):
                q, h = c // 2, c % 2
                n = half_cols(q == 1, h)
                if not (isinstance(b, int) and b == 0):
                    pe.wait_ge(gelu[(3, 3, 4, 5)[c]], CH[(3, 3, 4, 5)[c]] * b)
                pe.wait_ge(gelu[1], 8 * b + (3, 6, 7, 8)[c])
                for k, plane, col, n in taps_of(q, 4, h, n):
                    mm = pe.matmul(tail[c][:, 0:n], w[2][:, k, :], h1[:, plane, col:col + n],
                                   start=(k == 0), stop=(k == 2))
                mm.then_inc(pe_conv[2], 1)

            def conv3(c, b):
                n = half_cols(True, c)
                pe.wait_ge(gelu[2], 4 * b + 4)
                for k, plane, col, n in taps_of(0, 2, c, n):
                    mm = pe.matmul(tail[c][:, 0:n], w[3][:, k, :], h2[:, plane, col:col + n],
                                   start=(k == 0), stop=(k == 2))
                mm.then_inc(pe_conv[3], 1)

            def conv45(l, b):
                src, n, taps = (h3, T4, 3) if l == 4 else (h4, T5, 2)
                pe.wait_ge(gelu[l - 1], CH[l - 1] * (b + 1))
                for k in range(taps):
                    mm = pe.matmul(tail[l - 2][:, 0:n], w[l][:, k, :], src[:, k:k + 2 * n - 1:2],
                                   start=(k == 0), stop=(k == taps - 1))
                mm.then_inc(pe_conv[l], 1)

            def project(m, b):
                pe.wait_ge(gelu[5], b + 1)
                misc_free(m)
                for t in range(2):
                    mm = pe.matmul(misc[0:TQ[t], t * E:(t + 1) * E], h5[:, t * P:t * P + TQ[t]], pw[:],
                                   start=(t == 0), stop=(t == 1), skip_group_check=True)
                mm.then_inc(pe_misc, 1)

            def body(b, m, now=True, front=True, tail1=True, tail2=True):
                if now:
                    conv1(0, b, front)
                if front:
                    gram_matrix(b + 1, m)
                if tail2:
                    conv45(5, b - 2)
                if now:
                    conv1(1, b, front)
                if front:
                    gram_select(m)
                if tail1:
                    conv2(0, b - 1)
                if now:
                    conv1(2, b, front)
                if front:
                    gram_taps(m)
                if tail1:
                    conv2(1, b - 1)
                if tail2:
                    group_mean(5, m, b - 2)
                if tail1:
                    conv2(2, b - 1)
                if now:
                    conv1(3, b, front)
                if tail2:
                    project(m, b - 2)
                if tail1:
                    conv2(3, b - 1)
                if front:
                    gram_weights(m)
                if front:
                    moments0(m, b + 1)
                if now:
                    conv1(4, b, front)
                if tail1:
                    group_mean(2, m, b - 1)
                if front:
                    group_mean(0, m, b + 1)
                if now:
                    conv1(5, b, front)
                if front:
                    transposes(0, b + 1, m)
                if now:
                    conv1(6, b, front)
                if front:
                    transposes(1, b + 1, m)
                if tail1:
                    conv3(0, b - 1)
                if front:
                    pe.wait_ge(dve_misc, m[0])
                    for c in range(0, 3):
                        conv0(c, b + 1)
                if tail1:
                    conv3(1, b - 1)
                if front:
                    for c in range(3, 5):
                        conv0(c, b + 1)
                if now:
                    conv1(7, b, front)
                if tail1:
                    group_mean(3, m, b - 1)
                if front:
                    for c in range(5, 12):
                        conv0(c, b + 1)
                if now:
                    group_mean(1, m, b)
                if tail1:
                    conv45(4, b - 1)
                if front:
                    for c in range(12, 15):
                        conv0(c, b + 1)
                if tail1:
                    group_mean(4, m, b - 1)
                if front:
                    conv0(15, b + 1)

            pe.wait_ge(loads, LOADS_ALL)
            pe.wait_ge(ready, 2)
            m = [0]
            gram_matrix(0, m)
            gram_select(m)
            gram_taps(m)
            gram_weights(m)
            moments0(m, 0)
            group_mean(0, m, 0)
            transposes(0, 0, m)
            transposes(1, 0, m)
            pe.wait_ge(dve_misc, m[0])
            for c in range(16):
                conv0(c, 0, ringed=False)
            body(0, m, tail1=False, tail2=False)
            body(1, m, tail2=False)
            base = m[0]
            with pe.Fori(2, B - 1) as b:
                m = [(b - 2) * MISC_PER_BODY + base]
                body(b, m)
            m = [base + (B - 3) * MISC_PER_BODY]
            body(B - 1, m, front=False)
            body(B, m, now=False, front=False)
            body(B + 1, m, now=False, front=False, tail1=False)

        @block.scalar
        def _(act):
            def norm_gelu(l, c, b, out, psum, n, scale=None):
                if c == 0:
                    act.wait_ge(norm[l], b + 1)
                if l != 1:
                    act.wait_ge(pe_conv[l], CH[l] * b + c + 1)
                act.activation(out, psum, ACT.Gelu_apprx_tanh, bias=gbias[:, l:l + 1],
                               scale=gscale[:, l:l + 1] if scale is None else scale).then_inc(gelu[l], 1)

            def gelu0(c, b):
                v, h = L0_CHUNKS[c]
                n = half_cols(v == 7, h)
                norm_gelu(0, c, b, h0[:, v, h * HU:h * HU + n], ring[ring_bank((0, c))][:, 0:n], n,
                          scale=scale0[:, 0:1])

            def gelu1(i, b):
                q, h = GELU1[i]
                n = half_cols(q == 3, h)
                if i == 0 and not (isinstance(b, int) and b == 0):
                    act.wait_ge(pe_conv[2], 4 * b)
                norm_gelu(1, i, b, h1[:, q, h * HU:h * HU + n], h1r[:, q, h * HU:h * HU + n], n)

            def gelu2(c, b):
                q, h = c // 2, c % 2
                n = half_cols(q == 1, h)
                norm_gelu(2, c, b, h2[:, q, h * HU:h * HU + n], tail[c][:, 0:n], n)

            def gelu3(c, b):
                n = half_cols(True, c)
                norm_gelu(3, c, b, h3[:, c * HU:c * HU + n], tail[c][:, 0:n], n)

            def body(b, now=True, front=True, tail1=True, tail2=True):
                if tail2:
                    norm_gelu(4, 0, b - 2, h4[:, 0:T4], tail[2][:, 0:T4], T4)
                if tail1:
                    for i in range(8):
                        gelu1(i, b - 1)
                if tail2:
                    norm_gelu(5, 0, b - 2, h5[:, 0:T5], tail[3][:, 0:T5], T5)
                if tail1:
                    for c in range(4):
                        gelu2(c, b - 1)
                if front:
                    for c in range(9):
                        gelu0(c, b + 1)
                if tail1:
                    for c in range(2):
                        gelu3(c, b - 1)
                if front:
                    for c in range(9, 16):
                        gelu0(c, b + 1)

            for c in range(16):
                gelu0(c, 0)
            body(0, tail1=False, tail2=False)
            body(1, tail2=False)
            with act.Fori(2, B - 1) as b:
                body(b)
            body(B - 1, front=False)
            body(B, now=False, front=False)
            body(B + 1, now=False, front=False, tail1=False)

        @block.gpsimd
        def _(pool):
            pool.wait_ge(ready, 1)

            def powers(order, base):
                for i, l in enumerate(order):
                    pool.wait_ge(pow_in, base + (i + 1))
                    pool.tensor_tensor(rstd[:, l:l + 1], var[:, l, 2:3], mhalf[:, 0:1], ALU.pow).then_inc(pow_out, 1)

            start = [0] + [0, 1] + [2, 0, 3, 1, 4]
            powers(start, 0)
            with pool.Fori(2, B - 1) as b:
                powers([5, 2, 0, 3, 1, 4], (b - 2) * 6 + len(start))
            powers([5, 2, 3, 1, 4] + [5, 2, 3, 4] + [5], len(start) + 6 * (B - 3))

        @block.vector
        def _(dve):
            s = [0]
            count = [0]
            pw_n = [0]

            def then(ins):
                ins.then_inc(step, 1)
                s[0] = s[0] + 1
                count[0] += 1
                dve.wait_ge(step, s[0])

            def misc_there(m):
                m[0] = m[0] + 1
                dve.wait_ge(pe_misc, m[0])

            def split_x(h, m):
                n = (4 * P, U - 4 * P)[h]
                hi = xs[0:XR, h * 4 * P:h * 4 * P + n]
                misc_there(m)
                then(dve.tensor_copy(hi, misc[0:XR, 0:n]))
                dve.tensor_tensor(xs[LO:LO + XR, h * 4 * P:h * 4 * P + n], misc[0:XR, 0:n], hi,
                                  ALU.subtract).then_inc(dve_misc, 1)

            def keep(m, out, width, rows, scale=None):
                misc_there(m)
                src = misc[0:rows, 0:width]
                if scale is None:
                    dve.tensor_copy(out, src).then_inc(dve_misc, 1)
                else:
                    dve.tensor_scalar(out, src, scale, None, ALU.mult).then_inc(dve_misc, 1)

            def neg_last():
                then(dve.tensor_scalar(lastp[:, 1, :], lastp[:, 0, :], -1.0, None, ALU.mult))

            def finish_norm(l, m):
                misc_there(m)
                mean, sq = gm[:, l, 0:1], gm[:, l, 1:2]
                dve.tensor_copy(gm[:, l, :], misc[:, 0:2]).then_inc(dve_misc, 1)
                dve.wait_ge(dve_misc, m[0])
                then(dve.scalar_tensor_tensor(out=var[:, l, 0:1], in0=mean, scalar=mean, in1=sq,
                                              op0=ALU.mult, op1=ALU.subtract))
                then(dve.tensor_scalar(var[:, l, 1:2], var[:, l, 0:1], -1.0, 0.0, ALU.mult, ALU.max))
                dve.tensor_scalar(var[:, l, 2:3], var[:, l, 1:2], EPS, None, ALU.add).then_inc(pow_in, 1)
                if l == 0:
                    dve.tensor_scalar(dmean[:, l:l + 1], mean, -1.0, None, ALU.mult)
                else:
                    dve.tensor_tensor(dmean[:, l:l + 1], chan[:, l, 0:1], mean, ALU.subtract)
                pw_n[0] = pw_n[0] + 1
                dve.wait_ge(pow_out, pw_n[0])
                then(dve.tensor_tensor(gscale[:, l:l + 1], rstd[:, l:l + 1], chan[:, l, 1:2], ALU.mult))
                if l == 0:
                    then(dve.tensor_scalar(scale0[:], gscale[:, l:l + 1], 1.0 / S0, None, ALU.mult))
                dve.scalar_tensor_tensor(out=gbias[:, l:l + 1], in0=dmean[:, l:l + 1], scalar=gscale[:, l:l + 1],
                                         in1=chan[:, l, 2:3], op0=ALU.mult, op1=ALU.add).then_inc(norm[l], 1)

            def moments(l, bn, chunks):
                dve.sem_inc(alone, 1)
                then(dve.bn_aggr(st[:, l, :], bn[:, 0:chunks, :].rearrange("p c s -> p (c s)")))
                then(dve.tensor_tensor(st[:, l, 0:1], st[:, l, 0:1], chan[:, l, 0:1], ALU.add))
                dve.scalar_tensor_tensor(out=st[:, l, 1:2], in0=st[:, l, 0:1], scalar=st[:, l, 0:1],
                                         in1=st[:, l, 1:2], op0=ALU.mult, op1=ALU.add).then_inc(stats[l], 1)

            def out1(c, b):
                move1(c, b)
                stats1(c, b)

            def move1(c, b):
                q, h = L1_CHUNKS[c]
                n = half_cols(q == 3, h)
                y = h1r[:, q, h * HU:h * HU + n]
                dve.wait_ge(pe_conv[1], 8 * b + c + 1)
                if not (isinstance(b, int) and b == 0):
                    dve.wait_ge(gelu[1], 8 * b - 7 + GELU1.index((q, h)))
                dve.tensor_copy(y, ring[ring_bank((1, c))][:, 0:n]).then_inc(l1_out, 1)

            def stats1(c, b):
                q, h = L1_CHUNKS[c]
                dve.wait_ge(l1_out, 8 * b + c + 1)
                ins = dve.bn_stats(bn1[:, c, :], h1r[:, q, h * HU:h * HU + half_cols(q == 3, h)])
                if c == 7:
                    then(ins)
                    moments(1, bn1, 8)

            def stats_of(l, b, chunks=None):
                for c in chunks or range(CH[l]):
                    n = {2: half_cols(c >= 2, c % 2), 3: half_cols(True, c), 4: T4, 5: T5}[l]
                    bank = tail[c] if l < 4 else tail[l - 2]
                    dve.wait_ge(pe_conv[l], CH[l] * b + c + 1)
                    ins = dve.bn_stats(bn[:, c, :], bank[:, 0:n])
                if c == CH[l] - 1:
                    then(ins)
                    moments(l, bn, CH[l])

            def tokens(m, b):
                misc_there(m)
                dve.tensor_tensor(tok[:, b, 0, :], misc[:, 0:E], pb[:], ALU.add)
                dve.tensor_tensor(tok[0:TQ[1], b, 1, :], misc[0:TQ[1], E:2 * E], pb[0:TQ[1], :],
                                  ALU.add).then_inc(dve_misc, 1)
                dve.wait_ge(dve_misc, m[0])
                dve.sem_inc(alone, 1)
                for t in range(2):
                    ins = dve.bn_stats(bn_tok[:, t, :], tok[:, b, t, :])
                then(ins)
                dve.sem_inc(alone, 1)
                for t in range(2):
                    ins = dve.bn_aggr(mv_tok[:, t, :], bn_tok[:, t, :])
                then(ins)
                dve.tensor_copy(att.mv[:, 0, b, :], mv_tok[:, :, 0])
                dve.tensor_scalar(att.mv[:, 1, b, :], mv_tok[:, :, 1], EPS, None, ALU.add)

            def prep(i, m, b):
                if i == 0:
                    split_x(0, m)
                elif i == 1:
                    split_x(1, m)
                elif i == 2:
                    keep(m, gram[:], XR, XR)
                    neg_last()
                elif i == 3:
                    keep(m, gsel[:].rearrange("p v k -> p (v k)"), 88, XR)
                elif i == 4:
                    keep(m, g11[:], K0 + 1, K0 + 1, scale=1.0 / T0)
                elif i == 5:
                    misc_there(m)
                    dve.tensor_tensor(q11[:], misc[0:K0 + 1, 0:C], w11[:], ALU.mult).then_inc(dve_misc, 1)
                elif i == 6:
                    misc_there(m)
                    dve.tensor_copy(st[:, 0, :], misc[:, 0:2]).then_inc(dve_misc, 1)

            def body(b, m, now=True, front=True, tail1=True, tail2=True):
                if now:
                    out1(0, b)
                if front:
                    prep(2, m, b)
                if tail2:
                    stats_of(5, b - 2)
                if now:
                    out1(1, b)
                if front:
                    prep(3, m, b)
                if tail1:
                    stats_of(2, b - 1, [0])
                if now:
                    out1(2, b)
                if front:
                    prep(4, m, b)
                if tail1:
                    stats_of(2, b - 1, [1])
                if tail2:
                    finish_norm(5, m)
                if tail1:
                    stats_of(2, b - 1, [2])
                if now:
                    out1(3, b)
                if tail2:
                    tokens(m, b - 2)
                if front:
                    prep(5, m, b)
                if tail1:
                    stats_of(2, b - 1, [3])
                if front:
                    prep(6, m, b)
                if tail1:
                    finish_norm(2, m)
                if front:
                    finish_norm(0, m)
                if now:
                    out1(4, b)
                if front:
                    prep(0, m, b)
                if now:
                    out1(5, b)
                if now:
                    out1(6, b)
                if front:
                    prep(1, m, b)
                if tail1:
                    stats_of(3, b - 1)
                if now:
                    move1(7, b)
                if tail1:
                    finish_norm(3, m)
                if now:
                    stats1(7, b)
                    finish_norm(1, m)
                if tail1:
                    stats_of(4, b - 1)
                    finish_norm(4, m)

            dve.memset(ones[:], 1.0)
            dve.memset(tok[:, :, 1, :], 0.0)
            dve.memset(xs[:], 0.0)
            dve.memset(mhalf[:], -0.5).then_inc(ready, 1)
            dve.wait_ge(w0_loads, 16)
            then(dve.tensor_scalar(w0f[:], w0f[:], S0, None, ALU.mult))
            then(dve.tensor_copy(w0s[:, 0, :, :], w0f[:]))
            dve.tensor_tensor(w0s[:, 1, :, :], w0f[:], w0s[:, 0, :, :], ALU.subtract).then_inc(ready, 1)
            dve.wait_ge(loads, LOADS_ALL)
            m = [0]
            dve.wait_ge(x_loads, X_LOADS)
            for i in range(2, 7):
                prep(i, m, -1)
            finish_norm(0, m)
            prep(0, m, -1)
            prep(1, m, -1)
            body(0, m, tail1=False, tail2=False)
            body(1, m, tail2=False)
            base, s_base, p_base = m[0], s[0], pw_n[0]
            with dve.Fori(2, B - 1) as b:
                m = [(b - 2) * MISC_PER_BODY + base]
                s[0] = (b - 2) * STEPS + s_base
                pw_n[0] = (b - 2) * 6 + p_base
                n0 = count[0]
                body(b, m)
                assert count[0] - n0 == STEPS, count[0] - n0
            m = [base + (B - 3) * MISC_PER_BODY]
            s[0] = s_base + (B - 3) * STEPS
            pw_n[0] = p_base + (B - 3) * 6
            body(B - 1, m, front=False)
            body(B, m, now=False, front=False)
            body(B + 1, m, now=False, front=False, tail1=False)


class Experts:
    pass


def expert_state(nc, ctx):
    def sb(name, shape, dt=F32):
        return ctx.enter_context(nc.sbuf_tensor(name, shape, dt))

    m = Experts()
    m.w1 = sb("moe_w1", [P, 2, NE, HID])
    m.w2 = sb("moe_w2", [P, NE, HT, E])
    m.rw = sb("moe_rw", [P, 2, NE])
    m.pr = sb("pr", [P, NT, NE])
    m.sel = sb("moe_sel", [P, 2, NT, NE])
    m.run = sb("run", [P, NE])
    m.xs = nc.dram_tensor("xs_rows", (NE * CAP + P, XW), F32)
    m.ys = nc.dram_tensor("ys_rows", (RESULTS + 2 * P, E), F32)
    m.goal = sb("goal", [P, 2, 2])
    m.loads = ctx.enter_context(nc.semaphore("moe_loads"))
    m.rows = ctx.enter_context(nc.semaphore("moe_rows"))
    return m


def split_weights(nc, ctx, moe):
    moe.w1s = ctx.enter_context(nc.sbuf_tensor("moe_w1s", [P, 2, 2 * NE * HID], F16))
    moe.w2s = ctx.enter_context(nc.sbuf_tensor("moe_w2s", [P, NE * HT, 2, E], F16))


class Attention:
    pass


def attention_state(nc, ctx):
    def sb(name, shape, dt=F32):
        return ctx.enter_context(nc.sbuf_tensor(name, shape, dt))

    a = Attention()
    a.a_w = sb("a_w", [P, 2, 3, RANK])
    a.b_w = sb("b_w", [RANK, 2, 2, E])
    a.vb_w = sb("vb_w", [RANK, E])
    a.o_w = sb("o_w", [P, 2, E])
    a.rope = sb("rope", [96, 2, 2, 2 * P])
    a.maskf = sb("maskf", [P, P])
    a.iota = sb("iota", [P, 2, NE])
    a.countf = sb("countf", [P, 3, P])
    a.mv = sb("a_mv", [P, 2, B, 2])
    a.loads = ctx.enter_context(nc.semaphore("a_loads"))
    return a


def attention_stage(nc, ctx, tok, ident, mhalf, moe, att):
    def sb(name, shape, dt=F32):
        return ctx.enter_context(nc.sbuf_tensor(name, shape, dt))

    def sem(name):
        return ctx.enter_context(nc.semaphore(name))

    xn = sb("xn", [P, 2, E])
    xT = sb("xT", [P, 2, 2 * P])
    rT = sb("rT", [RANK, 3, 2 * P])
    rot = sb("rot", [96, 2, 2 * P])
    qk = sb("qk", [96, 2, 2, 2 * P])
    vz = sb("vz", [P, 2, 7 * P])
    nmax = sb("nmax", [P, 2, HEADS])
    probs = [sb(f"probs{i}", [P, HEADS, (i + 1) * P]) for i in range(2)]
    vs = sb("vs", [P, 2, E])
    pT = sb("pT", [P, HEADS, 3, P])
    total = sb("total", [P, 2, HEADS])
    rec = sb("rec", [P, 2, HEADS])
    oT = sb("oT", [P, 2, 2 * P])
    mask = sb("mask", [P, P], BF16)
    identb = sb("identb", [P, P], BF16)
    rstd = sb("a_rstd", [P, 32])

    xn2 = sb("xn2", [P, 2, E])
    xcopy = sb("xcopy", [P, 2, 2, XW])
    x2T = sb("x2T", [P, 2, 2 * P])
    bn2 = sb("bn2", [P, 2, 6])
    mv2 = sb("mv2", [P, 2, 2])
    veps2 = sb("veps2", [P, 2])
    rstd2 = sb("rstd2", [P, 2])
    lg = sb("lg", [P, 2, NE])
    ex = sb("ex", [P, 2, NE])
    col = sb("col", [P, 6, 2])
    key = sb("key", [P, 2, NE])
    picks = sb("picks", [P, 2, 2, NE])
    rest = sb("rest", [P, 2, NE])
    member = sb("member", [P, 2, NE], BF16)
    where = sb("where", [P, 2, NE])
    chosen = sb("chosen", [P, 2, 2, NE])
    rowf = sb("rowf", [P, 2, 2])
    rowi = sb("rowi", [P, 2, 2], U32)
    count = sb("count", [P, 3, P], BF16)

    front = [ctx.enter_context(nc.psum_tensor(f"front{i}", [P, 512], F32)) for i in range(2)]
    sc = ctx.enter_context(nc.psum_tensor("sc", [P, 3, 2, 2 * P], F32))
    pt = [ctx.enter_context(nc.psum_tensor(f"pt{i}", [P, 4, P], F32)) for i in range(2)]
    outp = ctx.enter_context(nc.psum_tensor("outp", [P, 512], F32))

    a_w, b_w, vb_w, o_w, rope = att.a_w, att.b_w, att.vb_w, att.o_w, att.rope
    zeros_set = sem("a_zeros")
    mask_set = sem("mask_set")
    step = sem("a_step")
    rstd_out = sem("a_rstd_out")
    xn_set = sem("xn_set")
    xT_mm = sem("xT_mm")
    xT_set = sem("xT_set")
    r_mm = sem("r_mm")
    r_set = sem("r_set")
    qk_mm = sem("qk_mm")
    qk_set = sem("qk_set")
    v_mm = sem("v_mm")
    v_set = sem("v_set")
    vz_set = sem("vz_set")
    s_mm = sem("s_mm")
    max_set = sem("max_set")
    exp_set = sem("exp_set")
    pt_mm = sem("pt_mm")
    pt_set = sem("pt_set")
    o_mm = sem("o_mm")
    probs_set = sem("probs_set")
    oT_set = sem("oT_set")
    out_mm = sem("out_mm")
    out_set = sem("out_set")
    alone2 = sem("alone2")
    alone3 = sem("alone3")
    var2_in = sem("var2_in")
    rstd2_out = sem("rstd2_out")
    xn2_set = sem("xn2_set")
    x2T_mm = sem("x2T_mm")
    x2T_set = sem("x2T_set")
    lg_mm = sem("lg_mm")
    lg_set = sem("lg_set")
    ex_set = sem("ex_set")
    member_set = sem("member_set")
    rank_mm = sem("rank_mm")
    row_set = sem("row_set")
    rank_read = sem("rank_read")
    w_step = sem("w_step")
    w_high = sem("w_high")
    w_low = sem("w_low")
    alone4 = sem("alone4")

    W1C, W2R = NE * HID // B, NE * HT // B

    def pieces(b):
        w1 = moe.w1[:].rearrange("p c e n -> p (c e n)")
        w2 = moe.w2[:].rearrange("p e i n -> p (e i n)")
        cuts = [(w1[0:rows, bass.ds(b * W1C + first, W1C)],) +
                tuple(moe.w1s[0:rows, half, bass.ds(b * W1C + first, W1C)] for half in range(2))
                for rows, first in ((P, 0), (64, NE * HID))]
        cuts.append((w2[:, bass.ds(b * (W2R * E), W2R * E)].rearrange("p (i n) -> p i n", n=E),) +
                    tuple(moe.w2s[:, bass.ds(b * W2R, W2R), half, :] for half in range(2)))
        return cuts

    PT = [(0, [(h, 0) for h in range(4)]), (0, [(4, 0), (5, 0)]),
          (1, [(h, 0) for h in range(4)]), (1, [(4, 0), (5, 0), (0, 1), (1, 1)]), (1, [(h, 1) for h in range(2, 6)])]

    def first(b):
        return isinstance(b, int) and b == 0

    with nc.Block() as block:
        @block.tensor
        def _(pe):
            pe.wait_ge(att.loads, 16 * 10)

            def tokens_T(b):
                pe.wait_ge(xn_set, b + 1)
                if not first(b):
                    pe.wait_ge(v_set, b)
                if not (isinstance(b, int) and b < 3):
                    pe.wait_ge(lg_set, b - 2)
                for t in range(2):
                    pe.transpose(front[0][:, t * P:(t + 1) * P], xn[:, t, 0:P], ident[:])
                    mm = pe.transpose(front[0][0:64, (2 + t) * P:(3 + t) * P], xn[:, t, P:E], ident[:])
                mm.then_inc(xT_mm, 1)

            def factor(b):
                pe.wait_ge(xT_set, b + 1)
                if not first(b):
                    pe.wait_ge(qk_set, 2 * b)
                if not (isinstance(b, int) and b < 3):
                    pe.wait_ge(x2T_set, b - 2)
                for i in range(3):
                    out = front[1][0:RANK, i * 2 * P:(i + 1) * 2 * P] if i < 2 else front[0][0:RANK, 0:2 * P]
                    pe.matmul(out, a_w[:, 0, i, :], xT[:, 0, :], start=True, stop=False)
                    mm = pe.matmul(out, a_w[0:64, 1, i, :], xT[0:64, 1, :], start=False, stop=True)
                    if i:
                        mm.then_inc(r_mm, 1)

            def qk_tile(t, b):
                pe.wait_ge(r_set, 2 * b + 2)
                if t:
                    pe.wait_ge(qk_set, 2 * b + 1)
                for r in range(2):
                    for i in range(2):
                        mm = pe.matmul(front[r][0:96, i * 2 * P:(i + 1) * 2 * P], b_w[:, i, r, 96 * t:96 * t + 96],
                                       rT[:, i, :], start=True, stop=True)
                mm.then_inc(qk_mm, 1)

            def values(b):
                pe.wait_ge(qk_set, 2 * b + 2)
                for t in range(2):
                    mm = pe.matmul(front[0][:, t * E:(t + 1) * E], rT[:, 2, t * P:(t + 1) * P], vb_w[:],
                                   start=True, stop=True)
                mm.then_inc(v_mm, 1)

            def scores(qt, b):
                pe.wait_ge(qk_set, 2 * b + 2)
                if qt or not first(b):
                    pe.wait_ge(exp_set, 2 * b + qt)
                n = (qt + 1) * P
                for g in range(3):
                    for t in range(2):
                        pe.matmul(sc[:, g, t, n - P:n], identb[:], mask[:], start=(t == 0), stop=False,
                                  skip_group_check=True)
                for t in range(2):
                    for g in range(3):
                        head = slice(32 * g, 32 * g + 32)
                        mm = pe.matmul(sc[:, g, t, 0:n], qk[head, t, 0, qt * P:(qt + 1) * P],
                                       qk[head, t, 1, 0:n], start=False, stop=(t == 1), skip_group_check=True)
                mm.then_inc(s_mm, 1)

            def probs_T(i, b):
                qt, blocks = PT[i]
                pe.wait_ge(probs_set, 2 * b + qt + 1)
                if not (first(b) and i < 2):
                    pe.wait_ge(pt_set, 5 * b + max(i - 1, 0))
                for j, (h, kt) in enumerate(blocks):
                    mm = pe.transpose(pt[i % 2][:, j, :], probs[qt][:, h, kt * P:(kt + 1) * P], ident[:])
                mm.then_inc(pt_mm, 1)

            def weighted(t, b):
                if t == 0:
                    pe.wait_ge(pt_set, 5 * b + 5)
                    pe.wait_ge(vz_set, b + 1)
                    if not first(b):
                        pe.wait_ge(out_set, b)
                    if not (isinstance(b, int) and b < 2):
                        pe.wait_ge(rank_read, b - 1)
                rows, heads = ((P, range(4)), (2 * HD, range(4, HEADS)))[t]
                for h in heads:
                    for kt in range(2):
                        mm = pe.matmul(outp[0:rows, (2 * t + kt) * P:(2 * t + 2) * P], vz[:, kt, h * P:h * P + rows],
                                       pT[:, h, 2 * kt:2 + kt, :].rearrange("p j n -> p (j n)"),
                                       start=(h == heads[0] and kt == 0), stop=(h == heads[-1] and kt == 1),
                                       skip_group_check=True)
                if t == 1:
                    mm.then_inc(o_mm, 1)

            def out_proj(b):
                pe.wait_ge(oT_set, b + 1)
                for t in range(2):
                    o = outp[:, t * E:(t + 1) * E]
                    pe.matmul(o, oT[:, 0, t * P:(t + 1) * P], o_w[:, 0, :], start=True, stop=False)
                    mm = pe.matmul(o, oT[0:64, 1, t * P:(t + 1) * P], o_w[0:64, 1, :], start=False, stop=True)
                mm.then_inc(out_mm, 1)

            def route_T(b, f):
                pe.wait_ge(xn2_set, b + 1)
                pe.wait_ge(qk_set, 2 * f)
                for t in range(2):
                    pe.transpose(front[1][:, t * P:(t + 1) * P], xn2[:, t, 0:P], ident[:])
                    mm = pe.transpose(front[1][0:64, (2 + t) * P:(3 + t) * P], xn2[:, t, P:E], ident[:])
                mm.then_inc(x2T_mm, 1)

            def logits(b, f):
                pe.wait_ge(x2T_set, b + 1)
                pe.wait_ge(v_set, f)
                for t in range(2):
                    pe.matmul(front[0][:, t * NE:(t + 1) * NE], x2T[:, 0, t * P:(t + 1) * P], moe.rw[:, 0, :],
                              start=True, stop=False)
                    mm = pe.matmul(front[0][:, t * NE:(t + 1) * NE], x2T[0:64, 1, t * P:(t + 1) * P],
                                   moe.rw[0:64, 1, :], start=False, stop=True)
                mm.then_inc(lg_mm, 1)

            def ranks(b):
                pe.wait_ge(member_set, b + 1)
                pe.wait_ge(out_set, min(b + 2, B) if isinstance(b, int) else b + 2)
                if not first(b):
                    pe.wait_ge(rank_read, b)
                o = outp[:, 0:3 * NE]
                pe.matmul(o[:, 0:NE], count[:, 0, :], member[:, 0, :], start=True, stop=True)
                pe.matmul(o[:, NE:2 * NE], count[:, 0, :], member[:, 1, :], start=True, stop=False)
                pe.matmul(o[:, NE:2 * NE], count[:, 1, :], member[:, 0, :], start=False, stop=True)
                pe.matmul(o[:, 2 * NE:3 * NE], count[:, 1, :], member[:, 0, :], start=True, stop=False)
                pe.matmul(o[:, 2 * NE:3 * NE], count[:, 2, :], member[:, 1, :], start=False,
                          stop=True).then_inc(rank_mm, 1)

            def body(b, now=True, after=True, late=True, later=True):
                front_done = b + 2 if after else B
                if now:
                    scores(0, b)
                if after:
                    tokens_T(b + 1)
                    factor(b + 1)
                if late:
                    for i in range(2, 5):
                        probs_T(i, b - 1)
                if now:
                    scores(1, b)
                if late:
                    for t in range(2):
                        weighted(t, b - 1)
                if after:
                    qk_tile(0, b + 1)
                if now:
                    probs_T(0, b)
                    probs_T(1, b)
                if late:
                    out_proj(b - 1)
                if after:
                    qk_tile(1, b + 1)
                if later:
                    ranks(b - 2)
                if after:
                    values(b + 1)
                if late:
                    route_T(b - 1, front_done)
                    logits(b - 1, front_done)

            pe.wait_ge(mask_set, 3)
            pe.wait_ge(moe.loads, 16 * 4)
            tokens_T(0)
            factor(0)
            qk_tile(0, 0)
            qk_tile(1, 0)
            values(0)
            body(0, late=False, later=False)
            body(1, later=False)
            with pe.Fori(2, B - 1) as b:
                body(b)
            body(B - 1, after=False)
            pe.wait_ge(lg_set, B - 1)
            body(B, now=False, after=False)
            ranks(B - 1)

        @block.scalar
        def _(act):
            def move_x2T(b):
                act.wait_ge(x2T_mm, b + 1)
                act.copy(x2T[:, 0, :], front[1][:, 0:2 * P])
                act.copy(x2T[0:64, 1, :], front[1][0:64, 2 * P:4 * P]).then_inc(x2T_set, 1)

            def exp_logits(b):
                act.wait_ge(lg_set, b + 1)
                act.activation(ex[:], lg[:], ACT.Exp).then_inc(ex_set, 1)

            def move_xT(b):
                act.wait_ge(xT_mm, b + 1)
                act.copy(xT[:, 0, :], front[0][:, 0:2 * P])
                act.copy(xT[0:64, 1, :], front[0][0:64, 2 * P:4 * P]).then_inc(xT_set, 1)

            def move_r(b):
                act.wait_ge(r_mm, 2 * b + 1)
                act.copy(rT[:, 0:2, :], front[1][0:RANK, :].rearrange("p (i n) -> p i n", i=2)).then_inc(r_set, 1)
                act.wait_ge(r_mm, 2 * b + 2)
                act.copy(rT[:, 2, :], front[0][0:RANK, 0:2 * P]).then_inc(r_set, 1)

            def move_v(b):
                act.wait_ge(v_mm, b + 1)
                if not first(b):
                    act.wait_ge(vz_set, b)
                act.copy(vs[:].rearrange("p t e -> p (t e)"), front[0][:, 0:2 * E]).then_inc(v_set, 1)

            def exps(qt, b):
                act.wait_ge(max_set, 2 * b + qt + 1)
                if not first(b):
                    act.wait_ge(pt_mm, 5 * b - (3 if qt == 0 else 0))
                n = (qt + 1) * P
                for h in range(HEADS):
                    ins = act.activation(probs[qt][:, h, :], sc[:, h % 3, h // 3, 0:n], ACT.Exp,
                                         bias=nmax[:, qt, h:h + 1], scale=1.0)
                ins.then_inc(exp_set, 1)

            def move_pT(i, b):
                qt, blocks = PT[i]
                act.wait_ge(pt_mm, 5 * b + i + 1)
                if i == 0 and not first(b):
                    act.wait_ge(o_mm, b)
                runs = {}
                for j, (h, kt) in enumerate(blocks):
                    runs.setdefault(kt, []).append((j, h))
                for kt, r in runs.items():
                    (j0, h0), n = r[0], len(r)
                    ins = act.copy(pT[:, h0:h0 + n, qt + kt, :], pt[i % 2][:, j0:j0 + n, :])
                ins.then_inc(pt_set, 1)

            def move_oT(b):
                act.wait_ge(o_mm, b + 1)
                if not first(b):
                    act.wait_ge(out_mm, b)
                act.copy(oT[:, 0, :], outp[:, 0:2 * P])
                act.copy(oT[0:64, 1, :], outp[0:64, 2 * P:4 * P]).then_inc(oT_set, 1)

            def body(b, now=True, after=True, late=True):
                if after:
                    move_xT(b + 1)
                if now:
                    exps(0, b)
                if after:
                    move_r(b + 1)
                if late:
                    for i in range(2, 5):
                        move_pT(i, b - 1)
                if now:
                    exps(1, b)
                if late:
                    move_oT(b - 1)
                if now:
                    move_pT(0, b)
                    move_pT(1, b)
                if after:
                    move_v(b + 1)
                if late:
                    move_x2T(b - 1)
                    exp_logits(b - 1)
                if now:
                    split_high(b)

            def split_high(b):
                for x, _, _ in pieces(b):
                    act.activation(x, x, ACT.Copy, scale=S0).then_inc(w_step, 1)
                act.wait_ge(w_step, 3 * b + 3)
                act.sem_inc(alone4, 1)
                for x, high, _ in pieces(b):
                    act.activation(high, x, ACT.Copy).then_inc(w_high, 1)

            act.wait_ge(moe.loads, 16 * 4)
            move_xT(0)
            move_r(0)
            move_v(0)
            body(0, late=False)
            with act.Fori(1, B - 1) as b:
                body(b)
            body(B - 1, after=False)
            body(B, now=False, after=False)

        @block.gpsimd
        def _(pool):
            pool.tensor_tensor(rstd[:].rearrange("p (b t) -> p b t", t=2), att.mv[:, 1],
                               mhalf[:].rearrange("p (b t) -> p b t", t=2), ALU.pow).then_inc(rstd_out, 1)

            def power(b):
                pool.wait_ge(var2_in, b + 1)
                pool.tensor_tensor(rstd2[:], veps2[:], mhalf[:, 0:2], ALU.pow).then_inc(rstd2_out, 1)

            def scatter(b):
                pool.wait_ge(row_set, b + 1)
                pool.sem_inc(alone3, 1)
                for t in range(2):
                    for c in range(2):
                        pool.indirect_dma_start(
                            moe.xs.ap(), bass.IndirectOffsetOnAxis(rowi[0:TQ[t], c, t:t + 1], 0),
                            xcopy[0:TQ[t], c, t, :], None).then_inc(moe.rows, 16)

            def place_values(b):
                pool.wait_ge(v_set, b + 1)
                pool.sem_inc(alone3, 1)
                if not first(b):
                    pool.wait_ge(o_mm, b)
                    pool.sem_inc(alone3, 1)
                for t in range(2):
                    for h0, h1 in ((0, 4), (4, HEADS)):
                        n = h1 - h0
                        own = vz[:, t, h0 * P:h0 * P + n * (P + HD)].rearrange("p (h x) -> p h x", h=n)
                        ins = pool.tensor_copy(own[:, :, 0:HD], vs[:, t, h0 * HD:h1 * HD].rearrange(
                            "p (h d) -> p h d", d=HD))
                ins.then_inc(vz_set, 1)

            pool.wait_ge(zeros_set, 1)
            pool.sem_inc(alone3, 1)
            def split_low(b):
                pool.wait_ge(w_high, 3 * b + 3)
                pool.sem_inc(alone3, 1)
                for x, high, low in pieces(b):
                    pool.tensor_tensor(low, x, high, ALU.subtract).then_inc(w_low, 1)

            place_values(0)
            place_values(1)
            power(0)
            split_low(0)
            split_low(1)
            with pool.Fori(2, B) as b:
                place_values(b)
                power(b - 1)
                split_low(b)
                scatter(b - 2)
            power(B - 1)
            scatter(B - 2)
            scatter(B - 1)

        @block.vector
        def _(dve):
            dve.memset(vz[:], 0.0).then_inc(zeros_set, 1)
            dve.wait_ge(att.loads, 16 * 10)
            dve.tensor_copy(mask[:], att.maskf[:]).then_inc(mask_set, 1)
            dve.tensor_copy(identb[:], ident[:]).then_inc(mask_set, 1)
            dve.tensor_copy(count[:], att.countf[:]).then_inc(mask_set, 1)
            dve.wait_ge(rstd_out, 1)
            steps, counted = [0], [0]

            def then(ins):
                ins.then_inc(step, 1)
                steps[0] = steps[0] + 1
                counted[0] += 1
                dve.wait_ge(step, steps[0])

            def normalise(b):
                if not first(b):
                    dve.wait_ge(xT_mm, b)
                for t in range(2):
                    ins = dve.tensor_scalar(xn[:, t, :], tok[:, b, t, :], att.mv[:, 0, b, t:t + 1],
                                            rstd[:, bass.ds(2 * b + t, 1)], ALU.subtract, ALU.mult)
                ins.then_inc(xn_set, 1)

            def rotate(t, b):
                dve.wait_ge(qk_mm, 2 * b + t + 1)
                q = qk[:, t, :, :]
                dve.tensor_tensor(q, front[0][0:96, :].rearrange("p (i n) -> p i n", i=2), rope[:, 0], ALU.mult)
                then(dve.tensor_tensor(rot[:], front[1][0:96, :].rearrange("p (i n) -> p i n", i=2), rope[:, 1],
                                       ALU.mult))
                dve.tensor_tensor(q, q, rot[:], ALU.add).then_inc(qk_set, 1)

            def maxima(qt, b):
                dve.wait_ge(s_mm, 2 * b + qt + 1)
                n = (qt + 1) * P
                dve.tensor_reduce(nmax[:, qt, :].rearrange("p (t g) -> p g t", g=3), sc[:, :, :, 0:n],
                                  AX.X, ALU.max, negate=True).then_inc(max_set, 1)

            def divide(qt, b):
                dve.wait_ge(exp_set, 2 * b + qt + 1)
                p = probs[qt][:]
                then(dve.tensor_reduce(total[:, qt, :], p, AX.X, ALU.add))
                then(dve.reciprocal(rec[:, qt, :], total[:, qt, :]))
                dve.tensor_tensor(p, p, rec[:, qt, :].unsqueeze(2).broadcast_to([P, HEADS, (qt + 1) * P]),
                                  ALU.mult).then_inc(probs_set, 1)

            def residual(b):
                dve.wait_ge(out_mm, b + 1)
                x = tok[:, b, :, :]
                dve.tensor_tensor(x, outp[:, 0:2 * E].rearrange("p (t e) -> p t e", t=2), x,
                                  ALU.add).then_inc(out_set, 1)

            def second_moments(b):
                dve.wait_ge(out_set, b + 1)
                dve.sem_inc(alone2, 1)
                for t in range(2):
                    ins = dve.bn_stats(bn2[:, t, :], tok[:, b, t, :])
                then(ins)
                dve.sem_inc(alone2, 1)
                for t in range(2):
                    ins = dve.bn_aggr(mv2[:, t, :], bn2[:, t, :])
                then(ins)
                dve.tensor_scalar(veps2[:], mv2[:, :, 1], EPS, None, ALU.add).then_inc(var2_in, 1)

            def normalise2(b):
                dve.wait_ge(rstd2_out, b + 1)
                for t in range(2):
                    ins = dve.tensor_scalar(xn2[:, t, :], tok[:, b, t, :], mv2[:, t, 0:1], rstd2[:, t:t + 1],
                                            ALU.subtract, ALU.mult)
                ins.then_inc(xn2_set, 1)

            def wide(c):
                return col[:, c, :].unsqueeze(2).broadcast_to([P, 2, NE])

            def shifted_logits(b):
                dve.wait_ge(lg_mm, b + 1)
                o = front[0][:, 0:2 * NE].rearrange("p (t e) -> p t e", t=2)
                then(dve.tensor_reduce(col[:, 0, :], o, AX.X, ALU.max))
                dve.tensor_tensor(lg[:], o, wide(0), ALU.subtract).then_inc(lg_set, 1)

            def pick(src, c):
                flat = "p t e -> p (t e)"
                then(dve.tensor_reduce(col[:, 2, :], src, AX.X, ALU.max))
                then(dve.tensor_tensor(key[:], src, wide(2), ALU.is_equal))
                then(dve.scalar_tensor_tensor(out=key[:].rearrange(flat), in0=key[:].rearrange(flat),
                                              scalar=-float(NE), in1=att.iota[:].rearrange(flat),
                                              op0=ALU.mult, op1=ALU.add))
                then(dve.tensor_reduce(col[:, 3, :], key[:], AX.X, ALU.min))
                then(dve.tensor_tensor(picks[:, c], key[:], wide(3), ALU.is_equal))

            def choose(b):
                flat = "p t e -> p (t e)"
                dve.wait_ge(ex_set, b + 1)
                then(dve.tensor_reduce(col[:, 1, :], ex[:], AX.X, ALU.add))
                then(dve.reciprocal(col[:, 1, :], col[:, 1, :]))
                p = ex[:]
                then(dve.tensor_tensor(p, p, wide(1), ALU.mult))
                dve.tensor_copy(moe.pr[:, bass.ds(2 * b, 2), :], p)
                pick(p, 0)
                then(dve.scalar_tensor_tensor(out=rest[:].rearrange(flat), in0=picks[:, 0].rearrange(flat),
                                              scalar=-2.0, in1=p.rearrange(flat), op0=ALU.mult, op1=ALU.add))
                pick(rest[:], 1)
                dve.tensor_copy(moe.sel[:, :, bass.ds(2 * b, 2), :], picks[:])
                dve.tensor_tensor(member[:], picks[:, 0], picks[:, 1], ALU.add).then_inc(member_set, 1)

            def copy_rows(b):
                if not first(b):
                    dve.wait_ge(moe.rows, b * 64)
                for c in range(2):
                    dve.tensor_copy(xcopy[:, c, :, 0:E], xn2[:])
                then(dve.tensor_copy(xcopy[:, :, :, E], moe.goal[:]))
                then(dve.tensor_scalar(moe.goal[:], moe.goal[:], float(4 * P), None, ALU.add))

            def place(b):
                dve.wait_ge(rank_mm, b + 1)
                run = moe.run[:].unsqueeze(1).broadcast_to([P, 2, NE])
                o = outp[:, 0:3 * NE]
                then(dve.tensor_tensor(where[:], o[:, 0:2 * NE].rearrange("p (t e) -> p t e", t=2), run, ALU.add))
                dve.tensor_tensor(moe.run[:], o[:, 2 * NE:3 * NE], moe.run[:], ALU.add).then_inc(rank_read, 1)
                for c in range(2):
                    ins = dve.tensor_tensor(chosen[:, c], where[:], picks[:, c], ALU.mult)
                then(ins)
                then(dve.tensor_reduce(rowf[:], chosen[:], AX.X, ALU.add))
                if not first(b):
                    dve.wait_ge(moe.rows, b * 64)
                dve.tensor_copy(rowi[:], rowf[:]).then_inc(row_set, 1)

            def body(b, now=True, after=True, late=True, later=True, ahead=True):
                if now:
                    maxima(0, b)
                if late:
                    divide(1, b - 1)
                if now:
                    divide(0, b)
                if later:
                    choose(b - 2)
                    copy_rows(b - 2)
                if now:
                    maxima(1, b)
                if after:
                    rotate(0, b + 1)
                if late:
                    residual(b - 1)
                    second_moments(b - 1)
                if after:
                    rotate(1, b + 1)
                if late:
                    normalise2(b - 1)
                if ahead:
                    normalise(b + 2)
                if later:
                    place(b - 2)
                if late:
                    shifted_logits(b - 1)

            normalise(0)
            rotate(0, 0)
            rotate(1, 0)
            normalise(1)
            body(0, late=False, later=False)
            body(1, later=False)
            base = steps[0]
            with dve.Fori(2, B - 2) as b:
                steps[0] = base + (b - 2) * ASTEPS
                n0 = counted[0]
                body(b)
                assert counted[0] - n0 == ASTEPS, counted[0] - n0
            steps[0] = base + (B - 4) * ASTEPS
            body(B - 2, ahead=False)
            body(B - 1, after=False, ahead=False)
            body(B, now=False, after=False, ahead=False)
            choose(B - 1)
            copy_rows(B - 1)
            place(B - 1)


def expert_stage(nc, io, ctx, tok, ident, moe):
    def sb(name, shape, dt=F32):
        return ctx.enter_context(nc.sbuf_tensor(name, shape, dt))

    def sem(name):
        return ctx.enter_context(nc.semaphore(name))

    NB = 4
    zero = sb("zero", [P, XW])
    lane = sb("lane", [P, NE])
    behind = sb("behind", [P, NE], U32)
    nblk = sb("nblk", [P, 5, NE])
    nblki = sb("nblki", [P, 2, NE], I32)
    onerow = sb("onerow", [P, NE])
    blk = sb("blk", [1, NBLK, NE])
    past = sb("past", [1, 2, NBLK, NE])
    tabf = sb("tabf", [1, 2, NBLK])
    tab = sb("tab", [1, 2, NBLK], I32)
    count_w = sb("count_w", [P, 2, P])
    imp2 = sb("imp2", [P, 2, NE])
    load = sb("load", [P, 3, NE])
    g = sb("g", [P, 2, NT, NE])
    wts = sb("wts", [P, 3, NT, 2])
    goals = sb("goals", [P, NBLK], U32)
    goal_now = sb("goal_now", [P, 2], U32)
    col = sb("w_col", [P, 2, NT])
    xb = sb("xb", [P, 2, XW])
    xT = sb("b_xT", [P, 2, 2, 2, P], F16)
    hs = sb("hs", [P, 2, HID])
    hT = sb("hT", [P, 2, 2, HT * P], F16)
    yb = sb("yb", [P, 2, E])

    px = [ctx.enter_context(nc.psum_tensor(f"px{i}", [P, 2, P], F32)) for i in range(2)]
    ph = [ctx.enter_context(nc.psum_tensor(f"ph{i}", [P, HID], F32)) for i in range(2)]
    pt = [ctx.enter_context(nc.psum_tensor(f"pht{i}", [P, HT, P], F32)) for i in range(2)]
    py = [ctx.enter_context(nc.psum_tensor(f"py{i}", [P, 512], F32)) for i in range(2)]

    loads = sem("e_loads")
    step = sem("e_step")
    zero_set = sem("zero_set")
    behind_set = sem("behind_set")
    rest_out = sem("rest_out")
    tab_set = sem("tab_set")
    x_in = [sem(f"x_in{i}") for i in range(2)]
    x_mm = sem("x_mm")
    x_set = sem("x_set")
    x_low = sem("x_low")
    h_mm = sem("h_mm")
    h_set = sem("h_set")
    t_mm = sem("t_mm")
    t_high = sem("t_high")
    t_set = sem("t_set")
    y_mm = sem("y_mm")
    y_set = sem("y_set")
    y_out = [sem(f"y_out{i}") for i in range(2)]
    goals_set = sem("goals_set")
    goal_step = sem("goal_step")
    imp_in = sem("imp_in")
    imp_mm = sem("imp_mm")
    imp_read = sem("imp_read")
    g_in = [sem(f"g_in{i}") for i in range(2 * B // NB)]
    added = sem("added")
    alone = sem("e_alone")
    done = sem("done")

    ZERO_ROWS = 16 * NE
    HALVES = ((0, 0), (0, 1), (1, 0))

    def is_int(j):
        return isinstance(j, int)

    def got(g_, n):
        size = NB * 2 * E
        w1 = moe.w1[:].rearrange("p c e n -> p (c e n)")
        w2 = moe.w2[:].rearrange("p e i n -> p (e i n)")
        in_w1 = 2 * NE * HID // size
        w, k = (w1, g_) if g_ < in_w1 else (w2, g_ - in_w1)
        return w[0:n, k * size:(k + 1) * size].rearrange("p (b c e) -> p b c e", b=NB, c=2)

    def scattered(j, par):
        return (j // 2) * 16 if is_int(j) else (j - par) * 8

    with nc.Block() as block:
        @block.sync
        def _(sp):
            for dst, name in ((lane[:], "lane"), (blk[:], "block0"), (count_w[:], "count_w"),
                              (zero[:, E:XW], "nobody")):
                sp.dma_start(dst, io[name]).then_inc(loads, 16)
            sp.wait_ge(zero_set, 1)
            sp.wait_ge(loads, 16 * 4)
            sp.dma_start(moe.xs.ap()[NE * CAP:NE * CAP + P, :], zero[:]).then_inc(rest_out, 16)
            sp.wait_ge(tab_set, 1)
            sp.wait_ge(moe.rows, 64 * B + ZERO_ROWS)
            sp.wait_ge(rest_out, 16)

            def row(j):
                return sp.value_load(tab[0:1, 1, bass.ds(j, 1)] if not is_int(j) else tab[0:1, 1, j:j + 1],
                                     min_val=0, max_val=NE * CAP)

            def load(j, par):
                first = row(j)
                if not (is_int(j) and j < 2):
                    sp.wait_ge(x_mm, j - 1)
                    sp.wait_ge(goals_set, j - 1)
                sp.dma_start(xb[:, par, :], moe.xs.ap()[bass.ds(first, P), :]).then_inc(x_in[par], 16)

            load(0, 0)
            load(1, 1)
            with sp.Fori(1, NBLK // 2) as i:
                for par in range(2):
                    load(2 * i + par, par)
            for par in range(2):
                sp.wait_ge(y_out[par], 16 * (NBLK // 2))
            results = moe.ys.ap()[0:RESULTS, :].rearrange("(b t p c) e -> t p b (c e)", t=2, p=P, c=2)
            groups = [(t, b) for b in range(0, B, NB) for t in range(2)]

            for g_, (t, b) in enumerate(groups):
                sp.dma_start(got(g_, TQ[t]).rearrange("p b c e -> p b (c e)"),
                             results[t, 0:TQ[t], b:b + NB]).then_inc(g_in[g_], 16)
            for g_, (t, b) in enumerate(groups):
                sp.wait_ge(added, 2 * NB * (g_ + 1))
                sp.dma_start(io["out"][b:b + NB, t * P:t * P + TQ[t], :].rearrange("b t e -> t b e"),
                             tok[0:TQ[t], b:b + NB, t, :]).then_inc(done, 16)
            sp.wait_ge(done, 16 * len(groups))

        @block.tensor
        def _(pe):
            def load_T(j, par):
                pe.wait_ge(x_in[par], (j // 2 + 1) * 16 if is_int(j) else (j + (2 - par)) * 8)
                if not (is_int(j) and j < 2):
                    pe.wait_ge(x_low, j - 1)
                pe.transpose(px[par][:, 0, :], xb[:, par, 0:P], ident[:])
                pe.transpose(px[par][0:64, 1, :], xb[:, par, P:E], ident[:]).then_inc(x_mm, 1)

            def expert(j):
                return pe.value_load(tab[0:1, 0, bass.ds(j, 1)] if not is_int(j) else tab[0:1, 0, j:j + 1],
                                     min_val=0, max_val=NE - 1)

            def hidden(j, par, e=None):
                e = expert(j) if e is None else e
                pe.wait_ge(x_low, j + 1)
                if not (is_int(j) and j < 2):
                    pe.wait_ge(h_set, j - 1)
                for xpart, wpart in HALVES:
                    for c, rows in ((0, P), (1, 64)):
                        mm = pe.matmul(ph[par][:], xT[0:rows, par, xpart, c, :],
                                       moe.w1s[0:rows, wpart, bass.ds(e * HID + c * NE * HID, HID)],
                                       start=(xpart == wpart == c == 0), stop=(xpart == 1 and c == 1))
                mm.then_inc(h_mm, 1)

            def hidden_T(j, par):
                pe.wait_ge(h_set, j + 1)
                if not (is_int(j) and j < 2):
                    pe.wait_ge(t_set, j - 1)
                for i in range(HT):
                    mm = pe.transpose(pt[par][:, i, :], hs[:, par, i * P:(i + 1) * P], ident[:])
                mm.then_inc(t_mm, 1)

            def output(j, par, e=None):
                e = expert(j) if e is None else e
                pe.wait_ge(t_set, j + 1)
                if not (is_int(j) and j < 2):
                    pe.wait_ge(y_set, j - 1)
                w = moe.w2s[:].rearrange("p i h n -> p (i h n)")
                for hpart, n in ((0, 2 * E), (1, E)):
                    for i in range(HT):
                        mm = pe.matmul(py[par][:, 0:n], hT[:, par, hpart, i * P:(i + 1) * P],
                                       w[:, bass.ds(e * (HT * 2 * E) + i * 2 * E, n)],
                                       start=(i == hpart == 0), stop=(i == HT - 1 and hpart == 1))
                mm.then_inc(y_mm, 1)

            pe.wait_ge(loads, 16 * 4)
            pe.wait_ge(imp_in, 1)
            for t in range(2):
                mm = pe.matmul(py[1][:, 0:NE], count_w[:, t, :], imp2[:, t, :], start=(t == 0), stop=(t == 1))
            mm.then_inc(imp_mm, 1)
            pe.wait_ge(tab_set, 1)
            load_T(0, 0)
            load_T(1, 1)
            hidden(0, 0)
            load_T(2, 0)
            hidden(1, 1)
            hidden_T(0, 0)
            pe.wait_ge(imp_read, 1)

            def pair(i):
                for par in range(2):
                    e = expert(2 * i + par)
                    load_T(2 * i + (par + 1), 1 - par)
                    hidden(2 * i + par, par, e)
                    hidden_T(2 * i + (par - 1), 1 - par)
                    before = pe.snap(held[par], min_val=0, max_val=NE - 1)
                    output(2 * i + (par - 2), par, before)
                    pe.reg_mov(held[par], e)

            held = [pe.alloc_register(f"held_expert{k}") for k in range(2)]
            for k in range(2):
                pe.reg_mov(held[k], expert(k))
            pair(1)
            with pe.Fori(2, NBLK // 2 - 1) as i:
                pair(i)
            j = NBLK - 2
            load_T(j + 1, 1)
            hidden(j, 0)
            hidden_T(j - 1, 1)
            output(j - 2, 0)
            hidden(j + 1, 1)
            hidden_T(j, 0)
            output(j - 1, 1)
            hidden_T(j + 1, 1)
            output(j, 0)
            output(j + 1, 1)

        @block.scalar
        def _(act):
            def move_xT(j, par):
                act.wait_ge(x_mm, j + 1)
                if not (is_int(j) and j < 2):
                    act.wait_ge(h_mm, j - 1)
                act.activation(xT[:, par, 0, 0, :], px[par][:, 0, :], ACT.Copy, scale=SX)
                act.activation(xT[0:64, par, 0, 1, :], px[par][0:64, 1, :], ACT.Copy, scale=SX).then_inc(x_set, 1)

            def high_hT(j, par):
                act.wait_ge(t_mm, j + 1)
                if not (is_int(j) and j < 2):
                    act.wait_ge(y_mm, j - 1)
                act.activation(hT[:, par, 0, :], pt[par][:].rearrange("p i n -> p (i n)"), ACT.Copy,
                               scale=SH).then_inc(t_high, 1)

            def silu(j, par):
                act.wait_ge(h_mm, j + 1)
                if not (is_int(j) and j < 2):
                    act.wait_ge(t_mm, j - 1)
                act.activation(hs[:, par, :], ph[par][:], ACT.Silu, scale=1.0 / (SX * S0)).then_inc(h_set, 1)

            move_xT(0, 0)
            move_xT(1, 1)
            silu(0, 0)
            move_xT(2, 0)
            silu(1, 1)
            high_hT(0, 0)
            with act.Fori(1, NBLK // 2 - 1) as i:
                for par in range(2):
                    move_xT(2 * i + (par + 1), 1 - par)
                    silu(2 * i + par, par)
                    high_hT(2 * i + (par - 1), 1 - par)
            j = NBLK - 2
            move_xT(j + 1, 1)
            silu(j, 0)
            high_hT(j - 1, 1)
            silu(j + 1, 1)
            high_hT(j, 0)
            high_hT(j + 1, 1)

        @block.gpsimd
        def _(pool):
            pool.wait_ge(behind_set, 1)
            for e in range(NE):
                pool.indirect_dma_start(moe.xs.ap(), bass.IndirectOffsetOnAxis(behind[:, e:e + 1], 0),
                                        zero[:], None).then_inc(moe.rows, 16)

            def scatter(j, par):
                pool.wait_ge(y_set, j + 1)
                if not (is_int(j) and j < 2):
                    pool.wait_ge(y_out[par], scattered(j, par))
                pool.sem_inc(alone, 1)
                pool.tensor_copy(goal_now[:, par:par + 1], goals[:, bass.ds(j, 1)]).then_inc(goal_step, 1)
                pool.wait_ge(goal_step, j + 1)
                pool.sem_inc(alone, 1)
                pool.indirect_dma_start(moe.ys.ap(), bass.IndirectOffsetOnAxis(goal_now[:, par:par + 1], 0),
                                        yb[:, par, :], None).then_inc(y_out[par], 16)

            scatter(0, 0)
            scatter(1, 1)
            with pool.Fori(1, NBLK // 2) as i:
                for par in range(2):
                    scatter(2 * i + par, par)

        @block.vector
        def _(dve):
            steps = [0]

            def then(ins):
                ins.then_inc(step, 1)
                steps[0] = steps[0] + 1
                dve.wait_ge(step, steps[0])

            dve.memset(onerow[:], 1.0)
            dve.memset(zero[:, 0:E], 0.0).then_inc(zero_set, 1)
            dve.wait_ge(loads, 16 * 4)
            dve.tensor_tensor(behind[:], moe.run[:], lane[:], ALU.add).then_inc(behind_set, 1)
            n0 = nblk[:, 0, :]
            then(dve.tensor_copy(nblk[:, 1, :], moe.run[:]))
            for e in range(NE):
                ins = dve.tensor_scalar(nblk[:, 0, e:e + 1], nblk[:, 1, e:e + 1], float(P - 1 - e * CAP), None, ALU.add)
            then(ins)
            then(dve.tensor_copy(nblki[:, 0, :], n0))
            then(dve.tensor_scalar(nblki[:, 1, :], nblki[:, 0, :], 7, None, ALU.arith_shift_right))
            then(dve.tensor_copy(nblk[:, 1, :], nblki[:, 1, :]))
            then(dve.tensor_tensor_scan(nblk[:, 2, :], onerow[:], nblk[:, 1, :], 0.0, ALU.mult, ALU.add))
            then(dve.tensor_scalar(nblk[:, 3, :], nblk[:, 1, :], -float(P), float(CAP), ALU.mult, ALU.add))
            ends = nblk[0:1, 2, :].unsqueeze(1).broadcast_to([1, NBLK, NE])
            adds = nblk[0:1, 3, :].unsqueeze(1).broadcast_to([1, NBLK, NE])
            then(dve.tensor_tensor(past[:, 0], blk[:], ends, ALU.is_ge))
            then(dve.tensor_tensor(past[:, 1], past[:, 0], adds, ALU.mult))
            then(dve.tensor_reduce(tabf[:], past[:], AX.X, ALU.add))
            then(dve.scalar_tensor_tensor(out=tabf[:, 1, :], in0=blk[:, :, 0], scalar=float(P), in1=tabf[:, 1, :],
                                          op0=ALU.mult, op1=ALU.add))
            dve.tensor_scalar(tabf[:, 0, :], tabf[:, 0, :], float(NE - 1), None, ALU.min)
            then(dve.tensor_scalar(tabf[:, 1, :], tabf[:, 1, :], float(NE * CAP), None, ALU.min))
            dve.tensor_copy(tab[:], tabf[:]).then_inc(tab_set, 1)
            dve.tensor_reduce(imp2[:], moe.pr[:].rearrange("p (b t) e -> p t e b", t=2), AX.X,
                              ALU.add).then_inc(imp_in, 1)
            dve.wait_ge(imp_mm, 1)
            dve.tensor_scalar(load[:, 0, :], py[1][:, 0:NE], -1.0, 1.0 - DECAY, ALU.add, ALU.mult).then_inc(imp_read, 1)
            dve.wait_ge(imp_read, 1)
            then(dve.tensor_scalar(load[:, 1, :], load[:, 0, :], 1.0, LOAD_EPS, ALU.add, ALU.add))
            then(dve.reciprocal(load[:, 2, :], load[:, 1, :]))
            w = load[:, 2, :].unsqueeze(1).broadcast_to([P, NT, NE])
            then(dve.tensor_tensor(moe.pr[:], moe.pr[:], w, ALU.mult))
            for c in range(2):
                then(dve.tensor_tensor(g[:, c], moe.pr[:], moe.sel[:, c], ALU.mult))
                then(dve.tensor_reduce(wts[:, 0, :, c], g[:, c], AX.X, ALU.add))
            then(dve.tensor_tensor(col[:, 0, :], wts[:, 0, :, 0], wts[:, 0, :, 1], ALU.add))
            then(dve.reciprocal(col[:, 1, :], col[:, 0, :]))
            then(dve.tensor_scalar(wts[:, 0], wts[:, 0], 1.0 / (SH * S0), None, ALU.mult))
            then(dve.tensor_tensor(wts[:, 1], wts[:, 0], col[:, 1, :].unsqueeze(2).broadcast_to([P, NT, 2]), ALU.mult))

            def move_hT(j, par):
                dve.wait_ge(t_high, j + 1)
                dve.scalar_tensor_tensor(out=hT[:, par, 1, :], in0=pt[par][:].rearrange("p i n -> p (i n)"),
                                         scalar=SH, in1=hT[:, par, 0, :], op0=ALU.mult,
                                         op1=ALU.subtract).then_inc(t_set, 1)

            def low_xT(j, par):
                dve.wait_ge(x_set, j + 1)
                dve.scalar_tensor_tensor(out=xT[:, par, 1, 0, :], in0=px[par][:, 0, :], scalar=SX,
                                         in1=xT[:, par, 0, 0, :], op0=ALU.mult, op1=ALU.subtract)
                dve.scalar_tensor_tensor(out=xT[0:64, par, 1, 1, :], in0=px[par][0:64, 1, :], scalar=SX,
                                         in1=xT[0:64, par, 0, 1, :], op0=ALU.mult,
                                         op1=ALU.subtract).then_inc(x_low, 1)

            def move_y(j, par):
                dve.wait_ge(y_mm, j + 1)
                if not (is_int(j) and j < 2):
                    dve.wait_ge(y_out[par], scattered(j, par))
                dve.tensor_reduce(yb[:, par, :], py[par][:, 0:2 * E].rearrange("p (h n) -> p n h", h=2), AX.X,
                                  ALU.add).then_inc(y_set, 1)

            def take_goals(j, par):
                dve.wait_ge(x_in[par], (j // 2 + 1) * 16 if is_int(j) else (j + (2 - par)) * 8)
                col = xb[:, par, E:XW]
                if par == 0:
                    dve.tensor_copy(goals[:, bass.ds(j, 1)], col).then_inc(goals_set, 1)
                else:
                    dve.scalar_tensor_tensor(out=goals[:, bass.ds(j, 1)], in0=col, scalar=float(RESULTS), in1=col,
                                             op0=ALU.is_ge, op1=ALU.add).then_inc(goals_set, 1)

            take_goals(0, 0)
            low_xT(0, 0)
            take_goals(1, 1)
            low_xT(1, 1)
            take_goals(2, 0)
            low_xT(2, 0)
            move_hT(0, 0)

            def pair(i):
                for par in range(2):
                    take_goals(2 * i + (par + 1), 1 - par)
                    low_xT(2 * i + (par + 1), 1 - par)
                    move_hT(2 * i + (par - 1), 1 - par)
                    move_y(2 * i + (par - 2), par)

            pair(1)
            with dve.Fori(2, NBLK // 2 - 1) as i:
                pair(i)
            j = NBLK - 2
            take_goals(j + 1, 1)
            low_xT(j + 1, 1)
            move_hT(j - 1, 1)
            move_y(j - 2, 0)
            move_hT(j, 0)
            move_y(j - 1, 1)
            move_hT(j + 1, 1)
            move_y(j, 0)
            move_y(j + 1, 1)
            groups = [(t, b) for b in range(0, B, NB) for t in range(2)]
            for g_, (t, b0) in enumerate(groups):
                n = TQ[t]
                dve.wait_ge(g_in[g_], 16)
                for c in range(2):
                    if c:
                        dve.wait_ge(added, NB * (2 * g_ + 1))
                    for b in range(b0, b0 + NB):
                        x = tok[0:n, b, t, :]
                        dve.scalar_tensor_tensor(out=x, in0=got(g_, n)[:, b - b0, c, :],
                                                 scalar=wts[0:n, 1, 2 * b + t, c:c + 1], in1=x,
                                                 op0=ALU.mult, op1=ALU.add).then_inc(added, 1)




def laid_out(inputs):
    f = np.float32
    got = {k: np.asarray(v) for k, v in inputs.items()}
    x = got["x"]
    a = {}
    xp = np.zeros((B, 40 * UT * P + XR), f)
    xp[:, :T_IN] = x
    idx = 40 * np.arange(UT * P)[:, None] + np.arange(WIN)[None, :]
    xw = np.ones((B, UT * P, XR), f)
    xw[:, :, :WIN] = xp[:, idx]
    a["xw"] = np.ascontiguousarray(xw.reshape(B, UT, P, XR).transpose(0, 2, 1, 3))
    last = np.zeros((B, 1, K0 + 1), f)
    last[:, 0, :5] = x[:, 5 * T0:]
    last[:, 0, K0] = 1.0
    a["xlast"] = last
    w0 = got["L0_tok_cw0"].reshape(C, K0).T
    w0win = np.zeros((P, 8, C), f)
    for base in (0, LO):
        for v in range(8):
            w0win[base + 5 * v:base + 5 * v + K0, v, :] = w0
        w0win[base + WIN, :, :] = got["L0_tok_cb0"]
    a["w0win"] = w0win
    a["w11"] = np.concatenate([w0, got["L0_tok_cb0"][None]], 0)
    for l in range(1, 6):
        a[f"w{l}T"] = np.ascontiguousarray(got[f"L0_tok_cw{l}"].transpose(1, 2, 0))
    a["chan"] = np.stack([np.stack([got[f"L0_tok_{n}{l}"] for n in ("cb", "gw", "gb")], -1)
                          for l in range(6)], 1)
    a["pwT"] = np.ascontiguousarray(got["L0_tok_pw"].T)
    a["pb"] = got["L0_tok_pb"][None]
    a["ident"] = np.eye(P, dtype=f)
    a["gavg"] = np.kron(np.eye(C // GROUP), np.full((GROUP, GROUP), 1.0 / GROUP)).astype(f)
    sel = np.zeros((XR, 8, K0 + 1), f)
    for v in range(8):
        sel[5 * v + np.arange(K0), v, np.arange(K0)] = 1.0
        sel[WIN, v, K0] = 1.0
    a["sel"] = sel
    a_w = np.zeros((P, 2, 3, RANK), f)
    for i, n in enumerate("qkv"):
        m = got[f"L0_attn_{n}A"]
        a_w[:, 0, i], a_w[:64, 1, i] = m[:P], m[P:]
    a["a_w"] = a_w
    swap = (np.arange(E) // HD) * HD + (np.arange(E) % HD + HD // 2) % HD
    a["b_w"] = np.stack([np.stack([got[f"L0_attn_{n}B"], got[f"L0_attn_{n}B"][:, swap]], 1) for n in "qk"], 1)
    a["vb_w"] = got["L0_attn_vB"]
    o_w = np.zeros((P, 2, E), f)
    o_w[:, 0], o_w[:64, 1] = got["L0_attn_o_w"][:P], got["L0_attn_o_w"][P:]
    a["o_w"] = o_w
    inv = (1.0 / 10000.0 ** (np.arange(0, HD, 2, dtype=f) / f(HD))).astype(f)
    angle = np.outer(np.concatenate([inv, inv]), np.arange(2 * P, dtype=f)).astype(f)
    sign = np.where(np.arange(HD) < HD // 2, -1.0, 1.0)[:, None]
    rope = np.stack([np.cos(angle.astype(np.float64)), sign * np.sin(angle.astype(np.float64))], 1)
    rope = np.stack([rope / np.sqrt(HD), rope], 2)
    a["rope"] = np.tile(rope, (3, 1, 1, 1)).astype(f)
    rw = np.zeros((P, 2, NE), f)
    rw[:, 0], rw[:64, 1] = got["L0_ffn_router_w"].T[:P], got["L0_ffn_router_w"].T[P:]
    a["rw"] = rw
    w1 = got["L0_ffn_w1"].transpose(2, 0, 1)
    a["w1a"], a["w1b"] = np.ascontiguousarray(w1[:P]), np.ascontiguousarray(w1[P:])
    a["w2x"] = np.ascontiguousarray(got["L0_ffn_w2"].reshape(NE, E, HT, P).transpose(3, 0, 2, 1))
    a["iota"] = np.tile(np.arange(NE, dtype=f), (P, 2, 1))
    count = np.ones((P, 3, P), f)
    count[:, 0] = np.triu(np.ones((P, P)), 1)
    count[TQ[1]:, 2] = 0.0
    a["count"] = count
    a["goal"] = ((np.arange(2)[None, None] * P + np.arange(P)[:, None, None]) * 2
                 + np.arange(2)[None, :, None]).astype(f)
    a["row0"] = np.tile(np.arange(NE, dtype=f) * CAP, (P, 1))
    a["nobody"] = (RESULTS + 2 * np.arange(P, dtype=f))[:, None]
    a["lane"] = np.tile(np.arange(P, dtype=f)[:, None], (1, NE))
    a["block0"] = np.tile(np.arange(NBLK, dtype=f)[None, :, None], (1, 1, NE))
    count_w = np.ones((P, 2, P), f)
    count_w[TQ[1]:, 1] = 0.0
    a["count_w"] = count_w
    a["mask"] = np.where(np.arange(P)[:, None] >= np.arange(P)[None], 0.0, -1e30).astype(f)
    return a


def kernel(**inputs):
    import concourse.bacc as bacc
    from concourse.bass_utils import run_bass_kernel_spmd

    nc = bacc.Bacc("TRN2", target_bir_lowering=False, num_devices=1)
    arrays, io = {}, {}
    for name, a in laid_out(inputs).items():
        arrays[f"in_{name}"] = a
        io[name] = nc.dram_tensor(f"in_{name}", a.shape, mybir.dt.from_np(a.dtype), kind="ExternalInput").ap()
    io["out"] = nc.dram_tensor("out_0", (B, T5, E), F32, kind="ExternalOutput").ap()
    audio_tower(nc, io)
    r = run_bass_kernel_spmd(nc, [arrays], core_ids=[0])
    return r.results[0]["out_0"]
```
